# Optimizing a Trainium2 kernel written in Bass

```python
import numpy as np
import jax
import jax.numpy as jnp

def _softmax(x, axis=-1):
    return jax.nn.softmax(x, axis=axis)

def _gelu(x):
    return jax.nn.gelu(x, approximate=True)

def _silu(x):
    return jax.nn.silu(x)

def _sigmoid(x):
    return jax.nn.sigmoid(x)

def _layernorm(x, axis=-1, eps=1e-05):
    m = jnp.mean(x, axis=axis, keepdims=True)
    v = jnp.var(x, axis=axis, keepdims=True)
    return (x - m) / jnp.sqrt(v + eps)

def _scatter_add(tgt, idx, src, axis=0):
    return tgt.at[idx].add(src)

def _segment_sum(src, seg, n):
    return jax.ops.segment_sum(src, seg, n)
kernel_name = 'mk_flamingo_gated_d4_seqx_r8_622149'

def setup_inputs(seed: int=0):
    np.random.seed(seed)
    _w = jnp.asarray

    def _rec_inputs():
        import jax
        import jax.numpy as jnp
        _rk = jax.random.key(seed)
        x = -0.000125 + 0.9999 * jax.random.normal(jax.random.fold_in(_rk, 1), (32, 128, 128), jnp.float32)
        _lenS = 128 - jax.random.randint(jax.random.fold_in(_rk, 7), (32,), 0, max(1, 128 // 4) + 1, jnp.int32)
        _lenS2 = 77 - jax.random.randint(jax.random.fold_in(_rk, 8), (32,), 0, max(1, 77 // 4) + 1, jnp.int32)
        _ctx_1024P = jax.random.normal(jax.random.fold_in(_rk, 11), (32, 16, 128), jnp.float32)
        _ctx_1024c = jax.random.dirichlet(jax.random.fold_in(_rk, 511), 0.3 * jnp.ones((16,), jnp.float32), (32, 77))
        _ctx_1024t = jnp.einsum('bsk,bkd->bsd', _ctx_1024c, _ctx_1024P)
        _ctx_1024t = _ctx_1024t * jax.lax.rsqrt(jnp.mean(jnp.square(_ctx_1024t)) + 1e-12) * 0.953939
        ctx_1024 = -5.72187e-05 + 0.999849 * (_ctx_1024t + 0.3 * jax.random.normal(jax.random.fold_in(_rk, 611), (32, 77, 128), jnp.float32))
        itok_BxS_1_4095 = jax.random.randint(jax.random.fold_in(_rk, 13), (32, 128), 1, 512, jnp.int32)
        _validS = jnp.arange(128)[None, :] < _lenS[:, None]
        _validS2 = jnp.arange(77)[None, :] < _lenS2[:, None]
        _causal = jnp.tril(jnp.ones((128, 128), dtype=bool))
        mask_BxS2_bk0 = jnp.logical_not(jnp.broadcast_to(_validS2[:, :], (32, 77)))
        _g = jax.random.normal(jax.random.fold_in(_rk, 9001), (2, 4), jnp.float32)
        _g = jnp.sign(_g) * jnp.maximum(jnp.abs(_g), 1.0) + (_g == 0) * 1.0
        g_xattn = _g[0]
        g_ffn = _g[1]
        return (x, ctx_1024, itok_BxS_1_4095, mask_BxS2_bk0, g_xattn, g_ffn)
    x, ctx_1024, itok_BxS_1_4095, mask_BxS2_bk0, g_xattn, g_ffn = _rec_inputs()

    def _L0_xattn_setup():
        import jax, jax.numpy as jnp
        import numpy as np
        EPS = 1e-08
        B, Q, S, D = (128, 32, 64, 128)

        def l2norm(x, axis):
            norm = jnp.sqrt(jnp.sum(x * x, axis=axis, keepdims=True) + EPS) + EPS
            return x / norm
        key = jax.random.key(seed)
        ks = jax.random.split(key, 4)
        return {'query': jax.random.normal(ks[0], (B, Q, D), jnp.float32), 'context': jax.random.normal(ks[1], (B, S, D), jnp.float32), 'W_lin': jax.random.normal(ks[2], (2 * D, D), jnp.float32) * 0.02, 'b_lin': jnp.zeros((D,), jnp.float32), 'W_gate': jax.random.normal(ks[3], (2 * D, D), jnp.float32) * 0.02, 'b_gate': jnp.zeros((D,), jnp.float32), 'smooth': 9}
    _L0_xattn_all = _L0_xattn_setup()
    _L0_xattn_in = {k: v for k, v in _L0_xattn_all.items() if k in ('W_lin', 'b_lin', 'W_gate', 'b_gate')}
    del _L0_xattn_all

    def _L0_ffn_setup():
        import jax, jax.numpy as jnp
        import numpy as np
        import math
        BETA = 0.9
        THRESHOLD = 1.0
        NUM_STEPS = 5
        ALPHA = 2.0

        @jax.custom_vjp
        def spike_fn(u):
            return (u > 0).astype(u.dtype)

        def _spike_fwd(u):
            return (spike_fn(u), u)

        def _spike_bwd(u, g):
            s = jnp.pi / 2.0 * ALPHA * u
            return (g * (ALPHA / 2.0) / (1.0 + s * s),)
        spike_fn.defvjp(_spike_fwd, _spike_bwd)
        key = jax.random.key(seed)
        k1, k2, k3 = jax.random.split(key, 3)
        n_embd = 128
        x = jax.random.normal(k1, (4, 256, n_embd), dtype=jnp.float32)
        W_fc = jax.random.normal(k2, (4 * n_embd, n_embd), dtype=jnp.float32) / math.sqrt(n_embd)
        W_proj = jax.random.normal(k3, (n_embd, 4 * n_embd), dtype=jnp.float32) / math.sqrt(4 * n_embd)
        return {'x': x, 'W_fc': W_fc, 'W_proj': W_proj}
    _L0_ffn_all = _L0_ffn_setup()
    _L0_ffn_in = {k: v for k, v in _L0_ffn_all.items() if k in ('W_fc', 'W_proj')}
    del _L0_ffn_all

    def _L1_xattn_setup():
        import jax, jax.numpy as jnp
        import numpy as np
        EMBED_DIM = 128
        NUM_HEADS = 16
        HEAD_DIM = EMBED_DIM // NUM_HEADS
        B, T, S = (2, 256, 256)
        key = jax.random.key(seed)
        ks = jax.random.split(key, 5)
        scale_w = 1.0 / np.sqrt(EMBED_DIM)
        return {'q': jax.random.normal(ks[0], (B, T, EMBED_DIM), dtype=jnp.float32), 'k': jax.random.normal(ks[1], (B, S, EMBED_DIM), dtype=jnp.float32), 'v': jax.random.normal(ks[2], (B, S, EMBED_DIM), dtype=jnp.float32), 'in_proj_weight': jax.random.normal(ks[3], (3 * EMBED_DIM, EMBED_DIM), dtype=jnp.float32) * scale_w, 'in_proj_bias': jnp.zeros((3 * EMBED_DIM,), dtype=jnp.float32), 'out_w': jax.random.normal(ks[4], (EMBED_DIM, EMBED_DIM), dtype=jnp.float32) * scale_w, 'out_b': jnp.zeros((EMBED_DIM,), dtype=jnp.float32)}
    _L1_xattn_all = _L1_xattn_setup()
    _L1_xattn_in = {k: v for k, v in _L1_xattn_all.items() if k in ('in_proj_weight', 'in_proj_bias', 'out_w', 'out_b')}
    del _L1_xattn_all

    def _L1_ffn_setup():
        import jax, jax.numpy as jnp
        import numpy as np
        E, K, D, H = (8, 2, 128, 256)
        B, S = (1, 128)

        def _grouped_swiglu(x_sorted, counts, w1, w2, w3):
            if hasattr(jax.lax, 'ragged_dot'):
                gs = counts.astype(jnp.int32)
                h = jax.nn.silu(jax.lax.ragged_dot(x_sorted, w1, gs)) * jax.lax.ragged_dot(x_sorted, w3, gs)
                return jax.lax.ragged_dot(h, w2, gs)
            pos = jnp.arange(x_sorted.shape[0])
            eid = jnp.searchsorted(jnp.cumsum(counts), pos, side='right')
            out = jnp.zeros((x_sorted.shape[0], w2.shape[-1]), x_sorted.dtype)
            for e in range(w1.shape[0]):
                xm = jnp.where((eid == e)[:, None], x_sorted, 0.0)
                he = jax.nn.silu(xm @ w1[e]) * (xm @ w3[e])
                out = out + he @ w2[e]
            return out
        key = jax.random.key(seed)
        k0, k1, k2, k3, k4 = jax.random.split(key, 5)
        sD = 1.0 / np.sqrt(D)
        sH = 1.0 / np.sqrt(H)
        return {'hidden_states': jax.random.normal(k0, (B, S, D), jnp.float32), 'gate_w': jax.random.normal(k1, (E, D), jnp.float32) * sD, 'w1': jax.random.normal(k2, (E, D, H), jnp.float32) * sD, 'w2': jax.random.normal(k3, (E, H, D), jnp.float32) * sH, 'w3': jax.random.normal(k4, (E, D, H), jnp.float32) * sD}
    _L1_ffn_all = _L1_ffn_setup()
    _L1_ffn_in = {k: v for k, v in _L1_ffn_all.items() if k in ('gate_w', 'w1', 'w2', 'w3')}
    del _L1_ffn_all

    def _L2_xattn_setup():
        import jax, jax.numpy as jnp
        import numpy as np
        NUM_HEADS, NUM_KV, HEAD_DIM, WIDTH = (4, 1, 32, 128)
        MASK_FILL = -2.3819763e+38

        def _apply_rope(x, positions, max_wavelength=10000.0):
            d = x.shape[-1]
            freq_exp = 2.0 / d * jnp.arange(d // 2, dtype=jnp.float32)
            timescale = max_wavelength ** freq_exp
            radians = positions[..., None].astype(jnp.float32) / timescale
            radians = radians[..., None, :]
            sin, cos = (jnp.sin(radians), jnp.cos(radians))
            x1, x2 = jnp.split(x, 2, axis=-1)
            out = jnp.concatenate([x1 * cos - x2 * sin, x2 * cos + x1 * sin], axis=-1)
            return out.astype(x.dtype)

        def _rmsnorm(x, scale):
            var = jnp.mean(jnp.square(x.astype(jnp.float32)), axis=-1, keepdims=True)
            normed = x * jax.lax.rsqrt(var + 1e-06)
            return (normed * (1 + scale)).astype(x.dtype)
        key = jax.random.key(seed)
        ks = jax.random.split(key, 7)
        B, T, S = (8, 64, 256)
        return {'x': jax.random.normal(ks[0], (B, T, WIDTH), jnp.float32), 'mem_seq': jax.random.normal(ks[1], (B, S, WIDTH), jnp.float32), 'mem_mask': jax.random.randint(ks[2], (B, S), 0, 2).astype(bool), 'rms_scale': jax.random.normal(ks[3], (WIDTH,), jnp.float32) * 0.02, 'q_w': jax.random.normal(ks[4], (NUM_HEADS, WIDTH, HEAD_DIM), jnp.float32) / np.sqrt(WIDTH), 'kv_w': jax.random.normal(ks[5], (2, NUM_KV, WIDTH, HEAD_DIM), jnp.float32) / np.sqrt(WIDTH), 'out_w': jax.random.normal(ks[6], (NUM_HEADS, HEAD_DIM, WIDTH), jnp.float32) / np.sqrt(NUM_HEADS * HEAD_DIM)}
    _L2_xattn_all = _L2_xattn_setup()
    _L2_xattn_in = {k: v for k, v in _L2_xattn_all.items() if k in ('rms_scale', 'q_w', 'kv_w', 'out_w')}
    del _L2_xattn_all

    def _L2_ffn_setup():
        import jax, jax.numpy as jnp
        import numpy as np
        D_MODEL, D_FF, N_EXPERTS, TOP_K = (128, 512, 8, 2)
        B, S = (2, 256)
        key = jax.random.key(seed)
        ks = jax.random.split(key, 7)
        scale = 0.02
        return {'x': jax.random.normal(ks[0], (B, S, D_MODEL), dtype=jnp.float32), 'W1': jax.random.normal(ks[1], (N_EXPERTS, D_MODEL, D_FF), dtype=jnp.float32) * scale, 'b1': jnp.zeros((N_EXPERTS, D_FF), dtype=jnp.float32), 'W2': jax.random.normal(ks[2], (N_EXPERTS, D_FF, D_MODEL), dtype=jnp.float32) * scale, 'b2': jnp.zeros((N_EXPERTS, D_MODEL), dtype=jnp.float32), 'Wg': jax.random.normal(ks[3], (D_MODEL, N_EXPERTS), dtype=jnp.float32) * scale, 'bg': jnp.zeros((N_EXPERTS,), dtype=jnp.float32)}
    _L2_ffn_all = _L2_ffn_setup()
    _L2_ffn_in = {k: v for k, v in _L2_ffn_all.items() if k in ('W1', 'b1', 'W2', 'b2', 'Wg', 'bg')}
    del _L2_ffn_all

    def _L3_xattn_setup():
        import jax, jax.numpy as jnp
        import numpy as np
        EMBED_DIM = 128
        NUM_HEADS = 16
        HEAD_DIM = EMBED_DIM // NUM_HEADS
        ROPE_BASE = 10000.0

        def _apply_rope(q, position_ids):
            hd = q.shape[-1]
            inv_freq = 1.0 / ROPE_BASE ** (jnp.arange(0, hd, 2, dtype=jnp.float32) / hd)
            ang = position_ids.astype(jnp.float32)[:, :, None] * inv_freq
            cos = jnp.cos(ang)[:, :, None, :]
            sin = jnp.sin(ang)[:, :, None, :]
            q1, q2 = (q[..., :hd // 2], q[..., hd // 2:])
            return jnp.concatenate([q1 * cos - q2 * sin, q2 * cos + q1 * sin], axis=-1)
        key = jax.random.key(seed)
        ks = jax.random.split(key, 12)
        B, T, M, D = (4, 256, 256, EMBED_DIM)
        query = jax.random.normal(ks[0], (B, T, D), dtype=jnp.float32)
        k_in = jax.random.normal(ks[1], (B, M, D), dtype=jnp.float32)
        v_in = jax.random.normal(ks[2], (B, M, D), dtype=jnp.float32)
        query_position_ids = jnp.sort(jax.random.randint(ks[3], (B, T), 0, 512), axis=-1).astype(jnp.int64)
        lim = float(np.sqrt(6.0 / (D + D)))
        Wq = jax.random.uniform(ks[4], (D, D), minval=-lim, maxval=lim, dtype=jnp.float32)
        Wk = jax.random.uniform(ks[5], (D, D), minval=-lim, maxval=lim, dtype=jnp.float32)
        Wv = jax.random.uniform(ks[6], (D, D), minval=-lim, maxval=lim, dtype=jnp.float32)
        Wo = jax.random.uniform(ks[7], (D, D), minval=-lim, maxval=lim, dtype=jnp.float32)
        bq = jnp.zeros((D,), jnp.float32)
        bk = jnp.zeros((D,), jnp.float32)
        bv = jnp.zeros((D,), jnp.float32)
        bo = jnp.zeros((D,), jnp.float32)
        return dict(query=query, key=k_in, value=v_in, query_position_ids=query_position_ids, Wq=Wq, bq=bq, Wk=Wk, bk=bk, Wv=Wv, bv=bv, Wo=Wo, bo=bo)
    _L3_xattn_all = _L3_xattn_setup()
    _L3_xattn_in = {k: v for k, v in _L3_xattn_all.items() if k in ('Wq', 'bq', 'Wk', 'bk', 'Wv', 'bv', 'Wo', 'bo')}
    del _L3_xattn_all

    def _L3_ffn_setup():
        import jax, jax.numpy as jnp
        import numpy as np
        B, T, C, H, E = (4, 256, 128, 256, 8)
        CAPACITY_FACTOR = 1.0
        key = jax.random.key(seed)
        ks = jax.random.split(key, 5)
        scale = 0.02
        return {'x': jax.random.normal(ks[0], (B, T, C), dtype=jnp.float32), 'Wg': jax.random.normal(ks[1], (E, C), dtype=jnp.float32) * scale, 'W1': jax.random.normal(ks[2], (E, H, C), dtype=jnp.float32) * scale, 'W2': jax.random.normal(ks[3], (E, C, H), dtype=jnp.float32) * scale, 'W3': jax.random.normal(ks[4], (E, H, C), dtype=jnp.float32) * scale}
    _L3_ffn_all = _L3_ffn_setup()
    _L3_ffn_in = {k: v for k, v in _L3_ffn_all.items() if k in ('Wg', 'W1', 'W2', 'W3')}
    del _L3_ffn_all
    return {'x': x, 'ctx_1024': ctx_1024, 'itok_BxS_1_4095': itok_BxS_1_4095, 'mask_BxS2_bk0': mask_BxS2_bk0, 'g_xattn': g_xattn, 'g_ffn': g_ffn, 'L0_xattn_W_lin': _L0_xattn_in['W_lin'], 'L0_xattn_b_lin': _L0_xattn_in['b_lin'], 'L0_xattn_W_gate': _L0_xattn_in['W_gate'], 'L0_xattn_b_gate': _L0_xattn_in['b_gate'], 'L0_ffn_W_fc': _L0_ffn_in['W_fc'], 'L0_ffn_W_proj': _L0_ffn_in['W_proj'], 'L1_xattn_in_proj_weight': _L1_xattn_in['in_proj_weight'], 'L1_xattn_in_proj_bias': _L1_xattn_in['in_proj_bias'], 'L1_xattn_out_w': _L1_xattn_in['out_w'], 'L1_xattn_out_b': _L1_xattn_in['out_b'], 'L1_ffn_gate_w': _L1_ffn_in['gate_w'], 'L1_ffn_w1': _L1_ffn_in['w1'], 'L1_ffn_w2': _L1_ffn_in['w2'], 'L1_ffn_w3': _L1_ffn_in['w3'], 'L2_xattn_rms_scale': _L2_xattn_in['rms_scale'], 'L2_xattn_q_w': _L2_xattn_in['q_w'], 'L2_xattn_kv_w': _L2_xattn_in['kv_w'], 'L2_xattn_out_w': _L2_xattn_in['out_w'], 'L2_ffn_W1': _L2_ffn_in['W1'], 'L2_ffn_b1': _L2_ffn_in['b1'], 'L2_ffn_W2': _L2_ffn_in['W2'], 'L2_ffn_b2': _L2_ffn_in['b2'], 'L2_ffn_Wg': _L2_ffn_in['Wg'], 'L2_ffn_bg': _L2_ffn_in['bg'], 'L3_xattn_Wq': _L3_xattn_in['Wq'], 'L3_xattn_bq': _L3_xattn_in['bq'], 'L3_xattn_Wk': _L3_xattn_in['Wk'], 'L3_xattn_bk': _L3_xattn_in['bk'], 'L3_xattn_Wv': _L3_xattn_in['Wv'], 'L3_xattn_bv': _L3_xattn_in['bv'], 'L3_xattn_Wo': _L3_xattn_in['Wo'], 'L3_xattn_bo': _L3_xattn_in['bo'], 'L3_ffn_Wg': _L3_ffn_in['Wg'], 'L3_ffn_W1': _L3_ffn_in['W1'], 'L3_ffn_W2': _L3_ffn_in['W2'], 'L3_ffn_W3': _L3_ffn_in['W3']}

def reference(x, ctx_1024, itok_BxS_1_4095, mask_BxS2_bk0, g_xattn, g_ffn, L0_xattn_W_lin, L0_xattn_b_lin, L0_xattn_W_gate, L0_xattn_b_gate, L0_ffn_W_fc, L0_ffn_W_proj, L1_xattn_in_proj_weight, L1_xattn_in_proj_bias, L1_xattn_out_w, L1_xattn_out_b, L1_ffn_gate_w, L1_ffn_w1, L1_ffn_w2, L1_ffn_w3, L2_xattn_rms_scale, L2_xattn_q_w, L2_xattn_kv_w, L2_xattn_out_w, L2_ffn_W1, L2_ffn_b1, L2_ffn_W2, L2_ffn_b2, L2_ffn_Wg, L2_ffn_bg, L3_xattn_Wq, L3_xattn_bq, L3_xattn_Wk, L3_xattn_bk, L3_xattn_Wv, L3_xattn_bv, L3_xattn_Wo, L3_xattn_bo, L3_ffn_Wg, L3_ffn_W1, L3_ffn_W2, L3_ffn_W3):
    import jax
    import jax.numpy as jnp

    def _L0_xattn_ref(query, context, W_lin, b_lin, W_gate, b_gate, smooth):
        import jax, jax.numpy as jnp
        import numpy as np
        EPS = 1e-08
        B, Q, S, D = (128, 32, 64, 128)

        def l2norm(x, axis):
            norm = jnp.sqrt(jnp.sum(x * x, axis=axis, keepdims=True) + EPS) + EPS
            return x / norm
        attn = jnp.einsum('bsd,bqd->bsq', context, query)
        attn = jax.nn.leaky_relu(attn, negative_slope=0.1)
        attn = l2norm(attn, axis=2)
        a = jax.nn.softmax(jnp.swapaxes(attn, 1, 2) * smooth, axis=2)
        weighted_ctx = jnp.einsum('bqs,bsd->bqd', a, context)
        cat = jnp.concatenate([query, weighted_ctx], axis=2)
        h = jnp.tanh(cat @ W_lin + b_lin)
        g = jax.nn.sigmoid(cat @ W_gate + b_gate)
        return query * g + h * (1.0 - g)

    def _L0_ffn_ref(x, W_fc, W_proj):
        import jax, jax.numpy as jnp
        import numpy as np
        import math
        BETA = 0.9
        THRESHOLD = 1.0
        NUM_STEPS = 5
        ALPHA = 2.0

        @jax.custom_vjp
        def spike_fn(u):
            return (u > 0).astype(u.dtype)

        def _spike_fwd(u):
            return (spike_fn(u), u)

        def _spike_bwd(u, g):
            s = jnp.pi / 2.0 * ALPHA * u
            return (g * (ALPHA / 2.0) / (1.0 + s * s),)
        spike_fn.defvjp(_spike_fwd, _spike_bwd)
        h = jnp.square(jax.nn.relu(jnp.einsum('bsd,fd->bsf', x, W_fc)))
        y = jnp.einsum('bsf,df->bsd', h, W_proj)

        def step(mem, _):
            reset = jax.lax.stop_gradient(spike_fn(mem - THRESHOLD))
            mem_new = BETA * mem + y - reset * THRESHOLD
            spk = spike_fn(mem_new - THRESHOLD)
            return (mem_new, spk)
        mem0 = jnp.zeros_like(y)
        _, spks = jax.lax.scan(step, mem0, None, length=NUM_STEPS)
        return jnp.sum(spks, axis=0) / NUM_STEPS

    def _L1_xattn_ref(q, k, v, in_proj_weight, in_proj_bias, out_w, out_b):
        import jax, jax.numpy as jnp
        import numpy as np
        EMBED_DIM = 128
        NUM_HEADS = 16
        HEAD_DIM = EMBED_DIM // NUM_HEADS
        B, T, S = (2, 256, 256)
        H, D = (NUM_HEADS, HEAD_DIM)
        w_q, w_k, w_v = jnp.split(in_proj_weight, 3, axis=0)
        b_q, b_k, b_v = jnp.split(in_proj_bias, 3, axis=0)
        qp = q @ w_q.T + b_q
        kp = k @ w_k.T + b_k
        vp = v @ w_v.T + b_v
        bsz, t, _ = qp.shape
        s = kp.shape[1]
        qh = qp.reshape(bsz, t, H, D).transpose(0, 2, 1, 3)
        kh = kp.reshape(bsz, s, H, D).transpose(0, 2, 1, 3)
        vh = vp.reshape(bsz, s, H, D).transpose(0, 2, 1, 3)
        scale = D ** (-0.5)
        attn = jnp.einsum('bhtd,bhsd->bhts', qh, kh) * scale
        attn = jax.nn.softmax(attn, axis=-1)
        ctx = jnp.einsum('bhts,bhsd->bhtd', attn, vh)
        ctx = ctx.transpose(0, 2, 1, 3).reshape(bsz, t, H * D)
        out = ctx @ out_w.T + out_b
        return out

    def _L1_ffn_ref(hidden_states, gate_w, w1, w2, w3):
        import jax, jax.numpy as jnp
        import numpy as np
        E, K, D, H = (8, 2, 128, 256)
        B, S = (1, 128)

        def _grouped_swiglu(x_sorted, counts, w1, w2, w3):
            if hasattr(jax.lax, 'ragged_dot'):
                gs = counts.astype(jnp.int32)
                h = jax.nn.silu(jax.lax.ragged_dot(x_sorted, w1, gs)) * jax.lax.ragged_dot(x_sorted, w3, gs)
                return jax.lax.ragged_dot(h, w2, gs)
            pos = jnp.arange(x_sorted.shape[0])
            eid = jnp.searchsorted(jnp.cumsum(counts), pos, side='right')
            out = jnp.zeros((x_sorted.shape[0], w2.shape[-1]), x_sorted.dtype)
            for e in range(w1.shape[0]):
                xm = jnp.where((eid == e)[:, None], x_sorted, 0.0)
                he = jax.nn.silu(xm @ w1[e]) * (xm @ w3[e])
                out = out + he @ w2[e]
            return out
        x = hidden_states.reshape(-1, D)
        N = x.shape[0]
        scores = jax.nn.softmax(x @ gate_w.T, axis=-1)
        top_scores, sel = jax.lax.top_k(scores, K)
        sel_flat = sel.T.reshape(-1)
        scores_flat = top_scores.T.reshape(-1)
        order = jnp.argsort(sel_flat, stable=True)
        tok_sorted = order % N
        scores_sorted = scores_flat[order]
        counts = jnp.bincount(sel_flat, length=E)
        x_sorted = x[tok_sorted]
        y = _grouped_swiglu(x_sorted, counts, w1, w2, w3)
        weighted = y * scores_sorted[:, None]
        out = jnp.zeros((N, D), x.dtype).at[tok_sorted].add(weighted)
        return out.reshape(hidden_states.shape)

    def _L2_xattn_ref(x, mem_seq, mem_mask, rms_scale, q_w, kv_w, out_w):
        import jax, jax.numpy as jnp
        import numpy as np
        NUM_HEADS, NUM_KV, HEAD_DIM, WIDTH = (4, 1, 32, 128)
        MASK_FILL = -2.3819763e+38

        def _apply_rope(x, positions, max_wavelength=10000.0):
            d = x.shape[-1]
            freq_exp = 2.0 / d * jnp.arange(d // 2, dtype=jnp.float32)
            timescale = max_wavelength ** freq_exp
            radians = positions[..., None].astype(jnp.float32) / timescale
            radians = radians[..., None, :]
            sin, cos = (jnp.sin(radians), jnp.cos(radians))
            x1, x2 = jnp.split(x, 2, axis=-1)
            out = jnp.concatenate([x1 * cos - x2 * sin, x2 * cos + x1 * sin], axis=-1)
            return out.astype(x.dtype)

        def _rmsnorm(x, scale):
            var = jnp.mean(jnp.square(x.astype(jnp.float32)), axis=-1, keepdims=True)
            normed = x * jax.lax.rsqrt(var + 1e-06)
            return (normed * (1 + scale)).astype(x.dtype)
        B, S, _ = mem_seq.shape
        T = x.shape[1]
        G = NUM_HEADS // NUM_KV
        xn = _rmsnorm(x, rms_scale)
        mn = _rmsnorm(mem_seq, rms_scale)
        q = jnp.einsum('BTD,NDH->BTNH', xn, q_w)
        kv = jnp.einsum('BSD,cKDH->cBSKH', mn, kv_w)
        k, v = (kv[0], kv[1])
        q_pos = jnp.broadcast_to(jnp.arange(S, T + S), (B, T))
        k_pos = jnp.broadcast_to(jnp.arange(S), (B, S))
        q = _apply_rope(q, q_pos) * HEAD_DIM ** (-0.5)
        k = _apply_rope(k, k_pos)
        q = q.reshape(B, T, NUM_KV, G, HEAD_DIM)
        logits = jnp.einsum('BTKGH,BSKH->BKGTS', q, k, preferred_element_type=jnp.float32)
        masked = jnp.where(mem_mask[:, None, None, None, :], logits, MASK_FILL)
        probs = jax.nn.softmax(masked, axis=-1).astype(x.dtype)
        enc = jnp.einsum('BKGTS,BSKH->BTKGH', probs, v).reshape(B, T, NUM_HEADS, HEAD_DIM)
        return jnp.einsum('BTNH,NHD->BTD', enc, out_w)

    def _L2_ffn_ref(x, W1, b1, W2, b2, Wg, bg):
        import jax, jax.numpy as jnp
        import numpy as np
        D_MODEL, D_FF, N_EXPERTS, TOP_K = (128, 512, 8, 2)
        B, S = (2, 256)
        Bx, Sx, d = x.shape
        E = W1.shape[0]
        logits = jnp.einsum('bsd,de->bse', x, Wg) + bg
        topk_scores, topk_idx = jax.lax.top_k(logits, TOP_K)
        topk_scores = jax.nn.softmax(topk_scores, axis=-1)
        tokens = x.reshape(-1, d)
        idx_flat = topk_idx.reshape(-1, TOP_K)
        sc_flat = topk_scores.reshape(-1, TOP_K)
        comb = (jax.nn.one_hot(idx_flat, E, dtype=x.dtype) * sc_flat[..., None]).sum(axis=1)
        h = jnp.einsum('td,edf->etf', tokens, W1) + b1[:, None, :]
        even = (jnp.arange(E) % 2 == 0)[:, None, None]
        a = jnp.where(even, jax.nn.gelu(h, approximate=False), jax.nn.silu(h))
        y = jnp.einsum('etf,efd->etd', a, W2) + b2[:, None, :]
        out = jnp.einsum('te,etd->td', comb, y)
        return out.reshape(Bx, Sx, d)

    def _L3_xattn_ref(query, key, value, query_position_ids, Wq, bq, Wk, bk, Wv, bv, Wo, bo):
        import jax, jax.numpy as jnp
        import numpy as np
        EMBED_DIM = 128
        NUM_HEADS = 16
        HEAD_DIM = EMBED_DIM // NUM_HEADS
        ROPE_BASE = 10000.0

        def _apply_rope(q, position_ids):
            hd = q.shape[-1]
            inv_freq = 1.0 / ROPE_BASE ** (jnp.arange(0, hd, 2, dtype=jnp.float32) / hd)
            ang = position_ids.astype(jnp.float32)[:, :, None] * inv_freq
            cos = jnp.cos(ang)[:, :, None, :]
            sin = jnp.sin(ang)[:, :, None, :]
            q1, q2 = (q[..., :hd // 2], q[..., hd // 2:])
            return jnp.concatenate([q1 * cos - q2 * sin, q2 * cos + q1 * sin], axis=-1)
        B, T, D = query.shape
        M = key.shape[1]
        H, hd = (NUM_HEADS, HEAD_DIM)
        scaling = 1.0 / np.sqrt(hd)
        q = (query @ Wq.T + bq).reshape(B, T, H, hd)
        k = (key @ Wk.T + bk).reshape(B, M, H, hd)
        v = (value @ Wv.T + bv).reshape(B, M, H, hd)
        q = _apply_rope(q, query_position_ids)
        scores = jnp.einsum('bthd,bmhd->bhtm', q, k) * scaling
        attn = jax.nn.softmax(scores, axis=-1)
        out = jnp.einsum('bhtm,bmhd->bthd', attn, v).reshape(B, T, D)
        return out @ Wo.T + bo

    def _L3_ffn_ref(x, Wg, W1, W2, W3):
        import jax, jax.numpy as jnp
        import numpy as np
        B, T, C, H, E = (4, 256, 128, 256, 8)
        CAPACITY_FACTOR = 1.0
        b, t, c = x.shape
        e = Wg.shape[0]
        n = b * t
        capacity = max(1, int(CAPACITY_FACTOR * n / e))
        x_flat = x.reshape(n, c)
        scores = (x_flat @ Wg.T).T
        top_vals, token_idx = jax.lax.top_k(scores, capacity)
        token_w = jax.nn.softmax(top_vals, axis=-1)
        xg = x_flat[token_idx]
        h = jax.nn.silu(jnp.einsum('eic,ehc->eih', xg, W1)) * jnp.einsum('eic,ehc->eih', xg, W3)
        y = jnp.einsum('eih,ech->eic', h, W2) * token_w[..., None]
        out = jnp.zeros_like(x_flat).at[token_idx.reshape(-1)].add(y.reshape(-1, c))
        return out.reshape(b, t, c)
    x = x + jnp.tanh(g_xattn[0]) * _L0_xattn_ref(_layernorm(x, axis=-1), ctx_1024, L0_xattn_W_lin, L0_xattn_b_lin, L0_xattn_W_gate, L0_xattn_b_gate, 9)
    x = x + jnp.tanh(g_ffn[0]) * _L0_ffn_ref(_layernorm(x, axis=-1), L0_ffn_W_fc, L0_ffn_W_proj)
    x = x + jnp.tanh(g_xattn[1]) * _L1_xattn_ref(_layernorm(x, axis=-1), ctx_1024, ctx_1024, L1_xattn_in_proj_weight, L1_xattn_in_proj_bias, L1_xattn_out_w, L1_xattn_out_b)
    x = x + jnp.tanh(g_ffn[1]) * _L1_ffn_ref(_layernorm(x, axis=-1), L1_ffn_gate_w, L1_ffn_w1, L1_ffn_w2, L1_ffn_w3)
    x = x + jnp.tanh(g_xattn[2]) * _L2_xattn_ref(_layernorm(x, axis=-1), ctx_1024, mask_BxS2_bk0, L2_xattn_rms_scale, L2_xattn_q_w, L2_xattn_kv_w, L2_xattn_out_w)
    x = x + jnp.tanh(g_ffn[2]) * _L2_ffn_ref(_layernorm(x, axis=-1), L2_ffn_W1, L2_ffn_b1, L2_ffn_W2, L2_ffn_b2, L2_ffn_Wg, L2_ffn_bg)
    x = x + jnp.tanh(g_xattn[3]) * _L3_xattn_ref(_layernorm(x, axis=-1), ctx_1024, ctx_1024, itok_BxS_1_4095, L3_xattn_Wq, L3_xattn_bq, L3_xattn_Wk, L3_xattn_bk, L3_xattn_Wv, L3_xattn_bv, L3_xattn_Wo, L3_xattn_bo)
    x = x + jnp.tanh(g_ffn[3]) * _L3_ffn_ref(_layernorm(x, axis=-1), L3_ffn_Wg, L3_ffn_W1, L3_ffn_W2, L3_ffn_W3)
    return x

_drawn_inputs = setup_inputs


def setup_inputs(seed=0):
    import zlib

    import numpy as np

    out = dict(_drawn_inputs(seed))
    spreads = {'L0_xattn_b_lin': (0.0, 0.1),
     'L0_xattn_b_gate': (0.0, 0.357),
     'L1_xattn_in_proj_bias': (0.0, 0.1),
     'L1_xattn_out_b': (0.0, 0.1),
     'L2_ffn_b1': (0.0, 0.8),
     'L2_ffn_b2': (0.0, 0.1),
     'L2_ffn_bg': (0.0, 0.306),
     'L3_xattn_bq': (0.0, 0.706),
     'L3_xattn_bk': (0.0, 0.8),
     'L3_xattn_bv': (0.0, 0.1),
     'L3_xattn_bo': (0.0, 0.1)}
    factors = {'g_ffn': 8.0,
     'L2_xattn_rms_scale': 7.83,
     'L2_ffn_W1': 3.383,
     'L2_ffn_W2': 3.088,
     'L3_ffn_Wg': 8.0,
     'L3_ffn_W1': 8.0,
     'L3_ffn_W2': 8.0,
     'L3_ffn_W3': 8.0}
    for name, (base, spread) in spreads.items():
        noise = np.random.default_rng([zlib.crc32(name.encode()), seed]).standard_normal(out[name].shape)
        drawn = base * np.exp(spread * noise) if base else spread * noise
        out[name] = jnp.asarray(drawn.astype(out[name].dtype))
    for name, factor in factors.items():
        out[name] = (out[name] * factor).astype(out[name].dtype)
    return out
```

```python
from contextlib import ExitStack

import numpy as np

import concourse.bass as bass
from concourse import mybir

ALU = mybir.AluOpType
ACT = mybir.ActivationFunctionType
AX = mybir.AxisListType
F32 = mybir.dt.float32
BF16 = mybir.dt.bfloat16
F16 = mybir.dt.float16
I32 = mybir.dt.int32
U32 = mybir.dt.uint32
U8 = mybir.dt.uint8

P = 128
B, T, D = 32, 128, 128
S = 77
NT = B * T // P
E = 8
LN_EPS = 1e-5


def cnt(value):
    return max(value, 0) if isinstance(value, int) else value


def span(n, size):
    return bass.ds(n * size, size)


class Unit:

    def __init__(self, i, w, unroll):
        self.n, self.v, self.round = i * unroll + w, w % unroll, i + w // unroll
        self.two = self.v % 2


def pipeline(eng, units, lag, unroll, step):
    first, full = -(-(lag + unroll) // unroll), units // unroll

    def straight(t):
        step(lambda k: Unit(0, t - k, unroll) if 0 <= t - k < units else None)

    for t in range(first * unroll):
        straight(t)
    with eng.Fori(first, full) as i:
        for u in range(unroll):
            step(lambda k, u=u: Unit(i, u - k, unroll))
    for t in range(full * unroll, units + lag):
        straight(t)


class Chain:

    def __init__(self, eng, sem, base=0):
        self.eng, self.sem, self.base, self.n = eng, sem, base, 0

    def mark(self, instruction):
        self.n += 1
        instruction.then_inc(self.sem, 1)

    def link(self, instruction):
        self.mark(instruction)
        self.eng.wait_ge(self.sem, self.base + self.n)


class Memory:

    used = []

    def __init__(self, nc, ctx, prefix):
        self.nc, self.ctx, self.prefix = nc, ctx, prefix

    def sb(self, name, shape, dtype=F32):
        return self.ctx.enter_context(self.nc.sbuf_tensor(f"{self.prefix}_{name}", shape, dtype))

    def ps(self, name, shape=(P, 512), dtype=F32):
        return self.ctx.enter_context(self.nc.psum_tensor(f"{self.prefix}_{name}", list(shape), dtype))

    def sem(self, name):
        handle = self.nc.alloc_semaphore(name=f"{self.prefix}_{name}")
        self.used.append(handle)
        return handle


def recycle_semaphores(nc):
    nc.clear_and_free_semaphores(Memory.used)
    Memory.used.clear()
    nc.all_engine_barrier()


def row_bcast(ap, parts=P):
    n = ap.shape[-1]
    return ap.rearrange("(o n) -> o n", o=1).broadcast_to([parts, n])


def load_inputs(nc, g, io):
    with ExitStack() as ctx:
        block = ctx.enter_context(nc.Block())

        @block.sync
        def _(sp):
            for dst, src in g.loads["start"]:
                sp.dma_start(dst, src).then_inc(g.start_in, 16)
            for half in range(2):
                tiles = slice(half * NT // 2, (half + 1) * NT // 2)
                sp.dma_start(g.x[:, tiles, :], io["x"][:, tiles, :]).then_inc(g.x_in, 16)
            for name in ("L0a", "L0f", "L1a", "moe", "L1f"):
                for dst, src in g.loads[name]:
                    sp.dma_start(dst, src).then_inc(g.weights_in[name], 16)

        @block.gpsimd
        def _(pool):
            for name in ("L2a", "L2f", "L3a", "L3c"):
                for dst, src in g.loads[name]:
                    pool.dma_start(dst, src).then_inc(g.weights_in[name], 16)

        @block.scalar
        def _(act):
            act.wait_ge(g.start_in, 16 * len(g.loads["start"]))
            act.activation(g.tanh_gate[:, :], g.gates[:, :], ACT.Tanh).then_inc(g.gates_done, 1)

        @block.vector
        def _(dve):
            dve.wait_ge(g.x_in, 32)
            dve.memset(g.carrier[:, :], 0.0)
            dve.memset(g.ones[:, :], 1.0)
            dve.memset(g.ones16[:, :], 1.0)
            dve.memset(g.bias_router[:, 0, :], 0.0)
            with dve.Fori(0, NT // 4) as i:
                for u in range(4):
                    dve.bn_stats(tile_of(g.bn6, i * 4 + u), tile_of(g.x, i * 4 + u)).then_inc(g.stat6, 1)
            dve.wait_ge(g.stat6, NT)


def load_later(nc, g):
    with nc.Block() as block:
        @block.sync
        def _(sp):
            sp.wait_ge(g.weights_in["L1f"], 16 * len(g.loads["L1f"]))
            for dst, src in g.loads["L3f"]:
                sp.dma_start(dst, src).then_inc(g.weights_in["L3f"], 16)


def rstd_block(nc, g, name, rms=False):
    with ExitStack() as ctx:
        m = Memory(nc, ctx, name)
        a, b = m.sb("a", [P, NT]), m.sb("b", [P, NT])
        shifted, rooted = m.sem("shifted"), m.sem("rooted")
        STEPS = 8
        block = ctx.enter_context(nc.Block())
        even, odd = g.bn6[:, :, 1], g.bn6[:, :, 4]
        even2, odd2 = g.bn6[:, :, 2], g.bn6[:, :, 5]
        mean, var = g.mv[:, :, 0], g.mv[:, :, 1]

        @block.vector
        def _(dve):
            ch = Chain(dve, shifted)
            ch.link(dve.tensor_tensor(a[:, :], even, odd, ALU.subtract))
            ch.link(dve.tensor_tensor(a[:, :], a[:, :], a[:, :], ALU.mult))
            ch.link(dve.tensor_tensor(b[:, :], even2, odd2, ALU.add))
            ch.link(dve.tensor_scalar(b[:, :], b[:, :], 1.0 / D, None, ALU.mult))
            ch.link(dve.scalar_tensor_tensor(var, a[:, :], 0.25, b[:, :], ALU.mult, ALU.add))
            ch.link(dve.tensor_tensor(b[:, :], even, odd, ALU.add))
            ch.link(dve.tensor_scalar(mean, b[:, :], 0.5, None, ALU.mult))
            ch.mark(dve.tensor_scalar(a[:, :], var, LN_EPS, None, ALU.add))
            assert ch.n == STEPS
            dve.wait_ge(rooted, 1)
            ch.link(dve.reciprocal(g.rstd[:, :], b[:, :]))
            if rms:
                ch.link(dve.tensor_tensor(a[:, :], g.rstd[:, :], g.rstd[:, :], ALU.mult))
                ch.link(dve.tensor_tensor(a[:, :], a[:, :], var, ALU.mult))
                ch.mark(dve.tensor_scalar(a[:, :], a[:, :], 1e-6, None, ALU.add))
                dve.wait_ge(rooted, 2)
                ch.link(dve.reciprocal(a[:, :], b[:, :]))
                ch.link(dve.tensor_tensor(g.rstd[:, :], g.rstd[:, :], a[:, :], ALU.mult))

        @block.scalar
        def _(act):
            act.wait_ge(shifted, STEPS)
            act.activation(b[:, :], a[:, :], ACT.Sqrt).then_inc(rooted, 1)
            if rms:
                act.wait_ge(shifted, STEPS + 4)
                act.activation(b[:, :], a[:, :], ACT.Sqrt).then_inc(rooted, 1)


def layer_norm(dve, g, out, n):
    return dve.tensor_scalar(out, tile_of(g.x, n), mv_of(g, n)[:, 0:1], g.rstd[:, bass.ds(n, 1)],
                             ALU.subtract, ALU.mult)


def mv_of(g, n):
    return g.mv[:, bass.ds(n, 1), :].rearrange("p a c -> p (a c)")


def tile_of(tensor, n):
    return tensor[:, bass.ds(n, 1), :].rearrange("p a d -> p (a d)")


ADD_STEPS = 2


def add_into_x(dve, g, ch, value, scale, n):
    ch.mark(dve.scalar_tensor_tensor(tile_of(g.x, n), value, scale, tile_of(g.x, n), ALU.mult, ALU.add))
    tile_stats(dve, g, ch, n)


def tile_stats(dve, g, ch, n):
    dve.wait_ge(ch.sem, ch.base + ch.n)
    dve.tensor_scalar(g.carrier[:, 0:1], g.carrier[:, 1:2], 0.0, None, ALU.mult)
    ch.mark(dve.bn_stats(tile_of(g.bn6, n), tile_of(g.x, n)))


def l0_attention(nc, g, io):
    with ExitStack() as outer:
        mo = Memory(nc, outer, "a0")
        attn = mo.sb("attn", [S, NT, T])
        sumsq = mo.sb("sumsq", [S, NT])
        root = mo.sb("root", [S, NT])
        nine = mo.sb("nine", [S, NT])
        xn_all = mo.sb("xn_all", [P, NT, D])
        xT_all = mo.sb("xT_all", [P, NT, T])
        l0_scores(nc, g, io, attn, sumsq, xn_all, xT_all)
        l0_norms(nc, g, sumsq, root, nine)
        l0_mix(nc, g, io, attn, nine, xn_all, xT_all)


def l0_scores(nc, g, io, attn, sumsq, xn_all, xT_all):
    with ExitStack() as ctx:
        m = Memory(nc, ctx, "a0s")
        xn = m.sb("xn", [P, 2, D])
        xT = m.sb("xT", [P, 2, T])
        ctxT = m.sb("ctxT", [P, 4, S])
        tenth = m.sb("tenth", [S, 2, T])
        junk = m.sb("junk", [S, 2, T])
        pT = [m.ps(f"pT{i}") for i in range(2)]
        pS = [m.ps(f"pS{i}") for i in range(2)]
        ctx_in = [m.sem(f"ctx_in{i}") for i in range(4)]
        normed, turned, copied, scored, tenthed, leaked, squared = (
            m.sem(k) for k in ("normed", "turned", "copied", "scored", "tenthed", "leaked", "squared"))
        block = ctx.enter_context(nc.Block())

        @block.sync
        def _(sp):
            def step(at):
                if k := at(0):
                    sp.wait_ge(scored, cnt(k.n - 3))
                    sp.dma_start(ctxT[:, k.v, :], io["ctxT"][bass.ds(k.n, 1), :, :].rearrange("a p s -> p (a s)")
                                 ).then_inc(ctx_in[k.v], 16)
            pipeline(sp, NT, 0, 4, step)

        @block.vector
        def _(dve):
            def step(at):
                if k := at(0):
                    dve.wait_ge(turned, cnt(k.n - 1))
                    layer_norm(dve, g, xn[:, k.two, :], k.n).then_inc(normed, 1)
                    layer_norm(dve, g, tile_of(xn_all, k.n), k.n).then_inc(normed, 1)
                if k := at(2):
                    dve.wait_ge(tenthed, k.n + 1)
                    dve.tensor_tensor(tile_of(attn, k.n), pS[k.two][0:S, 0:T], tenth[:, k.two, :],
                                      ALU.max).then_inc(leaked, 1)
            pipeline(dve, NT, 3, 4, step)

        @block.tensor
        def _(pe):
            def step(at):
                if k := at(0):
                    pe.wait_ge(normed, k.n * 2 + 1)
                    pe.wait_ge(copied, cnt(k.n * 2 - 2))
                    pe.transpose(pT[k.two][:, 0:T], xn[:, k.two, :], g.ident[:, :]).then_inc(turned, 1)
                if k := at(1):
                    pe.wait_ge(ctx_in[k.v], k.round * 16 + 16)
                    pe.wait_ge(copied, k.n * 2 + 1)
                    pe.wait_ge(leaked, cnt(k.n - 1))
                    pe.matmul(pS[k.two][0:S, 0:T], ctxT[:, k.v, :], xT[:, k.two, :],
                              start=True, stop=True).then_inc(scored, 1)
            pipeline(pe, NT, 3, 4, step)

        @block.scalar
        def _(act):
            def step(at):
                if k := at(0):
                    act.wait_ge(turned, k.n + 1)
                    act.wait_ge(scored, cnt(k.n - 1))
                    act.copy(xT[:, k.two, :], pT[k.two][:, 0:T]).then_inc(copied, 1)
                    act.copy(tile_of(xT_all, k.n), pT[k.two][:, 0:T]).then_inc(copied, 1)
                if k := at(1):
                    act.wait_ge(scored, k.n + 1)
                    act.wait_ge(leaked, cnt(k.n - 1))
                    act.mul(tenth[:, k.two, :], pS[k.two][0:S, 0:T], 0.1).then_inc(tenthed, 1)
                if k := at(3):
                    act.wait_ge(leaked, k.n + 1)
                    act.wait_ge(squared, cnt(k.n - 1))
                    act.activation(junk[:, k.two, :], tile_of(attn, k.n), ACT.Square,
                                   accum_out=sumsq[:, bass.ds(k.n, 1)]).then_inc(squared, 1)
            pipeline(act, NT, 3, 4, step)


def l0_norms(nc, g, sumsq, root, nine):
    with ExitStack() as ctx:
        m = Memory(nc, ctx, "a0n")
        shifted, rooted = m.sem("shifted"), m.sem("rooted")
        block = ctx.enter_context(nc.Block())

        @block.vector
        def _(dve):
            ch = Chain(dve, shifted)
            ch.mark(dve.tensor_scalar(sumsq[:, :], sumsq[:, :], 1e-8, None, ALU.add))
            dve.wait_ge(rooted, 1)
            ch.link(dve.tensor_scalar(root[:, :], root[:, :], 1e-8, None, ALU.add))
            ch.link(dve.reciprocal(nine[:, :], root[:, :]))
            ch.link(dve.tensor_scalar(nine[:, :], nine[:, :], 9.0, None, ALU.mult))

        @block.scalar
        def _(act):
            act.wait_ge(shifted, 1)
            act.activation(root[:, :], sumsq[:, :], ACT.Sqrt).then_inc(rooted, 1)


def l0_mix(nc, g, io, attn, nine, xn_all, xT_all):
    with ExitStack() as ctx:
        m = Memory(nc, ctx, "a0b")
        N2 = 2 * D
        ex = m.sb("ex", [S, 2, T])
        xT = m.sb("xT", [P, 2, T])
        numT = m.sb("numT", [P, 2, T])
        ctxr = m.sb("ctxr", [S, 4, D])
        ones = m.sb("ones", [S, 1])
        rden = m.sb("rden", [P, 2, 1])
        za, z, h = m.sb("za", [P, 2, N2]), m.sb("z", [P, 2, N2]), m.sb("h", [P, 2, N2])
        mix = m.sb("mix", [P, 2, D])
        junk = m.sb("junk", [S, 2, D])
        summed_ctx = m.sem("summed_ctx")
        pN, pA, pB = ([m.ps(f"{k}{i}") for i in range(2)] for k in ("pN", "pA", "pB"))
        ctx_in = [m.sem(f"ctx_in{i}") for i in range(4)]
        ready, exped, summed, num_copied, x_copied, x_part, ctx_part, added, divided, tanhed, mixed = (
            m.sem(k) for k in ("ready", "exped", "summed", "num_copied", "x_copied", "x_part", "ctx_part", "added",
                               "divided", "tanhed", "mixed"))
        K = 3 + ADD_STEPS
        block = ctx.enter_context(nc.Block())

        @block.sync
        def _(sp):
            def step(at):
                if k := at(0):
                    sp.wait_ge(summed, cnt(k.n - 3))
                    sp.wait_ge(summed_ctx, cnt(k.n - 3))
                    sp.dma_start(ctxr[:, k.v, :], io["ctx"][bass.ds(k.n, 1), :, :].rearrange("a s d -> s (a d)")
                                 ).then_inc(ctx_in[k.v], 16)
            pipeline(sp, NT, 0, 4, step)

        @block.gpsimd
        def _(pool):
            pool.memset(ones[:, :], 1.0).then_inc(ready, 1)

        @block.scalar
        def _(act):
            def step(at):
                if k := at(0):
                    act.wait_ge(ctx_in[k.v], k.round * 16 + 16)
                    act.wait_ge(summed_ctx, cnt(k.n - 1))
                    act.activation(junk[:, k.two, :], ctxr[:, k.v, :], ACT.Square,
                                   accum_out=g.ctx_sum2[:, bass.ds(k.n, 1)]).then_inc(summed_ctx, 1)
                    act.wait_ge(summed, cnt(k.n - 1))
                    act.activation(ex[:, k.two, :], tile_of(attn, k.n), ACT.Exp,
                                   scale=nine[:, bass.ds(k.n, 1)]).then_inc(exped, 1)
                    act.wait_ge(x_part, cnt(k.n - 1))
                    act.copy(xT[:, k.two, :], tile_of(xT_all, k.n)).then_inc(x_copied, 1)
                if k := at(1):
                    act.wait_ge(summed, k.n + 1)
                    act.wait_ge(ctx_part, cnt(k.n - 1))
                    act.copy(numT[:, k.two, :], pN[k.two][:, 0:T]).then_inc(num_copied, 1)
                if k := at(3):
                    act.wait_ge(divided, k.n * 2 + 2)
                    act.wait_ge(mixed, cnt(k.n - 1) * K)
                    act.activation(h[:, k.two, 0:D], z[:, k.two, 0:D], ACT.Tanh).then_inc(tanhed, 1)
                    act.activation(h[:, k.two, D:N2], z[:, k.two, D:N2], ACT.Tanh, scale=0.5).then_inc(tanhed, 1)
            pipeline(act, NT, 4, 4, step)

        @block.tensor
        def _(pe):
            pe.wait_ge(ready, 1)
            pe.wait_ge(g.weights_in["L0a"], 16 * len(g.loads["L0a"]))

            def step(at):
                if k := at(2):
                    pe.wait_ge(num_copied, k.n + 1)
                    pe.wait_ge(divided, cnt(k.n * 2 - 2))
                    pe.matmul(pB[k.two][:, 0:N2], numT[:, k.two, :], g.w_l0[:, 1, :], start=True,
                              stop=True).then_inc(ctx_part, 1)
                if k := at(0):
                    pe.wait_ge(exped, k.n + 1)
                    pe.wait_ge(ctx_in[k.v], k.round * 16 + 16)
                    pe.wait_ge(divided, cnt(k.n * 2 - 3))
                    pe.matmul(pN[k.two][:, 0:T], ctxr[:, k.v, :], ex[:, k.two, :], start=True, stop=True)
                    pe.matmul(pN[k.two][:, T:T + 1], ex[:, k.two, :], ones[:, :], start=True,
                              stop=True).then_inc(summed, 1)
                    pe.wait_ge(x_copied, k.n + 1)
                    pe.wait_ge(added, cnt(k.n - 1))
                    pe.matmul(pA[k.two][:, 0:N2], xT[:, k.two, :], g.w_l0[:, 0, :], start=True,
                              stop=True).then_inc(x_part, 1)
            pipeline(pe, NT, 4, 4, step)

        @block.vector
        def _(dve):
            dve.wait_ge(g.weights_in["L0a"], 16 * len(g.loads["L0a"]))
            dve.wait_ge(g.gates_done, 1)

            def step(at):
                if k := at(1):
                    dve.wait_ge(x_part, k.n + 1)
                    dve.wait_ge(divided, cnt(k.n * 2 - 2))
                    dve.tensor_tensor(za[:, k.two, :], pA[k.two][:, 0:N2], g.b_l0[:, :], ALU.add).then_inc(added, 1)
                if k := at(2):
                    dve.wait_ge(num_copied, k.n + 1)
                    dve.reciprocal(rden[:, k.two, :], pN[k.two][:, T:T + 1]).then_inc(divided, 1)
                    dve.wait_ge(divided, k.n * 2 + 1)
                    dve.wait_ge(ctx_part, k.n + 1)
                    dve.wait_ge(added, k.n + 1)
                    dve.wait_ge(tanhed, cnt(k.n - 1) * 2)
                    dve.scalar_tensor_tensor(z[:, k.two, :], pB[k.two][:, 0:N2], rden[:, k.two, :], za[:, k.two, :],
                                             ALU.mult, ALU.add).then_inc(divided, 1)
                if k := at(4):
                    ch = Chain(dve, mixed, k.n * K)
                    hh, tt, mm = h[:, k.two, 0:D], h[:, k.two, D:N2], mix[:, k.two, :]
                    dve.wait_ge(tanhed, k.n * 2 + 2)
                    ch.link(dve.tensor_tensor(mm, tile_of(xn_all, k.n), hh, ALU.subtract))
                    ch.link(dve.scalar_tensor_tensor(mm, tt, 1.0, mm, ALU.add, ALU.mult))
                    ch.link(dve.scalar_tensor_tensor(mm, mm, 0.5, hh, ALU.mult, ALU.add))
                    add_into_x(dve, g, ch, mm, g.tanh_gate[:, 0:1], k.n)
                    assert ch.n == K
            pipeline(dve, NT, 4, 4, step)


SPIKES = 5


def l0_feed_forward(nc, g, io):
    FC = 512 // P
    with ExitStack() as ctx:
        m = Memory(nc, ctx, "f0")
        xn, xT = m.sb("xn", [P, 2, D]), m.sb("xT", [P, 2, T])
        act1, sq = m.sb("act1", [P, 2, FC * T]), m.sb("sq", [P, 2, FC * T])
        y, count, mem, drive = m.sb("y", [P, 2, D]), m.sb("count", [P, D]), m.sb("mem", [P, D]), m.sb("drive", [P, D])
        fifth = m.sb("fifth", [P, 1])
        pT, pH, pY = ([m.ps(f"{k}{i}") for i in range(2)] for k in ("pT", "pH", "pY"))
        ready, normed, turned, copied, hidden, relued, squared, projected, y_copied, spiked = (
            m.sem(k) for k in ("ready", "normed", "turned", "copied", "hidden", "relued", "squared", "projected",
                               "y_copied", "spiked"))
        K = 3 * SPIKES - 2 + ADD_STEPS
        block = ctx.enter_context(nc.Block())

        @block.vector
        def _(dve):
            dve.tensor_scalar(fifth[:, :], g.tanh_gate[:, 4:5], 1.0 / SPIKES, None, ALU.mult).then_inc(ready, 1)
            dve.wait_ge(ready, 1)

            def step(at):
                if k := at(0):
                    dve.wait_ge(turned, cnt(k.n - 1))
                    layer_norm(dve, g, xn[:, k.two, :], k.n).then_inc(normed, 1)
                if k := at(4):
                    ch = Chain(dve, spiked, k.n * K)
                    yy = y[:, k.two, :]
                    dve.wait_ge(y_copied, k.n + 1)
                    before = yy
                    ch.mark(dve.tensor_scalar(count[:, :], yy, 1.0, None, ALU.is_gt))
                    for _ in range(1, SPIKES):
                        ch.link(dve.scalar_tensor_tensor(drive[:, :], before, 1.0, yy, ALU.is_gt, ALU.subtract))
                        ch.link(dve.scalar_tensor_tensor(mem[:, :], before, 0.9, drive[:, :], ALU.mult, ALU.subtract))
                        ch.link(dve.scalar_tensor_tensor(count[:, :], mem[:, :], 1.0, count[:, :], ALU.is_gt, ALU.add))
                        before = mem[:, :]
                    add_into_x(dve, g, ch, count[:, :], fifth[:, 0:1], k.n)
                    assert ch.n == K
            pipeline(dve, NT, 4, 4, step)

        @block.tensor
        def _(pe):
            pe.wait_ge(g.weights_in["L0f"], 16 * len(g.loads["L0f"]))

            def step(at):
                if k := at(1):
                    pe.wait_ge(copied, k.n + 1)
                    pe.wait_ge(relued, cnt(k.n - 1))
                    for c in range(FC):
                        mm = pe.matmul(pH[k.two][:, c * T:(c + 1) * T], g.w_fc[:, c * P:(c + 1) * P], xT[:, k.two, :],
                                       start=True, stop=True)
                    mm.then_inc(hidden, 1)
                if k := at(0):
                    pe.wait_ge(normed, k.n + 1)
                    pe.wait_ge(copied, cnt(k.n - 1))
                    pe.transpose(pT[k.two][:, 0:T], xn[:, k.two, :], g.ident[:, :]).then_inc(turned, 1)
                if k := at(3):
                    pe.wait_ge(squared, k.n + 1)
                    pe.wait_ge(y_copied, cnt(k.n - 1))
                    for c in range(FC):
                        mm = pe.matmul(pY[k.two][:, 0:D], sq[:, k.two, c * T:(c + 1) * T], g.w_proj[:, c, :],
                                       start=(c == 0), stop=(c == FC - 1))
                    mm.then_inc(projected, 1)
            pipeline(pe, NT, 4, 4, step)

        @block.scalar
        def _(act):
            def step(at):
                if k := at(1):
                    act.wait_ge(hidden, k.n + 1)
                    act.wait_ge(squared, cnt(k.n - 1))
                    act.activation(act1[:, k.two, :], pH[k.two][:, 0:FC * T], ACT.Relu).then_inc(relued, 1)
                if k := at(0):
                    act.wait_ge(turned, k.n + 1)
                    act.wait_ge(hidden, cnt(k.n - 1))
                    act.copy(xT[:, k.two, :], pT[k.two][:, 0:T]).then_inc(copied, 1)
                if k := at(3):
                    act.wait_ge(projected, k.n + 1)
                    act.wait_ge(spiked, cnt(k.n - 1) * K)
                    act.copy(y[:, k.two, :], pY[k.two][:, 0:D]).then_inc(y_copied, 1)
            pipeline(act, NT, 4, 4, step)

        @block.gpsimd
        def _(pool):
            def step(at):
                if k := at(2):
                    pool.wait_ge(relued, k.n + 1)
                    pool.wait_ge(projected, cnt(k.n - 1))
                    pool.tensor_tensor(sq[:, k.two, :], act1[:, k.two, :], act1[:, k.two, :], ALU.mult
                                       ).then_inc(squared, 1)
            pipeline(pool, NT, 4, 4, step)


MASK_FILL = -2.3819763e38
HIGH = 3.3e38


class Heads:

    def __init__(self, name, heads, wq, wk, wv, wo, load, gate, rope=None, rms=False, bq=None, bk=None, bv=None,
                 bo=None):
        self.name, self.heads, self.width = name, heads, D // heads
        self.wq, self.wk, self.wv, self.wo = wq, wk, wv, wo
        self.load, self.gate, self.rope, self.rms = load, gate, rope, rms
        self.bq, self.bk, self.bv, self.bo = bq, bk, bv, bo
        per = 512 // S
        self.banks = [(h, min(per, heads - h)) for h in range(0, heads, per)]
        self.chunks = -(-heads * PITCH // P)
        self.groups = [range(c, min(c + 4, self.chunks)) for c in range(0, self.chunks, 4)]
        self.blocks = len(self.groups)


PITCH = 80
PERIOD = 5
FIRST_HEAD = (0, 1, 3, 4, 5)


def attention(nc, g, io, a):
    H, W = a.heads, a.width
    SB = len(a.banks)
    with ExitStack() as ctx:
        m = Memory(nc, ctx, a.name)
        xn, xT = m.sb("xn", [P, 2, D]), m.sb("xT", [P, 2, T])
        qT, kT = m.sb("qT", [P, 2, T]), m.sb("kT", [P, 2, S])
        kS = m.sb("kS", [P, 2, H, S])
        vS = m.sb("vS", [P, 4, a.chunks * D])
        ctxT = m.sb("ctxT", [P, 4, 3, PITCH])
        ex = m.sb("ex", [P, 2, a.chunks * P])
        exT = m.sb("exT", [P, 2, 4 * T])
        nmax, total, over = m.sb("nmax", [P, 2, H]), m.sb("total", [P, 2, H]), m.sb("over", [P, 2, H])
        overx, overT, oT = m.sb("overx", [P, 2, D]), m.sb("overT", [P, 2, T]), m.sb("oT", [P, 2, T])
        pF, pQ, pO = m.ps("pF"), m.ps("pQ"), m.ps("pO")
        pS = m.ps("pS", (P, SB, 512))
        pE = [m.ps(f"pE{i}") for i in range(2)]
        ctx_in = [m.sem(f"ctx_in{i}") for i in range(4)]
        (cleared, wide_bias, bias_product, bias_steps, scaled, normed, turned, x_copied, q_made, q_steps, q_turned,
         q_copied, k_made, k_copied, spread, v_taken, scored, shifted, exped, summed, spread_over, over_turned,
         over_copied, roped, ceiled, v_spread, ex_turned, ex_copied, weighted, divided, projected, added, biased, ctx_normed, ctx_turned,
         ctx_copied) = (m.sem(k) for k in (
             "cleared", "wide_bias", "bias_product", "bias_steps", "scaled", "normed", "turned", "x_copied", "q_made",
             "q_steps", "q_turned", "q_copied", "k_made", "k_copied", "spread", "v_taken", "scored",
             "shifted", "exped", "summed", "spread_over", "over_turned", "over_copied", "roped", "ceiled", "v_spread", "ex_turned", "ex_copied",
             "weighted", "divided", "projected", "added", "biased", "ctx_normed", "ctx_turned", "ctx_copied"))
        if a.rms:
            ctxr, ctxn = m.sb("ctxr", [S, 4, D]), m.sb("ctxn", [S, 2, D])
            ceiling, v_one = m.sb("ceiling", [P, NT * S]), m.sb("v_one", [P, 2, a.chunks * W])
            rq, rk = m.sb("rq", [P, 2, T]), m.sb("rk", [P, 2, S])
        if a.rope == "positions":
            qrow, biased_q, swapped = m.sb("qrow", [P, 2, D]), m.sb("biased_q", [P, 2, D]), m.sb("swapped", [P, D])
        if a.bo is not None:
            bv_wide, out_bias = m.sb("bv_wide", [P, P]), m.sb("out_bias", [P, D])
        SHIFT = 3 if a.rms else 2 * SB
        QSTEPS, QREADY = {None: (1, 1), "tables": (6, 5), "positions": (1, None)}[a.rope]
        ROPE = 4
        CLEARED = 3
        KC = 2 * T
        VC = KC + 2 * S if a.rms else T
        block = ctx.enter_context(nc.Block())

        def ex_heads(two):
            return ex[:, two, 0:H * PITCH].rearrange("p (h x) -> p h x", x=PITCH)[:, :, 0:S]

        def rows_of(slot, c):
            start = c * P % PITCH
            return ctxT[:, slot, :, :].rearrange("p a x -> p (a x)")[:, start:start + P]

        @block.sync
        def _(sp):
            def step(at):
                if k := at(0):
                    if a.rms:
                        sp.wait_ge(ctx_normed, cnt(k.n - 3))
                        sp.dma_start(ctxr[:, k.v, :], tile_rows(io["ctx"], k.n)).then_inc(ctx_in[k.v], 16)
                    else:
                        sp.wait_ge(q_made, cnt(k.n - 3))
                        sp.dma_start(ctxT[:, k.v, :, 0:S], tile_rows(io["ctxT"], k.n).unsqueeze(1).broadcast_to(
                            [P, 3, S])).then_inc(ctx_in[k.v], 16)
            sp.wait_ge(cleared, CLEARED)
            pipeline(sp, NT, 0, 4, step)

        @block.gpsimd
        def _(pool):
            for t in (vS, ex, ctxT):
                pool.memset(t[:], 0.0).then_inc(cleared, 1)
            if a.bo is not None:
                pool.wait_ge(bias_steps, 2)

            def rope(k):
                ch = Chain(pool, roped, k.n * ROPE)
                pool.wait_ge(q_steps, k.n * QSTEPS + QSTEPS)
                pool.wait_ge(q_turned, cnt(k.n - 1))
                pool.wait_ge(roped, k.n * ROPE)
                q0, q2 = (v.rearrange("p (h c f) -> p h c f", c=2, f=W // 2)
                          for v in (biased_q[:, k.two, :], swapped[:, :]))
                cos, sin = tile_of(g.cos_q, k.n), tile_of(g.sin_q, k.n)
                for half in range(2):
                    ch.mark(pool.tensor_tensor(
                        q2[:, :, half, :], q0[:, :, 1 - half, :],
                        wide(sin[:, half * W // 2:(half + 1) * W // 2], H), ALU.mult))
                ch.link(pool.tensor_tensor(qrow[:, k.two, :].rearrange("p (g f) -> p g f", f=W // 2),
                                           biased_q[:, k.two, :].rearrange("p (g f) -> p g f", f=W // 2),
                                           wide(cos, 2 * H), ALU.mult))
                ch.mark(pool.tensor_tensor(qrow[:, k.two, :], qrow[:, k.two, :], swapped[:, :], ALU.add))
                assert ch.n == ROPE

            def step(at):
                if e := at(3):
                    pool.wait_ge(summed, e.n * 2 + 2)
                    pool.wait_ge(over_turned, cnt(e.n - 1))
                    pool.tensor_tensor(overx[:, e.two, :].rearrange("p (h w) -> p h w", h=H),
                                       over[:, e.two, :].unsqueeze(2).broadcast_to([P, H, W]),
                                       g.ones[:, 0:D].rearrange("p (h w) -> p h w", h=H), ALU.mult
                                       ).then_inc(spread_over, 1)
                    if a.bo is not None:
                        pool.wait_ge(normed, e.n + 1)
                        pool.tensor_tensor(tile_of(g.x, e.n), tile_of(g.x, e.n), out_bias[:, :], ALU.add
                                           ).then_inc(biased, 1)
                k = at(0)
                if k and a.rope == "positions":
                    rope(k)
                if k:
                    if a.rms:
                        pool.wait_ge(q_steps, k.n * QSTEPS + QSTEPS)
                    else:
                        pool.wait_ge(k_copied, k.n + 1)
                    pool.wait_ge(scored, cnt(k.n - 1) * SB)
                    pool.tensor_tensor(kS[:, k.two, :, :], wide(kT[:, k.two, :], H), heads_mask(g, a),
                                       ALU.mult).then_inc(spread, 1)
                if k and a.rms:
                    pool.wait_ge(v_taken, k.n + 1)
                    pool.wait_ge(weighted, cnt(k.n - 3) * a.blocks)
                    shape = [P, a.chunks, H, W]
                    pool.tensor_tensor(vS[:, k.v, :].rearrange("p (c h w) -> p c h w", h=H, w=W),
                                       v_one[:, k.two, :].rearrange("p (c w) -> p c w", w=W).unsqueeze(2
                                                                                                   ).broadcast_to(shape),
                                       g.own_head.unsqueeze(3).broadcast_to(shape), ALU.mult).then_inc(v_spread, 1)
            pipeline(pool, NT, 4, 4, step)

        @block.tensor
        def _(pe):
            pe.wait_ge(g.weights_in[a.load], 16 * len(g.loads[a.load]))
            if a.bo is not None:
                pe.wait_ge(wide_bias, 1)
                pe.matmul(pO[:, 0:D], bv_wide[:, :], a.wo, start=True, stop=True).then_inc(bias_product, 1)
                pe.wait_ge(bias_steps, 1)
            if a.rms:
                pe.wait_ge(scaled, 3)

            def turn(k, b):
                pe.wait_ge(ex_copied, cnt(k.n * a.blocks + b - 1))
                r = (k.two * a.blocks + b) % 2
                for j, c in enumerate(a.groups[b]):
                    t = pe.transpose(pE[r][:, j * T:(j + 1) * T], ex[:, k.two, c * P:(c + 1) * P], g.ident[:, :])
                t.then_inc(ex_turned, 1)

            def weigh(k, b):
                pe.wait_ge(ex_copied, k.n * a.blocks + b + 1)
                r = (k.two * a.blocks + b) % 2
                for j, c in enumerate(a.groups[b]):
                    start = c * D - (0 if a.rms else W * (FIRST_HEAD[c % PERIOD] + c // PERIOD * H // 2))
                    t = pe.matmul(pO[:, 0:T], vS[:, k.v, start:start + D], exT[:, r, j * T:(j + 1) * T],
                                  start=(c == 0), stop=(c == a.chunks - 1))
                t.then_inc(weighted, 1)

            def make_v(k):
                for c in range(min(a.chunks, PERIOD)):
                    if a.rms:
                        t = pe.matmul(pQ[:, VC + c * W:VC + (c + 1) * W], rows_of(k.two, c), a.wv, start=True, stop=True)
                    else:
                        wv = a.wv.rearrange("p (g x) -> p g x", g=2)[:, :, W * FIRST_HEAD[c]:W * (FIRST_HEAD[c] + 3)]
                        t = pe.matmul(pQ[:, VC + c * 6 * W:VC + (c + 1) * 6 * W], rows_of(k.v, c), wv, start=True,
                                      stop=True)
                t.then_inc(q_made, 1)

            def q_and_k(k):
                pe.wait_ge(x_copied, k.n + 1)
                pe.wait_ge(v_taken, cnt(k.n))
                if a.rms:
                    pe.matmul(pQ[:, 0:T], a.wq[:, 0:D], xT[:, k.two, :], start=True, stop=True)
                    pe.matmul(pQ[:, T:2 * T], a.wq[:, D:2 * D], xT[:, k.two, :], start=True, stop=True)
                    pe.wait_ge(ctx_normed, k.n + 1)
                    pe.transpose(pF[:, 0:S], ctxn[:, k.two, :], g.ident[0:S, 0:S]).then_inc(ctx_turned, 1)
                    pe.wait_ge(ctx_copied, k.n + 1)
                    c = ctxT[:, k.two, 0, 0:S]
                    pe.matmul(pQ[:, KC:KC + S], a.wk[:, 0:D], c, start=True, stop=True)
                    pe.matmul(pQ[:, KC + S:KC + 2 * S], a.wk[:, D:2 * D], c, start=True, stop=True)
                    make_v(k)
                    return
                pe.wait_ge(ctx_in[k.v], k.round * 16 + 16)
                pe.matmul(pF[:, 0:S], a.wk, ctxT[:, k.v, 0, 0:S], start=True, stop=True).then_inc(k_made, 1)
                if a.rope == "positions":
                    pe.matmul(pQ[:, 0:D], xT[:, k.two, :], a.wq, start=True, stop=True)
                else:
                    pe.matmul(pQ[:, 0:T], a.wq, xT[:, k.two, :], start=True, stop=True)
                make_v(k)

            def step(at):
                k, r, c, e, o = (at(lag) for lag in range(5))
                if c:
                    pe.wait_ge(spread, c.n + 1)
                    if QREADY:
                        pe.wait_ge(q_steps, c.n * QSTEPS + QREADY)
                    else:
                        pe.wait_ge(q_copied, c.n + 1)
                    pe.wait_ge(shifted, c.n * SHIFT)
                    for j, (h, n) in enumerate(a.banks):
                        pe.matmul(pS[:, j, 0:n * S], qT[:, c.two, :],
                                  kS[:, c.two, h:h + n, :].rearrange("p h s -> p (h s)"), start=True, stop=True
                                  ).then_inc(scored, 1)
                if o:
                    pe.wait_ge(divided, o.n + 1)
                    pe.matmul(pO[:, 0:D], oT[:, o.two, :], a.wo, start=True, stop=True).then_inc(projected, 1)
                if k:
                    pe.wait_ge(ctx_copied if a.rms else k_copied, k.n)
                    pe.wait_ge(over_copied, cnt(k.n - 3))
                    if a.rope == "positions":
                        pe.wait_ge(q_copied, cnt(k.n - 1))
                    pe.wait_ge(normed, k.n + 1)
                    pe.transpose(pF[:, 0:T], xn[:, k.two, :], g.ident[:, :]).then_inc(turned, 1)
                if e:
                    pe.wait_ge(exped, e.n + 1)
                    turn(e, 0)
                if k:
                    q_and_k(k)
                if e:
                    if a.blocks > 1:
                        turn(e, 1)
                    pe.wait_ge(spread_over, e.n + 1)
                    if k:
                        pe.wait_ge(ctx_copied if a.rms else k_copied, k.n + 1)
                    else:
                        pe.wait_ge(over_copied, e.n)
                        if a.rope == "positions":
                            pe.wait_ge(q_copied, min(e.n + 2, NT))
                    pe.transpose(pF[:, 0:T], overx[:, e.two, :], g.ident[:, :]).then_inc(over_turned, 1)
                    pe.wait_ge(v_spread if a.rms else v_taken, e.n + 1)
                    pe.wait_ge(added, e.n * ADD_STEPS)
                    for b in range(a.blocks):
                        weigh(e, b)
                        if b + 2 < a.blocks:
                            turn(e, b + 2)
                if r and a.rope == "positions":
                    pe.wait_ge(roped, r.n * ROPE + ROPE)
                    if e:
                        pe.wait_ge(over_copied, e.n + 1)
                    elif k:
                        pe.wait_ge(k_copied, k.n + 1)
                    pe.transpose(pF[:, 0:T], qrow[:, r.two, :], g.ident[:, :]).then_inc(q_turned, 1)
            pipeline(pe, NT, 4, 4, step)

        @block.scalar
        def _(act):
            def copy_heads(e, b):
                act.wait_ge(ex_turned, e.n * a.blocks + b + 1)
                act.wait_ge(weighted, cnt(e.n * a.blocks + b - 1))
                r = (e.two * a.blocks + b) % 2
                n = len(a.groups[b]) * T
                act.copy(exT[:, r, 0:n], pE[r][:, 0:n]).then_inc(ex_copied, 1)

            def step(at):
                k, r, c, e = (at(lag) for lag in range(4))
                if k:
                    act.wait_ge(turned, k.n + 1)
                    act.wait_ge(q_made, cnt(k.n - 1))
                    act.copy(xT[:, k.two, :], pF[:, 0:T]).then_inc(x_copied, 1)
                if e and not a.rms:
                    copy_heads(e, 0)
                if k and a.rms:
                    act.wait_ge(ctx_turned, k.n + 1)
                    act.wait_ge(q_made, cnt(k.n - 1))
                    act.copy(ctxT[:, k.two, :, 0:S], wide(pF[:, 0:S], 3)).then_inc(ctx_copied, 1)
                elif k:
                    act.wait_ge(k_made, k.n + 1)
                    act.wait_ge(spread, cnt(k.n - 1))
                    act.activation(kT[:, k.two, :], pF[:, 0:S], ACT.Identity, bias=a.bk).then_inc(k_copied, 1)
                if e:
                    copy_heads(e, 0 if a.rms else 1)
                    act.wait_ge(over_turned, e.n + 1)
                    act.wait_ge(divided, cnt(e.n - 1))
                    act.copy(overT[:, e.two, :], pF[:, 0:T]).then_inc(over_copied, 1)
                    for b in range(2, a.blocks):
                        copy_heads(e, b)
                if r and a.rope == "positions":
                    act.wait_ge(q_turned, r.n + 1)
                    act.wait_ge(scored, cnt(r.n - 1) * SB)
                    act.copy(qT[:, r.two, :], pF[:, 0:T]).then_inc(q_copied, 1)
                if c:
                    act.wait_ge(shifted, c.n * SHIFT + SHIFT)
                    e1 = ex_heads(c.two)
                    act.activation(e1, e1, ACT.Exp, scale=float(W) ** -0.5).then_inc(exped, 1)
            pipeline(act, NT, 4, 4, step)

        @block.vector
        def _(dve):
            dve.wait_ge(g.weights_in[a.load], 16 * len(g.loads[a.load]))
            dve.wait_ge(g.gates_done, 1)
            dve.wait_ge(cleared, CLEARED)
            gate = g.tanh_gate[:, a.gate:a.gate + 1]
            if a.bo is not None:
                dve.tensor_scalar(bv_wide[:, :], g.ones[:, 0:P], a.bv, None, ALU.mult).then_inc(wide_bias, 1)
                dve.wait_ge(bias_product, 1)
                ch = Chain(dve, bias_steps)
                ch.link(dve.tensor_tensor(out_bias[:, :], pO[:, 0:D], a.bo, ALU.add))
                ch.mark(dve.tensor_scalar(out_bias[:, :], out_bias[:, :], gate, None, ALU.mult))
            if a.rms:
                dve.tensor_scalar(ceiling[:, :], g.mask8, HIGH, MASK_FILL, ALU.mult, ALU.add).then_inc(ceiled, 1)
                dve.wait_ge(ceiled, 1)
                for w in (a.wq, a.wk, a.wv):
                    dve.tensor_scalar(w, w, g.rms_scale[:, 0:1], None, ALU.mult).then_inc(scaled, 1)

            def shift(k, between):
                ch = Chain(dve, shifted, k.n * SHIFT)
                dve.wait_ge(scored, k.n * SB + 1)
                dve.wait_ge(ex_turned, cnt(k.n - 1) * a.blocks)
                if a.rms:
                    e1 = ex_heads(k.two)
                    if between:
                        between()
                    ch.link(dve.tensor_tensor(e1, pS[:, 0, 0:H * S].rearrange("p (h s) -> p h s", h=H),
                                              wide(ceiling[:, span(k.n, S)], H), ALU.min))
                    ch.link(dve.tensor_reduce(nmax[:, k.two, :], e1, AX.X, ALU.max, negate=True))
                    ch.mark(dve.tensor_tensor(e1, e1, nmax[:, k.two, :].unsqueeze(2).broadcast_to([P, H, S]), ALU.add))
                    assert ch.n == SHIFT
                    return
                for j, (h, n) in enumerate(a.banks):
                    dve.wait_ge(scored, k.n * SB + j + 1)
                    ch.mark(dve.tensor_reduce(nmax[:, k.two, h:h + n],
                                              pS[:, j, 0:n * S].rearrange("p (h s) -> p h s", h=n), AX.X, ALU.max,
                                              negate=True))
                if between:
                    between()
                for j, (h, n) in enumerate(a.banks):
                    dve.wait_ge(shifted, k.n * SHIFT + j + 1)
                    ch.mark(dve.tensor_tensor(ex_heads(k.two)[:, h:h + n, :],
                                              pS[:, j, 0:n * S].rearrange("p (h s) -> p h s", h=n),
                                              nmax[:, k.two, h:h + n].unsqueeze(2).broadcast_to([P, n, S]), ALU.add))
                assert ch.n == SHIFT

            def take_q(k):
                ch = Chain(dve, q_steps, k.n * QSTEPS)
                dve.wait_ge(q_made, k.n + 1)
                if a.rope is None:
                    dve.wait_ge(scored, cnt(k.n - 1) * SB)
                    ch.mark(dve.tensor_scalar(qT[:, k.two, :], pQ[:, 0:T], a.bq, None, ALU.add))
                elif a.rope == "tables":
                    dve.wait_ge(scored, cnt(k.n - 1))
                    r1, r2, k1, k2 = rq[:, 0, :], rq[:, 1, :], rk[:, 0, :], rk[:, 1, :]
                    ch.mark(dve.tensor_tensor(r1, pQ[:, 0:T], g.rope_q[:, 0, :], ALU.mult))
                    ch.mark(dve.tensor_tensor(r2, pQ[:, T:2 * T], g.rope_q[:, 1, :], ALU.mult))
                    ch.mark(dve.tensor_tensor(k1, pQ[:, KC:KC + S], g.rope_k[:, 0, :], ALU.mult))
                    ch.link(dve.tensor_tensor(k2, pQ[:, KC + S:KC + 2 * S], g.rope_k[:, 1, :], ALU.mult))
                    ch.mark(dve.tensor_tensor(qT[:, k.two, :], r1, r2, ALU.add))
                    dve.wait_ge(spread, cnt(k.n - 1))
                    ch.mark(dve.tensor_tensor(kT[:, k.two, :], k1, k2, ALU.add))
                else:
                    dve.wait_ge(roped, cnt(k.n - 1) * ROPE)
                    ch.mark(dve.tensor_tensor(biased_q[:, k.two, :], pQ[:, 0:D], a.bq, ALU.add))
                assert ch.n == QSTEPS

            def take_v(k):
                C = a.chunks
                if a.rms:
                    dve.wait_ge(v_spread, cnt(k.n - 1))
                    dve.tensor_scalar(v_one[:, k.two, :], pQ[:, VC:VC + C * W], 1.0, None, ALU.mult).then_inc(v_taken, 1)
                else:
                    dve.wait_ge(weighted, cnt(k.n - 3) * a.blocks)
                    v = pQ[:, VC:VC + C * 3 * W].rearrange("p (c g w) -> p g c w", g=2, w=3 * W)
                    to = vS[:, k.v, :].rearrange("p (g c x) -> p g c x", g=2, x=D)[:, :, :, 0:3 * W]
                    own = g.own_head_of3.unsqueeze(1).broadcast_to([P, 2, PERIOD, 3 * W])
                    dve.tensor_tensor(to, v, own, ALU.mult).then_inc(v_taken, 1)

            def step(at):
                k, c, e, o = at(0), at(2), at(3), at(4)

                def add_in():
                    dve.wait_ge(projected, o.n + 1)
                    if a.bo is not None:
                        dve.wait_ge(biased, o.n + 1)
                    add_into_x(dve, g, Chain(dve, added, o.n * ADD_STEPS), pO[:, 0:D], gate, o.n)

                if k:
                    dve.wait_ge(turned, cnt(k.n - 1))
                    layer_norm(dve, g, xn[:, k.two, :], k.n).then_inc(normed, 1)
                    if a.rms:
                        dve.wait_ge(ctx_in[k.v], k.round * 16 + 16)
                        dve.wait_ge(ctx_turned, cnt(k.n - 1))
                        dve.tensor_scalar(ctxn[:, k.two, :], ctxr[:, k.v, :], g.ctx_rstd[:, bass.ds(k.n, 1)], None,
                                          ALU.mult).then_inc(ctx_normed, 1)
                if e:
                    dve.wait_ge(exped, e.n + 1)
                    dve.wait_ge(spread_over, cnt(e.n - 1))
                    dve.tensor_reduce(total[:, e.two, :], ex_heads(e.two), AX.X, ALU.add).then_inc(summed, 1)
                    dve.wait_ge(summed, e.n * 2 + 1)
                    dve.reciprocal(over[:, e.two, :], total[:, e.two, :]).then_inc(summed, 1)
                if c:
                    shift(c, add_in if o else None)
                elif o:
                    add_in()
                if k:
                    take_q(k)
                    take_v(k)
                if e:
                    dve.wait_ge(weighted, e.n * a.blocks + a.blocks)
                    dve.wait_ge(over_copied, e.n + 1)
                    dve.wait_ge(projected, cnt(e.n - 1))
                    dve.tensor_tensor(oT[:, e.two, :], pO[:, 0:T], overT[:, e.two, :], ALU.mult).then_inc(divided, 1)
            pipeline(dve, NT, 4, 4, step)


def wide(ap, heads):
    return ap.unsqueeze(1).broadcast_to([ap.shape[0], heads, ap.shape[1]])


def heads_mask(g, a):
    return g.head_mask[a.heads].unsqueeze(2).broadcast_to([P, a.heads, S])


def tile_rows(ap, n):
    return ap[bass.ds(n, 1), :, :].rearrange("a p s -> p (a s)")


def ctx_rms(nc, g):
    with ExitStack() as ctx:
        m = Memory(nc, ctx, "cr")
        a, b = m.sb("a", [S, NT]), m.sb("b", [S, NT])
        shifted, rooted = m.sem("shifted"), m.sem("rooted")
        block = ctx.enter_context(nc.Block())

        @block.vector
        def _(dve):
            dve.wait_ge(g.weights_in["L2a"], 16 * len(g.loads["L2a"]))
            ch = Chain(dve, shifted)
            ch.mark(dve.tensor_scalar(a[:, :], g.ctx_sum2[:, :], 1.0 / D, 1e-6, ALU.mult, ALU.add))
            ch.mark(dve.tensor_scalar(g.rms_scale[:, :], g.rms_scale[:, :], 1.0, None, ALU.add))
            dve.wait_ge(rooted, 1)
            ch.mark(dve.reciprocal(g.ctx_rstd[:, :], b[:, :]))

        @block.scalar
        def _(act):
            act.wait_ge(shifted, 1)
            act.activation(b[:, :], a[:, :], ACT.Sqrt).then_inc(rooted, 1)


ROPE_BASE = 10000.0
TWO_PI = (6.28125, 0.0019350051879882812, 3.0199159819e-07)
NEAREST = 12582912.0
HALF_PI = 1.5707963267948966


def rope_angles(nc, g):
    F = 4
    with ExitStack() as ctx:
        m = Memory(nc, ctx, "ra")
        pos = m.sb("posf", [P, NT])
        ang, turns, low = m.sb("ang", [P, NT, F]), m.sb("turns", [P, NT, F]), m.sb("low", [P, NT, F])
        steps, waved = m.sem("steps"), m.sem("waved")
        READY = 11
        block = ctx.enter_context(nc.Block())

        @block.vector
        def _(dve):
            dve.wait_ge(g.weights_in["L3a"], 16 * len(g.loads["L3a"]))
            ch = Chain(dve, steps)
            ch.link(dve.tensor_scalar(pos[:, :], g.pos[:, :], 1.0, None, ALU.mult))
            for f in range(F):
                inverse = float(np.float32(1.0) / np.float32(ROPE_BASE) ** np.float32(2 * f / (2 * F)))
                last = dve.tensor_scalar(ang[:, :, f], pos[:, :], inverse, None, ALU.mult)
                (ch.mark if f < F - 1 else ch.link)(last)
            ch.link(dve.tensor_scalar(turns[:, :, :], ang[:, :, :], 1.0 / (2 * np.pi), NEAREST, ALU.mult, ALU.add))
            ch.link(dve.tensor_scalar(turns[:, :, :], turns[:, :, :], -NEAREST, None, ALU.add))
            for part in TWO_PI:
                ch.link(dve.scalar_tensor_tensor(ang[:, :, :], turns[:, :, :], -part, ang[:, :, :], ALU.mult, ALU.add))
            ch.link(dve.tensor_scalar(ang[:, :, :], ang[:, :, :], 3.1415925, -3.1415925, ALU.min, ALU.max))
            ch.link(dve.scalar_tensor_tensor(low[:, :, :], ang[:, :, :], -1.0, ang[:, :, :], ALU.mult, ALU.min))
            ch.mark(dve.tensor_scalar(low[:, :, :], low[:, :, :], HALF_PI, None, ALU.add))
            assert ch.n == READY + 2
            dve.wait_ge(waved, 2)
            ch.mark(dve.tensor_scalar(g.sin_q[:, :, 0:F], g.sin_q[:, :, F:2 * F], -1.0, None, ALU.mult))

        @block.scalar
        def _(act):
            act.wait_ge(steps, READY + 2)
            act.activation(g.sin_q[:, :, F:2 * F], ang[:, :, :], ACT.Sin).then_inc(waved, 1)
            act.activation(g.cos_q[:, :, :], low[:, :, :], ACT.Sin).then_inc(waved, 1)


class Mixture:

    def __init__(self, name, kind, choices, tiles, row, hidden, load, gate, wg, bg, w_up, w_down, b_up=None,
                 b_down=None):
        self.name, self.kind, self.choices, self.tiles, self.row = name, kind, choices, tiles, row
        self.hidden, self.load, self.gate = hidden, load, gate
        self.wg, self.bg, self.w_up, self.w_down, self.b_up, self.b_down = wg, bg, w_up, w_down, b_up, b_down


CHOICES = 2
TOP2_TILES = -(-(CHOICES * NT + E - 1) // 4) * 4
CAPACITY = B * T // E
CHOSEN_TILES = B * T // P
NOWHERE = 60000.0


def moe_front(nc, g, mix, rows, logits):
    with ExitStack() as ctx:
        m = Memory(nc, ctx, mix.name + "f")
        xn = m.sb("xn", [P, 4, D])
        xT = m.sb("xT", [P, 2, T])
        pT, pG = ([m.ps(f"{k}{i}") for i in range(2)] for k in ("pT", "pG"))
        stored = [m.sem(f"stored{i}") for i in range(4)]
        normed, turned, copied, scored, biased = (m.sem(k) for k in ("normed", "turned", "copied", "scored", "biased"))
        block = ctx.enter_context(nc.Block())

        @block.vector
        def _(dve):
            for name in ("moe", mix.load):
                dve.wait_ge(g.weights_in[name], 16 * len(g.loads[name]))
            if mix.kind != "experts_choose":
                dve.tensor_scalar(g.before[:, :], g.before_f[:, :], 1.0, None, ALU.mult)

            def step(at):
                if k := at(0):
                    dve.wait_ge(stored[k.v], k.round * 16)
                    dve.wait_ge(turned, cnt(k.n - 3))
                    layer_norm(dve, g, xn[:, k.v, :], k.n).then_inc(normed, 1)
                if k := at(2):
                    dve.wait_ge(scored, k.n + 1)
                    dve.tensor_tensor(tile_of(logits, k.n), pG[k.two][:, 0:E], mix.bg, ALU.add).then_inc(biased, 1)
            pipeline(dve, NT, 3, 4, step)

        @block.tensor
        def _(pe):
            for name in ("moe", mix.load):
                pe.wait_ge(g.weights_in[name], 16 * len(g.loads[name]))

            def step(at):
                if k := at(1):
                    pe.wait_ge(copied, k.n + 1)
                    pe.wait_ge(biased, cnt(k.n - 1))
                    pe.matmul(pG[k.two][:, 0:E], xT[:, k.two, :], mix.wg, start=True, stop=True).then_inc(scored, 1)
                if k := at(0):
                    pe.wait_ge(normed, k.n + 1)
                    pe.wait_ge(copied, cnt(k.n - 1))
                    pe.transpose(pT[k.two][:, 0:T], xn[:, k.v, :], g.ident[:, :]).then_inc(turned, 1)
            pipeline(pe, NT, 3, 4, step)

        @block.scalar
        def _(act):
            def step(at):
                if k := at(0):
                    act.wait_ge(turned, k.n + 1)
                    act.wait_ge(scored, cnt(k.n - 1))
                    act.copy(xT[:, k.two, :], pT[k.two][:, 0:T]).then_inc(copied, 1)
            pipeline(act, NT, 3, 4, step)

        @block.sync
        def _(sp):
            def step(at):
                if k := at(0):
                    sp.wait_ge(normed, k.n + 1)
                    sp.dma_start(rows[bass.ds(k.n * P, P), 0:D], xn[:, k.v, :]).then_inc(stored[k.v], 16)
            pipeline(sp, NT, 3, 4, step)
            for i in range(4):
                sp.wait_ge(stored[i], 16 * NT // 4)


def each_expert(ap):
    return ap.unsqueeze(2).broadcast_to([P, NT, E])


def each_tile(ap):
    return ap.unsqueeze(1).broadcast_to([P, NT, E])


def route_top2(nc, g, mix, logits, slots, weight, tile_expert, parity):
    with ExitStack() as ctx:
        m = Memory(nc, ctx, mix.name + "r")
        sc, t1, t2 = m.sb("sc", [P, NT, E]), m.sb("t1", [P, NT, E]), m.sb("t2", [P, NT, E])
        one = [m.sb(f"one{c}", [P, NT, E]) for c in range(CHOICES)]
        value = [m.sb(f"value{c}", [P, NT]) for c in range(CHOICES)]
        row = m.sb("row", [P, NT])
        chosen = m.sb("chosen", [P, NT, E], BF16)
        inc = m.sb("inc", [P, NT, E])
        tiles_i, tiles_f, base = m.sb("tiles_i", [P, E], I32), m.sb("tiles_f", [P, E]), m.sb("base", [P, E])
        past = m.sb("past", [P, mix.tiles, E - 1])
        expert_f, expert_i = m.sb("expert_f", [P, mix.tiles]), m.sb("expert_i", [P, mix.tiles], I32)
        pP, pT = m.ps("pP"), m.ps("pT")
        steps, exped, prefixed = m.sem("steps"), m.sem("exped"), m.sem("prefixed")
        marks = {}
        block = ctx.enter_context(nc.Block())

        @block.vector
        def _(dve):
            ch = Chain(dve, steps)

            def note(name):
                marks[name] = ch.n

            if mix.kind == "softmax_first":
                ch.link(dve.tensor_reduce(row[:, :], logits[:, :, :], AX.X, ALU.max, negate=True))
                ch.link(dve.tensor_tensor(sc[:, :, :], logits[:, :, :], each_expert(row[:, :]), ALU.add))
                note("shifted")
                dve.wait_ge(exped, 1)
                ch.link(dve.tensor_reduce(row[:, :], sc[:, :, :], AX.X, ALU.add))
                ch.link(dve.reciprocal(row[:, :], row[:, :]))
                ch.link(dve.tensor_tensor(sc[:, :, :], sc[:, :, :], each_expert(row[:, :]), ALU.mult))
            else:
                ch.link(dve.tensor_scalar(sc[:, :, :], logits[:, :, :], 1.0, None, ALU.mult))
            for c in range(CHOICES):
                ch.link(dve.tensor_reduce(value[c][:, :], sc[:, :, :], AX.X, ALU.max))
                ch.link(dve.tensor_tensor(t1[:, :, :], sc[:, :, :], each_expert(value[c][:, :]), ALU.is_equal))
                ch.link(dve.tensor_tensor(t1[:, :, :], t1[:, :, :], each_tile(g.down[:, :]), ALU.mult))
                ch.link(dve.tensor_reduce(row[:, :], t1[:, :, :], AX.X, ALU.max))
                ch.link(dve.tensor_tensor(one[c][:, :, :], t1[:, :, :], each_expert(row[:, :]), ALU.is_equal))
                if c < CHOICES - 1:
                    ch.link(dve.scalar_tensor_tensor(sc[:, :, :], one[c][:, :, :], -3.0e38, sc[:, :, :], ALU.mult,
                                                     ALU.add))
            ch.link(dve.tensor_tensor(chosen[:, :, :], one[0][:, :, :], one[1][:, :, :], ALU.add))
            note("chosen")
            if mix.kind == "softmax_first":
                for c in range(CHOICES):
                    ch.mark(dve.tensor_scalar(weight[:, c, :], value[c][:, :], g.tanh_gate[:, mix.gate:mix.gate + 1],
                                              None, ALU.mult))
            else:
                ch.link(dve.tensor_tensor(value[1][:, :], value[1][:, :], value[0][:, :], ALU.subtract))
                note("shifted")
                dve.wait_ge(exped, 1)
                ch.link(dve.tensor_scalar(row[:, :], value[1][:, :], 1.0, None, ALU.add))
                ch.link(dve.reciprocal(row[:, :], row[:, :]))
                ch.link(dve.tensor_scalar(weight[:, 0, :], row[:, :], g.tanh_gate[:, mix.gate:mix.gate + 1], None,
                                          ALU.mult))
                ch.link(dve.tensor_tensor(weight[:, 1, :], weight[:, 0, :], value[1][:, :], ALU.mult))
            dve.wait_ge(prefixed, 1)
            ch.link(dve.tensor_scalar(t2[:, :, :], pT[:, 0:NT * E].rearrange("p (n e) -> p n e", e=E), 1.0, None,
                                      ALU.mult))
            for e in range(E):
                scan = dve.tensor_tensor_scan(inc[:, :, e], g.ones[:, 0:NT], t2[:, :, e], 0.0, ALU.mult, ALU.add)
                (ch.mark if e < E - 1 else ch.link)(scan)
            ch.link(dve.tensor_scalar(tiles_i[:, :], inc[:, NT - 1, :], float(P - 1), None, ALU.add))
            ch.link(dve.tensor_scalar(tiles_i[:, :], tiles_i[:, :], 7, None, ALU.logical_shift_right))
            ch.link(dve.tensor_scalar(tiles_f[:, :], tiles_i[:, :], 1.0, None, ALU.mult))
            ch.link(dve.tensor_tensor_scan(base[:, :], g.ones[:, 0:E], tiles_f[:, :], 0.0, ALU.mult, ALU.add))
            ch.link(dve.tensor_tensor(past[:, :, :], g.up[:, 0:mix.tiles].unsqueeze(2).broadcast_to([P, mix.tiles, E - 1]),
                                      base[:, 0:E - 1].unsqueeze(1).broadcast_to([P, mix.tiles, E - 1]), ALU.is_ge))
            ch.link(dve.tensor_tensor(base[:, :], base[:, :], tiles_f[:, :], ALU.subtract))
            ch.link(dve.tensor_reduce(expert_f[:, :], past[:, :, :], AX.X, ALU.add))
            ch.mark(dve.tensor_scalar(tile_expert[:, :], expert_f[:, :], 1.0, None, ALU.mult))
            ch.link(dve.tensor_scalar(expert_i[:, :], expert_f[:, :], 1.0, None, ALU.mult))
            ch.link(dve.tensor_scalar(expert_i[:, :], expert_i[:, :], 1, None, ALU.bitwise_and))
            ch.link(dve.tensor_scalar(parity[:, 1, :], expert_i[:, :], 0.5, None, ALU.mult))
            ch.mark(dve.tensor_scalar(parity[:, 0, :], parity[:, 1, :], -2.0, 1.0, ALU.mult, ALU.add))
            ch.link(dve.tensor_scalar(base[:, :], base[:, :], float(P), None, ALU.mult))
            ch.link(dve.tensor_tensor(inc[:, :, :], inc[:, :, :], t2[:, :, :], ALU.subtract))
            ch.link(dve.tensor_tensor(inc[:, :, :], inc[:, :, :], each_tile(base[:, :]), ALU.add))
            ch.link(dve.tensor_tensor(inc[:, :, :], inc[:, :, :], pP[:, 0:NT * E].rearrange("p (n e) -> p n e", e=E),
                                      ALU.add))
            for c in range(CHOICES):
                ch.link(dve.tensor_tensor(t1[:, :, :], inc[:, :, :], one[c][:, :, :], ALU.mult))
                ch.link(dve.tensor_reduce(slots[:, :, c], t1[:, :, :], AX.X, ALU.add))

        @block.scalar
        def _(act):
            act.wait_ge(steps, marks["shifted"])
            v = sc[:, :, :] if mix.kind == "softmax_first" else value[1][:, :]
            act.activation(v, v, ACT.Exp).then_inc(exped, 1)

        @block.tensor
        def _(pe):
            pe.wait_ge(steps, marks["chosen"])
            flat = chosen[:, :, :].rearrange("p n e -> p (n e)")
            pe.matmul(pP[:, 0:NT * E], g.before[:, :], flat, start=True, stop=True)
            pe.matmul(pT[:, 0:NT * E], g.ones16[:, :], flat, start=True, stop=True).then_inc(prefixed, 1)


def build_index(nc, g, mix, slots, index):
    C, N = mix.choices, mix.tiles
    own = mix.kind == "experts_choose"
    reach = N // E if own else N
    with ExitStack() as ctx:
        m = Memory(nc, ctx, mix.name + "i")
        whole, low = m.sb("whole", [P, NT, C], I32), m.sb("low", [P, NT, C], I32)
        col, tile = m.sb("col", [P, NT, C]), m.sb("tile", [P, NT, C])
        columns, tiles, value = m.sb("columns", [P, 2, C, P], F16), m.sb("tiles", [P, 2, C, reach], F16), \
            m.sb("value", [P, 2, C, reach], F16)
        zero = m.sb("zero", [P, P], F16)
        pI = m.ps("pI")
        steps, made, placed, cleared = (m.sem(k) for k in ("steps", "made", "placed", "cleared"))
        K = 3
        block = ctx.enter_context(nc.Block())
        up = g.up16[:, 0:N].rearrange("p (c t) -> p c t", c=C) if own else \
            g.up16[:, 0:N].unsqueeze(1).broadcast_to([P, C, N])

        @block.gpsimd
        def _(pool):
            pool.memset(zero[:, :], 0.0).then_inc(cleared, 1)

        @block.vector
        def _(dve):
            ch = Chain(dve, steps)
            ch.link(dve.tensor_scalar(whole[:, :, :], slots[:, :, 0:C], 1.0, None, ALU.mult))
            ch.mark(dve.tensor_scalar(low[:, :, :], whole[:, :, :], P - 1, None, ALU.bitwise_and))
            ch.link(dve.tensor_scalar(whole[:, :, :], whole[:, :, :], 7, None, ALU.logical_shift_right))
            ch.mark(dve.tensor_scalar(col[:, :, :], low[:, :, :], 1.0, None, ALU.mult))
            ch.link(dve.tensor_scalar(tile[:, :, :], whole[:, :, :], 1.0, None, ALU.mult))

            def step(at):
                k = at(0)
                ch = Chain(dve, made, k.n * K)
                dve.wait_ge(placed, cnt(k.n - 1))
                dve.tensor_scalar(g.carrier[:, 0:1], g.carrier[:, 1:2], 0.0, None, ALU.mult)
                c1, t1 = tile_of(col, k.n), tile_of(tile, k.n)
                ch.mark(dve.tensor_tensor(columns[:, k.two, :, :], g.up16[:, 0:P].unsqueeze(1).broadcast_to([P, C, P]),
                                          c1.unsqueeze(2).broadcast_to([P, C, P]), ALU.is_equal))
                ch.link(dve.tensor_tensor(tiles[:, k.two, :, :], up,
                                          t1.unsqueeze(2).broadcast_to([P, C, reach]), ALU.is_equal))
                ch.mark(dve.tensor_scalar(value[:, k.two, :, :], tiles[:, k.two, :, :], g.token[:, bass.ds(k.n, 1)],
                                          None, ALU.mult))
            pipeline(dve, NT, 0, 4, step)
            dve.wait_ge(placed, NT)
            ch.link(dve.tensor_scalar(index[:, 0:N], pI[:, 0:N], float(B * T // 2), None, ALU.add))

        @block.tensor
        def _(pe):
            pe.wait_ge(cleared, 1)
            pe.matmul(pI[:, 0:N], zero[:, :], zero[:, 0:N], start=True, stop=True)

            def step(at):
                k = at(0)
                pe.wait_ge(made, k.n * K + K)
                for c in range(C):
                    to = slice(c * reach, (c + 1) * reach) if own else slice(0, N)
                    mm = pe.matmul(pI[:, to], columns[:, k.two, c, :], value[:, k.two, c, :], start=False, stop=True,
                                   skip_group_check=True)
                mm.then_inc(placed, 1)
            pipeline(pe, NT, 0, 4, step)


def choose_tokens(nc, g, mix, logits, slots, weight, rows):
    H2, R2 = 2, NT // 2
    with ExitStack() as ctx:
        m = Memory(nc, ctx, mix.name + "c")
        bits, flt = m.sb("bits", [P, H2, P], I32), m.sb("flt", [P, H2, P])
        part = [m.sb(f"part{i}", [P, H2, P], I32) for i in range(2)]
        sign, high, low = m.sb("sign", [P, H2, P]), m.sb("high", [P, H2, P]), m.sb("low", [P, H2, P])
        key, junk = m.sb("key", [P, H2, P]), m.sb("junk", [P, H2, P])
        above, equal, run = m.sb("above", [P, H2, P]), m.sb("equal", [P, H2, P]), m.sb("run", [P, H2, P])
        cand, half, gain, count = (m.sb(k, [P, 1]) for k in ("cand", "half", "gain", "count"))
        need, offset = m.sb("need", [P, 1]), m.sb("offset", [P, H2])
        sel, shift = m.sb("sel", [P, NT, E]), m.sb("shift", [P, NT, E])
        best, best8, diag = m.sb("best", [P, E]), m.sb("best8", [E, 1]), m.sb("diag", [E, E])
        sums, share = m.sb("sums", [P, E]), m.sb("share", [P, E])
        pL, pC, pM, pW = (m.ps(k) for k in ("pL", "pC", "pM", "pW"))
        steps, counted, exped, stored = (m.sem(k) for k in ("steps", "counted", "exped", "stored"))
        LOOP = 4
        marks, products = {}, {}
        block = ctx.enter_context(nc.Block())
        flat = lambda t: t[:, :, :].rearrange("p h t -> p (h t)")
        by_expert = lambda t: t[:, :, :].rearrange("p n e -> p e n")

        @block.vector
        def _(dve):
            dve.wait_ge(g.weights_in["L3c"], 16 * len(g.loads["L3c"]))
            ch = Chain(dve, steps)
            seen = [0]

            def product(name, instruction=None):
                marks[name] = ch.n
                seen[0] += 1
                products[name] = seen[0]
                dve.wait_ge(counted, seen[0])

            ch.link(dve.tensor_reduce(best[:, :], by_expert(logits), AX.X, ALU.max))
            product("turned")
            ch.mark(dve.tensor_reduce(best8[:, :], pM[0:E, 0:P], AX.X, ALU.max))
            dve.wait_ge(steps, ch.n)
            ch.link(dve.tensor_scalar(diag[:, :], g.ident[0:E, 0:E], best8[:, :], None, ALU.mult))
            product("best")
            ch.link(dve.tensor_tensor(shift[:, :, :], logits[:, :, :], each_tile(pM[:, 0:E]), ALU.subtract))
            marks["shifted"] = ch.n
            ch.link(dve.tensor_scalar(flat(flt), pL[:, 0:H2 * P], 1.0, None, ALU.mult))
            ch.link(dve.tensor_scalar(flat(bits), flat(flt).bitcast(I32), 0x7fffffff, None, ALU.bitwise_and))
            ch.mark(dve.tensor_scalar(flat(part[0]), flat(bits), 16, None, ALU.logical_shift_right))
            ch.mark(dve.tensor_scalar(flat(part[1]), flat(bits), 0xffff, None, ALU.bitwise_and))
            ch.link(dve.tensor_scalar(flat(sign), flat(flt), 0.0, -2.0, ALU.is_lt, ALU.mult))
            ch.link(dve.tensor_scalar(flat(sign), flat(sign), 1.0, None, ALU.add))
            ch.mark(dve.tensor_tensor(flat(high), flat(part[0]), flat(sign), ALU.mult))
            ch.link(dve.tensor_tensor(flat(low), flat(part[1]), flat(sign), ALU.mult))

            def bisect(source, bits_of, name):
                ch.mark(dve.memset(cand[:, :], 0.0))
                ch.link(dve.memset(half[:, :], float(2 ** bits_of)))
                marks[name], n0, first = ch.n, ch.n, seen[0]
                with dve.Fori(0, bits_of + 1) as i:
                    def at_step(s):
                        dve.wait_ge(steps, i * LOOP + (n0 + s))
                    dve.tensor_scalar(flat(junk), source, cand[:, :], None, ALU.is_ge, ALU.add,
                                      accum_out=count[:, :]).then_inc(steps, 1)
                    dve.wait_ge(counted, i + (first + 1))
                    dve.tensor_scalar(gain[:, :], pC[:, 0:1], CAPACITY - 0.5, half[:, :], ALU.is_ge, ALU.mult
                                      ).then_inc(steps, 1)
                    at_step(2)
                    dve.tensor_scalar(half[:, :], half[:, :], 0.5, None, ALU.mult).then_inc(steps, 1)
                    at_step(3)
                    dve.scalar_tensor_tensor(cand[:, :], gain[:, :], half[:, :], cand[:, :], ALU.subtract, ALU.add
                                             ).then_inc(steps, 1)
                    at_step(4)
                ch.n += (bits_of + 1) * LOOP
                seen[0] += bits_of + 1
                ch.link(dve.tensor_scalar(cand[:, :], cand[:, :], -0.5, None, ALU.add))

            bisect(flat(high), 15, "high")
            ch.link(dve.tensor_scalar(flat(key), flat(high), cand[:, :], float(2 ** 17), ALU.subtract, ALU.mult))
            ch.link(dve.tensor_tensor(flat(key), flat(key), flat(low), ALU.add))
            bisect(flat(key), 16, "both")
            ch.mark(dve.tensor_scalar(flat(above), flat(key), cand[:, :], None, ALU.is_gt, ALU.add,
                                      accum_out=count[:, :]))
            ch.link(dve.tensor_scalar(flat(equal), flat(key), cand[:, :], None, ALU.is_equal))
            product("above")
            ch.link(dve.tensor_scalar(need[:, :], pC[:, 0:1], -1.0, float(CAPACITY), ALU.mult, ALU.add))

            def rank(source, name):
                for h in range(H2):
                    (ch.mark if h < H2 - 1 else ch.link)(dve.tensor_tensor_scan(
                        run[:, h, :], g.ones[:, 0:P], source[:, h, :], 0.0, ALU.mult, ALU.add))
                product(name)
                ch.link(dve.tensor_scalar(offset[:, :], pC[:, 0:H2], 1.0, None, ALU.mult))
                ch.link(dve.tensor_tensor(run[:, :, :], run[:, :, :], source[:, :, :], ALU.subtract))
                for h in range(H2):
                    (ch.mark if h < H2 - 1 else ch.link)(dve.tensor_scalar(
                        run[:, h, :], run[:, h, :], offset[:, h:h + 1], None, ALU.add))

            rank(equal, "ties")
            ch.link(dve.scalar_tensor_tensor(flat(equal), flat(run), need[:, :], flat(equal), ALU.is_lt, ALU.mult))
            ch.link(dve.tensor_tensor(flat(above), flat(above), flat(equal), ALU.add))
            rank(above, "ranks")
            ch.link(dve.tensor_scalar(flat(run), flat(run), g.row_base[:, 0:1], -NOWHERE, ALU.add, ALU.add))
            ch.link(dve.tensor_tensor(flat(run), flat(run), flat(above), ALU.mult))
            ch.link(dve.tensor_scalar(flat(run), flat(run), NOWHERE, None, ALU.add))
            product("slots")
            ch.link(dve.tensor_scalar(slots[:, :, :].rearrange("p n e -> p (n e)"), pL[:, 0:NT * E], 1.0, None,
                                      ALU.mult))
            ch.link(dve.tensor_scalar(sel[:, :, :], slots[:, :, :], NOWHERE, None, ALU.is_lt))
            dve.wait_ge(exped, 1)
            ch.link(dve.tensor_tensor(shift[:, :, :], shift[:, :, :], sel[:, :, :], ALU.mult))
            ch.link(dve.tensor_reduce(sums[:, :], by_expert(shift), AX.X, ALU.add))
            product("sums")
            ch.link(dve.reciprocal(share[:, :], pW[:, 0:E]))
            ch.link(dve.tensor_scalar(share[:, :], share[:, :], g.tanh_gate[:, mix.gate:mix.gate + 1], None, ALU.mult))
            ch.mark(dve.tensor_tensor(weight[:, :, :], shift[:, :, :], each_tile(share[:, :]), ALU.mult))
            marks["weights"] = ch.n

        @block.scalar
        def _(act):
            act.wait_ge(steps, marks["shifted"])
            act.activation(shift[:, :, :], shift[:, :, :], ACT.Exp).then_inc(exped, 1)

        @block.tensor
        def _(pe):
            pe.wait_ge(g.weights_in["L3c"], 16 * len(g.loads["L3c"]))
            count_done = [0]

            def after(name):
                count_done[0] += 1
                assert products[name] == count_done[0]
                pe.wait_ge(steps, marks[name])

            after("turned")
            for h in range(H2):
                pe.transpose(pL[:, h * P:(h + 1) * P], logits[:, h * R2:(h + 1) * R2, :].rearrange("p n e -> p (n e)"),
                             g.ident[:, :])
            pe.transpose(pM[0:E, 0:P], best[:, :], g.ident[:, :]).then_inc(counted, 1)
            after("best")
            pe.matmul(pM[:, 0:E], g.ones[0:E, :], diag[:, :], start=True, stop=True).then_inc(counted, 1)
            for name, halvings in (("high", 16), ("both", 17)):
                with pe.Fori(0, halvings) as i:
                    pe.wait_ge(steps, i * LOOP + (marks[name] + 1))
                    pe.matmul(pC[:, 0:1], g.same_expert, count[:, :], start=True, stop=True).then_inc(counted, 1)
                count_done[0] += halvings
            after("above")
            pe.matmul(pC[:, 0:1], g.same_expert, count[:, :], start=True, stop=True).then_inc(counted, 1)
            for name in ("ties", "ranks"):
                after(name)
                last = [run[:, h, P - 1:P] for h in range(H2)]
                pe.matmul(pC[:, 0:1], g.earlier_row, last[0], start=True, stop=True)
                pe.matmul(pC[:, 1:2], g.same_expert, last[0], start=True, stop=False)
                pe.matmul(pC[:, 1:2], g.earlier_row, last[1], start=False, stop=True).then_inc(counted, 1)
            after("slots")
            for h in range(H2):
                t = pe.transpose(pL[:, h * P:(h + 1) * P], run[:, h, :], g.ident[:, :])
            t.then_inc(counted, 1)
            after("sums")
            pe.matmul(pW[:, 0:E], g.ones[:, :], sums[:, :], start=True, stop=True).then_inc(counted, 1)

        @block.sync
        def _(sp):
            sp.wait_ge(steps, marks["weights"])
            sp.dma_start(rows[:, D:D + E].rearrange("(n p) e -> p n e", p=P), weight[:, :, :]).then_inc(stored, 16)
            sp.wait_ge(stored, 16)


def run_experts(nc, g, mix, rows, index, tile_expert, parity, results):
    N, R, FH = mix.tiles, mix.row, mix.hidden
    HC = FH // P
    gelu, chosen = mix.kind == "logits_first", mix.kind == "experts_choose"
    with ExitStack() as ctx:
        m = Memory(nc, ctx, mix.name + "e")
        where = m.sb("where", [P, 4], U32)
        xg, xT = m.sb("xg", [P, 4, R]), m.sb("xT", [P, 2, P])
        first, gated = m.sb("first", [P, 2, FH]), m.sb("gated", [P, 2, FH])
        hT, y = m.sb("hT", [P, 2, FH]), m.sb("y", [P, 4, D])
        scratch = m.sb("scratch", [1, 4], I32)
        carried = [m.sem(f"carried{i}") for i in range(2)]
        pX, pU, pH, pY = ([m.ps(f"{k}{i}") for i in range(2)] for k in ("pX", "pU", "pH", "pY"))
        xg_in, y_out = ([m.sem(f"{k}{i}") for i in range(4)] for k in ("xg_in", "y_out"))
        (cleared, placed, turned, x_copied, upped, biased, acted, gates, h_turned, h_copied, downed, y_made, halved,
         x_stored) = (
            m.sem(k) for k in ("cleared", "placed", "turned", "x_copied", "upped", "biased", "acted", "gates",
                               "h_turned", "h_copied", "downed", "y_made", "halved", "x_stored"))
        if gelu:
            hid, tanh_h, halves = m.sb("hid", [P, 2, FH]), m.sb("tanh_h", [P, 2, FH]), m.sb("halves", [P, 2, FH])
        if chosen:
            to, share, noted = m.sb("to", [P, 4], U32), m.sb("share", [P, 4]), m.sem("noted")
        ACTS, GATE, YS = (2, 2, 1) if gelu else (1, 1, 2) if chosen else (1, 1, 1)
        read_up = biased if gelu else gates
        block = ctx.enter_context(nc.Block())

        def expert(eng, k):
            if chosen:
                return k.round
            return eng.value_load(tile_expert[0:1, bass.ds(k.n, 1)], min_val=0, max_val=E - 1)

        @block.gpsimd
        def _(pool):
            pool.memset(scratch[:, :], 0).then_inc(cleared, 1)
            pool.wait_ge(cleared, 1)
            if chosen:
                pool.wait_ge(x_stored, 16)

            def step(at):
                if k := at(0):
                    pool.wait_ge(placed, k.n + 1)
                    pool.wait_ge(carried[0], cnt(k.n))
                    pool.tensor_tensor(scratch[:, 0:1], scratch[:, 2:3], scratch[:, 3:4], ALU.add
                                       ).then_inc(carried[0], 1)
                    pool.indirect_dma_start(xg[:, k.v, :], None, rows,
                                            bass.IndirectOffsetOnAxis(ap=where[:, k.v:k.v + 1], axis=0)
                                            ).then_inc(xg_in[k.v], 16)
                if gelu and (k := at(5)):
                    pool.wait_ge(biased, k.n + 1)
                    pool.wait_ge(gates, cnt(k.n - 1) * GATE)
                    pool.tensor_tensor(halves[:, k.two, :], hid[:, k.two, :],
                                       parity[:, 1, bass.ds(k.n, 1)].broadcast_to([P, FH]), ALU.mult
                                       ).then_inc(halved, 1)
                if chosen and (k := at(7)):
                    if k.v == 0:
                        for i in range(4):
                            pool.wait_ge(y_out[i], k.round * 16)
                    pool.wait_ge(y_made, k.n * YS + YS)
                    pool.wait_ge(carried[1], cnt(k.n))
                    pool.tensor_tensor(scratch[:, 1:2], scratch[:, 2:3], scratch[:, 3:4], ALU.add
                                       ).then_inc(carried[1], 1)
                    pool.indirect_dma_start(results, bass.IndirectOffsetOnAxis(ap=to[:, k.v:k.v + 1], axis=0),
                                            y[:, k.v, :], None, compute_op=ALU.add).then_inc(y_out[k.v], 16)
            pipeline(pool, N, 8, 4, step)
            if chosen:
                for i in range(4):
                    pool.wait_ge(y_out[i], 16 * N // 4)

        @block.sync
        def _(sp):
            if chosen:
                sp.dma_start(results.rearrange("(n p) d -> p n d", p=P), g.x[:, :, :]).then_inc(x_stored, 16)
                return

            def step(at):
                if k := at(7):
                    sp.wait_ge(y_made, k.n * YS + YS)
                    sp.dma_start(results[bass.ds(k.n * P, P), :], y[:, k.v, :]).then_inc(y_out[k.v], 16)
            pipeline(sp, N, 8, 4, step)
            for i in range(4):
                sp.wait_ge(y_out[i], 16 * N // 4)

        @block.tensor
        def _(pe):
            def step(at):
                if k := at(4):
                    e = expert(pe, k)
                    pe.wait_ge(x_copied, k.n + 1)
                    pe.wait_ge(read_up, cnt(k.n - 1) * (1 if gelu else GATE))
                    pe.matmul(pU[k.two][:, :], xT[:, k.two, :], mix.w_up[:, bass.ds(e * 512, 512)], start=True,
                              stop=True).then_inc(upped, 1)
                if k := at(3):
                    pe.wait_ge(xg_in[k.v], k.round * 16 + 16)
                    pe.wait_ge(x_copied, cnt(k.n - 1))
                    pe.transpose(pX[k.two][:, 0:P], xg[:, k.v, 0:D], g.ident[:, :]).then_inc(turned, 1)
                if k := at(5 + gelu):
                    pe.wait_ge(gates, k.n * GATE + GATE)
                    pe.wait_ge(h_copied, cnt(k.n - 1))
                    for c in range(HC):
                        t = pe.transpose(pH[k.two][:, c * P:(c + 1) * P], gated[:, k.two, c * P:(c + 1) * P],
                                         g.ident[:, :])
                    t.then_inc(h_turned, 1)
                if k := at(6 + gelu):
                    e = expert(pe, k)
                    pe.wait_ge(h_copied, k.n + 1)
                    pe.wait_ge(y_made, cnt(k.n - 1) * YS)
                    for c in range(HC):
                        t = pe.matmul(pY[k.two][:, 0:D], hT[:, k.two, c * P:(c + 1) * P],
                                      mix.w_down[:, bass.ds(e * FH + c * D, D)], start=(c == 0), stop=(c == HC - 1))
                    t.then_inc(downed, 1)
            pipeline(pe, N, 8, 4, step)

        @block.scalar
        def _(act):
            def step(at):
                if k := at(3):
                    act.wait_ge(turned, k.n + 1)
                    act.wait_ge(upped, cnt(k.n - 1))
                    act.copy(xT[:, k.two, :], pX[k.two][:, 0:P]).then_inc(x_copied, 1)
                if k := at(5 + gelu):
                    act.wait_ge(h_turned, k.n + 1)
                    act.wait_ge(downed, cnt(k.n - 1))
                    act.copy(hT[:, k.two, :], pH[k.two][:, 0:FH]).then_inc(h_copied, 1)
                if k := at(4):
                    act.wait_ge(gates, cnt(k.n - 1) * GATE)
                    if gelu:
                        act.wait_ge(biased, k.n + 1)
                        act.activation(first[:, k.two, :], hid[:, k.two, :], ACT.Gelu).then_inc(acted, 1)
                        act.activation(tanh_h[:, k.two, :], hid[:, k.two, :], ACT.Tanh, scale=0.5).then_inc(acted, 1)
                    else:
                        act.wait_ge(upped, k.n + 1)
                        act.activation(first[:, k.two, :], pU[k.two][:, 0:FH], ACT.Silu).then_inc(acted, 1)
            pipeline(act, N, 8, 4, step)

        @block.vector
        def _(dve):
            def step(at):
                if k := at(0):
                    dve.wait_ge(xg_in[k.v], k.round * 16)
                    dve.wait_ge(turned, cnt(k.n - 3))
                    if chosen:
                        dve.wait_ge(noted, cnt(k.n - 3))
                    dve.tensor_scalar(where[:, k.v:k.v + 1], index[:, bass.ds(k.n, 1)], 1.0, None, ALU.mult
                                      ).then_inc(placed, 1)
                if chosen and (k := at(3)):
                    dve.wait_ge(xg_in[k.v], k.round * 16 + 16)
                    dve.wait_ge(y_made, cnt(k.n - 3) * YS)
                    dve.tensor_scalar(share[:, k.v:k.v + 1], xg[:, k.v, bass.ds(k.round + D, 1)], 1.0, None, ALU.mult
                                      ).then_inc(noted, 1)
                if gelu and (k := at(4)):
                    e = expert(dve, k)
                    dve.wait_ge(upped, k.n + 1)
                    dve.wait_ge(acted, cnt(k.n - 1) * ACTS)
                    dve.wait_ge(halved, cnt(k.n - 1))
                    dve.tensor_tensor(hid[:, k.two, :], pU[k.two][:, 0:FH], mix.b_up[:, bass.ds(e * 512, 512)],
                                      ALU.add).then_inc(biased, 1)
                if gelu and (k := at(5)):
                    ch = Chain(dve, gates, k.n * GATE)
                    dve.wait_ge(acted, k.n * ACTS + ACTS)
                    dve.wait_ge(halved, k.n + 1)
                    dve.wait_ge(h_turned, cnt(k.n - 1))
                    ch.link(dve.scalar_tensor_tensor(halves[:, k.two, :], tanh_h[:, k.two, :], 1.0,
                                                     halves[:, k.two, :], ALU.add, ALU.mult))
                    ch.mark(dve.scalar_tensor_tensor(gated[:, k.two, :], first[:, k.two, :],
                                                     parity[:, 0, bass.ds(k.n, 1)], halves[:, k.two, :],
                                                     ALU.mult, ALU.add))
                if not gelu and (k := at(4)):
                    dve.wait_ge(acted, k.n + 1)
                    dve.wait_ge(h_turned, cnt(k.n - 1))
                    dve.tensor_tensor(gated[:, k.two, :], first[:, k.two, :], pU[k.two][:, FH:2 * FH], ALU.mult
                                      ).then_inc(gates, 1)
                if k := at(6 + gelu):
                    e = expert(dve, k) if gelu else None
                    ch = Chain(dve, y_made, k.n * YS)
                    dve.wait_ge(y_out[k.v], k.round * 16)
                    dve.wait_ge(downed, k.n + 1)
                    if gelu:
                        ch.mark(dve.tensor_tensor(y[:, k.v, :], pY[k.two][:, 0:D], mix.b_down[:, bass.ds(e * D, D)],
                                                  ALU.add))
                    elif chosen:
                        dve.wait_ge(noted, k.n + 1)
                        ch.mark(dve.tensor_scalar(y[:, k.v, :], pY[k.two][:, 0:D], share[:, k.v:k.v + 1], None,
                                                  ALU.mult))
                        ch.mark(dve.tensor_scalar(to[:, k.v:k.v + 1], index[:, bass.ds(k.n, 1)], 1.0, None, ALU.mult))
                    else:
                        ch.mark(dve.tensor_scalar(y[:, k.v, :], pY[k.two][:, 0:D], 1.0, None, ALU.mult))

            pipeline(dve, N, 8, 4, step)


def combine_top2(nc, g, mix, results, slots, weight):
    C = CHOICES
    with ExitStack() as ctx:
        m = Memory(nc, ctx, mix.name + "k")
        where, yg = m.sb("where", [P, 4, C], U32), m.sb("yg", [P, 4, C, D])
        scratch = m.sb("scratch", [1, 4], I32)
        carried = [m.sem(f"carried{i}") for i in range(2)]
        y_in = [m.sem(f"y_in{i}") for i in range(4)]
        cleared, placed, added = m.sem("cleared"), m.sem("placed"), m.sem("added")
        K = 1 + ADD_STEPS
        block = ctx.enter_context(nc.Block())

        @block.gpsimd
        def _(pool):
            pool.memset(scratch[:, :], 0).then_inc(cleared, 1)
            pool.wait_ge(cleared, 1)

            def step(at):
                if k := at(0):
                    pool.wait_ge(placed, k.n + 1)
                    pool.wait_ge(carried[0], cnt(k.n))
                    pool.tensor_tensor(scratch[:, 0:1], scratch[:, 2:3], scratch[:, 3:4], ALU.add
                                       ).then_inc(carried[0], 1)
                    for c in range(C):
                        pool.indirect_dma_start(yg[:, k.v, c, :], None, results,
                                                bass.IndirectOffsetOnAxis(ap=where[:, k.v, c:c + 1], axis=0)
                                                ).then_inc(y_in[k.v], 16)
            pipeline(pool, NT, 3, 4, step)

        @block.vector
        def _(dve):
            def step(at):
                if k := at(3):
                    ch = Chain(dve, added, k.n * K)
                    dve.wait_ge(y_in[k.v], k.round * (16 * C) + 16 * C)
                    ch.link(dve.scalar_tensor_tensor(tile_of(g.x, k.n), yg[:, k.v, 0, :],
                                                     weight[:, 0, bass.ds(k.n, 1)], tile_of(g.x, k.n),
                                                     ALU.mult, ALU.add))
                    add_into_x(dve, g, ch, yg[:, k.v, 1, :], weight[:, 1, bass.ds(k.n, 1)], k.n)
                    assert ch.n == K
                if k := at(0):
                    dve.wait_ge(added, cnt(k.n - 3) * K)
                    dve.tensor_scalar(where[:, k.v, :], tile_of(slots, k.n), 1.0, None, ALU.mult).then_inc(placed, 1)
            pipeline(dve, NT, 3, 4, step)


def mixture(nc, g, mix, rows, results):
    C, N = mix.choices, mix.tiles
    with ExitStack() as ctx:
        m = Memory(nc, ctx, mix.name)
        logits, slots = m.sb("logits", [P, NT, E]), m.sb("slots", [P, NT, C])
        weight, index = m.sb("weight", [P, C, NT]), m.sb("index", [P, N], U32)
        tile_expert, parity = m.sb("tile_expert", [P, N], I32), m.sb("parity", [P, 2, N])
        moe_front(nc, g, mix, rows, logits)
        if mix.kind == "experts_choose":
            by_tile = weight[:, :, :].rearrange("p c n -> p (c n)").rearrange("p (n e) -> p n e", e=E)
            choose_tokens(nc, g, mix, logits, slots, by_tile, rows)
            build_index(nc, g, mix, slots, index)
            run_experts(nc, g, mix, rows, index, None, None, results)
            return
        route_top2(nc, g, mix, logits, slots, weight, tile_expert, parity)
        build_index(nc, g, mix, slots, index)
        run_experts(nc, g, mix, rows, index, tile_expert, parity, results)
        combine_top2(nc, g, mix, results, slots, weight)


class Globals:
    pass


def build(nc, io, out):
    with ExitStack() as ctx:
        m = Memory(nc, ctx, "g")
        g = Globals()
        g.x = m.sb("x", [P, NT, D])
        g.mv = m.sb("mv", [P, NT, 2])
        g.rstd = m.sb("rstd", [P, NT])
        g.bn6 = m.sb("bn6", [P, NT, 6])
        g.carrier = m.sb("carrier", [P, 2])
        g.gates, g.tanh_gate = m.sb("gates", [P, 8]), m.sb("tanh_gate", [P, 8])
        g.ident = m.sb("ident", [P, P])
        g.start_in, g.x_in, g.gates_done, g.stat6, g.stats_done, stored = (
            m.sem(k) for k in ("start_in", "x_in", "gates_done", "stat6", "stats_done", "stored"))
        g.w_l0, g.b_l0 = m.sb("w_l0", [P, 2, 2 * D]), m.sb("b_l0", [P, 2 * D])
        g.w_fc, g.w_proj = m.sb("w_fc", [P, 512]), m.sb("w_proj", [P, 4, D])
        g.ones = m.sb("ones", [P, P])
        g.head_mask = {16: m.sb("mask16", [P, 16])[:, :], 4: m.sb("mask4", [P, 4])[:, :]}
        w1 = m.sb("w_l1", [P, 4 * D])
        b1 = m.sb("b_l1", [P, 3 + D])
        w2 = m.sb("w_l2", [P, 4 * D + 32 + D])
        w3 = m.sb("w_l3", [P, 4 * D])
        up_swiglu, down_swiglu = m.sb("up_swiglu", [P, E * 512]), m.sb("down_swiglu", [P, E * 256])
        up2, down2 = m.sb("up2", [P, E * 512]), m.sb("down2", [P, E * 512])
        bias_up2, bias_down2 = m.sb("bias_up2", [P, E * 512]), m.sb("bias_down2", [P, E * D])
        router, bias_router = m.sb("router", [P, 3, E]), m.sb("bias_router", [P, 2, E])
        g.down, g.up, g.token = m.sb("down", [P, E]), m.sb("up", [P, P]), m.sb("token", [P, NT])
        g.up16, g.before, g.ones16 = m.sb("up16", [P, P], F16), m.sb("before", [P, P], BF16), m.sb("ones16", [P, P], BF16)
        g.before_f = m.sb("before_f", [P, P])
        chooser = m.sb("chooser", [P, 2 * P + 1])
        g.same_expert, g.earlier_row, g.row_base = chooser[:, 0:P], chooser[:, P:2 * P], chooser[:, 2 * P:]
        b3 = m.sb("b_l3", [P, 2 + 2 * D])
        own_of3, own = m.sb("own_of3", [P, PERIOD * 24]), m.sb("own", [P, 3 * 4])
        g.own_head_of3 = own_of3[:, :].rearrange("p (c x) -> p c x", c=PERIOD)
        g.own_head = own[:, :].rearrange("p (c h) -> p c h", h=4)
        g.rms_scale = m.sb("rms_scale", [P, 1])
        g.rope_q, g.rope_k = m.sb("rope_q", [P, 2, T]), m.sb("rope_k", [P, 2, S])
        mask_words = m.sb("mask_words", [P, NT * S // 4], I32)
        g.mask8 = mask_words[:, :].bitcast(U8)
        g.ctx_sum2, g.ctx_rstd = m.sb("ctx_sum2", [S, NT]), m.sb("ctx_rstd", [S, NT])
        g.pos = m.sb("pos", [P, NT], I32)
        g.cos_q, g.sin_q = m.sb("cos_q", [P, NT, 4]), m.sb("sin_q", [P, NT, 8])

        w = {
            "start": [(g.ident[:, :], io["ident"]), (g.gates[:, 0:4], row_bcast(io["g_xattn"])),
                      (g.gates[:, 4:8], row_bcast(io["g_ffn"]))],
            "L0a": [(g.w_l0[:, :, 0:D], io["L0_xattn_W_lin"].rearrange("(c p) n -> p c n", p=P)),
                    (g.w_l0[:, :, D:2 * D], io["L0_xattn_W_gate"].rearrange("(c p) n -> p c n", p=P)),
                    (g.b_l0[:, 0:D], row_bcast(io["L0_xattn_b_lin"])),
                    (g.b_l0[:, D:2 * D], row_bcast(io["L0_xattn_b_gate"]))],
            "L0f": [(g.w_fc[:, :], io["w_fcT"]), (g.w_proj[:, :, :], io["w_projT"])],
            "L1a": [(w1[:, 0:3 * D], io["w1_inT"]), (w1[:, 3 * D:4 * D], io["w1_outT"]), (b1[:, 0:3], io["b1_cols"]),
                    (b1[:, 3:3 + D], row_bcast(io["L1_xattn_out_b"])), (g.head_mask[16], io["mask16"]),
                    (g.head_mask[4], io["mask4"]), (own_of3[:, :], io["own_of3"]), (own[:, :], io["own"])],
            "L1f": [(up_swiglu[:, :], io["up1"]), (down_swiglu[:, :], io["down1"])],
            "moe": [(router[:, :, :], io["routers"]),
                    (g.down[:, :], io["down_to_1"]), (g.up[:, :], io["up_from_0"]), (g.token[:, :], io["token"]),
                    (g.up16[:, :], io["up16"]), (g.before_f[:, :], io["before"])],
            "L2a": [(w2[:, 0:4 * D + 32], io["w2_in"]), (w2[:, 4 * D + 32:], io["w2_out"]),
                    (g.rope_q[:, :, :], io["rope_q"]), (g.rope_k[:, :, :], io["rope_k"]),
                    (g.rms_scale[:, :], io["rms_scale"]), (mask_words[:, :], row_bcast(io["mask_words"]))],
            "L2f": [(up2[:, :], io["up2"]), (down2[:, :], io["down2"]), (bias_up2[:, :], row_bcast(io["bias_up2"])),
                    (bias_down2[:, :], row_bcast(io["bias_down2"])), (bias_router[:, 1, :], row_bcast(io["L2_ffn_bg"]))],
            "L3a": [(w3[:, :], io["w3"]), (b3[:, 0:2], io["b3_cols"]), (b3[:, 2:2 + D], row_bcast(io["L3_xattn_bq"])),
                    (b3[:, 2 + D:], row_bcast(io["L3_xattn_bo"])), (g.pos[:, :], io["pos"])],
            "L3c": [(chooser[:, :], io["chooser"])],
            "L3f": [(up_swiglu[:, :], io["up3"]), (down_swiglu[:, :], io["down3"])],
        }
        g.loads = w
        g.bias_router = bias_router
        rows = [nc.dram_tensor(f"rows{i}", (B * T, n), F32, kind="Internal").ap() for i, n in ((1, D), (2, D), (3, D + E))]
        results = [nc.dram_tensor(f"results{i}", (TOP2_TILES * P, D), F32, kind="Internal").ap() for i in (1, 2)]
        mix1 = Mixture("m1", "softmax_first", CHOICES, TOP2_TILES, D, 256, "L1f", 5, router[:, 0, :],
                       bias_router[:, 0, :], up_swiglu, down_swiglu)
        mix2 = Mixture("m2", "logits_first", CHOICES, TOP2_TILES, D, 512, "L2f", 6, router[:, 1, :],
                       bias_router[:, 1, :], up2, down2, bias_up2, bias_down2)
        mix3 = Mixture("m3", "experts_choose", E, CHOSEN_TILES, D + E, 256, "L3f", 7, router[:, 2, :],
                       bias_router[:, 0, :], up_swiglu, down_swiglu)
        g.weights_in = {k: m.sem(f"w_{k}") for k in w}
        heads1 = Heads("a1", 16, w1[:, 0:D], w1[:, D:2 * D], w1[:, 2 * D:3 * D], w1[:, 3 * D:], "L1a", 1,
                       bq=b1[:, 0:1], bk=b1[:, 1:2], bv=b1[:, 2:3], bo=b1[:, 3:])
        heads2 = Heads("a2", 4, w2[:, 0:2 * D], w2[:, 2 * D:4 * D], w2[:, 4 * D:4 * D + 32], w2[:, 4 * D + 32:],
                       "L2a", 2, rope="tables", rms=True)
        heads3 = Heads("a3", 16, w3[:, 0:D], w3[:, D:2 * D], w3[:, 2 * D:3 * D], w3[:, 3 * D:], "L3a", 3,
                       rope="positions", bq=b3[:, 2:2 + D], bk=b3[:, 0:1], bv=b3[:, 1:2], bo=b3[:, 2 + D:])
        blocks = [
            lambda: (rstd_block(nc, g, "r0"), l0_attention(nc, g, io)),
            lambda: (rstd_block(nc, g, "r1"), l0_feed_forward(nc, g, io)),
            lambda: (rstd_block(nc, g, "r2"), attention(nc, g, io, heads1)),
            lambda: (rstd_block(nc, g, "r3"), mixture(nc, g, mix1, rows[0], results[0])),
            lambda: (rstd_block(nc, g, "r4", rms=True), ctx_rms(nc, g), attention(nc, g, io, heads2)),
            lambda: (rstd_block(nc, g, "r5"), mixture(nc, g, mix2, rows[1], results[1])),
            lambda: (rstd_block(nc, g, "r6"), rope_angles(nc, g), attention(nc, g, io, heads3)),
            lambda: (load_later(nc, g), rstd_block(nc, g, "r7"), mixture(nc, g, mix3, rows[2], out)),
        ]
        Memory.used.clear()
        load_inputs(nc, g, io)
        for b, block in enumerate(blocks):
            block()
            if b in (2, 4, 5):
                recycle_semaphores(nc)


def kernel(**inputs):
    import concourse.bacc as bacc
    from concourse.bass_utils import run_bass_kernel_spmd

    a = {k: np.asarray(v) for k, v in inputs.items()}
    def rows(v):
        return v.reshape(-1, P, v.shape[-1]).transpose(1, 0, 2)

    def turned(v, width):
        return np.roll(v.reshape(D, -1, 2, width // 2), 1, axis=2).reshape(v.shape)

    q2 = a["L2_xattn_q_w"].transpose(1, 0, 2).reshape(D, D)
    k2 = np.tile(a["L2_xattn_kv_w"][0, 0], (1, 4))
    v2 = a["L2_xattn_kv_w"][1, 0]
    timescale = np.float32(10000.0) ** (np.float32(2.0 / 32) * np.arange(16, dtype=np.float32))
    part = np.arange(P) % 32

    def rope(positions):
        angle = positions.astype(np.float32)[None, :] / timescale[part % 16][:, None]
        sign = np.where(part < 16, -1, 1).astype(np.float32)[:, None]
        return np.stack([np.cos(angle), sign * np.sin(angle)], axis=1).astype(np.float32)

    def beside(parts):
        return parts.transpose(1, 0, 2).reshape(parts.shape[1], -1)

    def chunks(v):
        return v.reshape(E, -1, P, D).transpose(2, 0, 1, 3).reshape(P, -1)

    at = np.arange(P)
    same = at[:, None] % E == at[None, :] % E

    flat = np.arange(3 * P).reshape(3, P).T
    flat5 = np.arange(PERIOD * P).reshape(PERIOD, P).T
    own = (flat[:, :, None] // PITCH == np.arange(4)) & (flat[:, :, None] % PITCH < S)
    near = np.array(FIRST_HEAD)[:, None] + np.arange(3)
    own_of3 = (flat5[:, :, None] // PITCH == near) & (flat5[:, :, None] % PITCH < S)

    arrays = {
        "own": own.reshape(P, -1).astype(np.float32),
        "own_of3": np.repeat(own_of3, 8, axis=2).reshape(P, -1).astype(np.float32),
        "up1": beside(np.concatenate([a["L1_ffn_w1"], a["L1_ffn_w3"]], axis=2)), "down1": chunks(a["L1_ffn_w2"]),
        "up3": beside(np.concatenate([a["L3_ffn_W1"], a["L3_ffn_W3"]], axis=1).transpose(0, 2, 1)),
        "down3": chunks(a["L3_ffn_W2"].transpose(0, 2, 1)),
        "up2": beside(a["L2_ffn_W1"]), "down2": chunks(a["L2_ffn_W2"]),
        "bias_up2": a["L2_ffn_b1"].reshape(-1), "bias_down2": a["L2_ffn_b2"].reshape(-1), "L2_ffn_bg": a["L2_ffn_bg"],
        "routers": np.stack([a["L1_ffn_gate_w"].T, a["L2_ffn_Wg"], a["L3_ffn_Wg"].T], axis=1),
        "down_to_1": np.tile(np.arange(E, 0, -1, dtype=np.float32), (P, 1)),
        "up_from_0": np.tile(at.astype(np.float32), (P, 1)), "up16": np.tile(at.astype(np.float16), (P, 1)),
        "token": (np.arange(NT)[None, :] * P + at[:, None] - B * T // 2).astype(np.float32),
        "before": (at[:, None] < at[None, :]).astype(np.float32),
        "chooser": np.concatenate([same, same & (at[:, None] < at[None, :]), at[:, None] % E * CAPACITY],
                                  axis=1).astype(np.float32),
        "x": a["x"].transpose(1, 0, 2),
        "ctx": a["ctx_1024"],
        "ctxT": a["ctx_1024"].transpose(0, 2, 1),
        "pos": a["itok_BxS_1_4095"].astype(np.int32).T,
        "mask_words": a["mask_BxS2_bk0"].reshape(-1).view(np.int32),
        "g_xattn": a["g_xattn"], "g_ffn": a["g_ffn"],
        "ident": np.eye(P, dtype=np.float32),
        "mask16": (np.arange(P)[:, None] // 8 == np.arange(16)).astype(np.float32),
        "mask4": (np.arange(P)[:, None] // 32 == np.arange(4)).astype(np.float32),
        "w_fcT": a["L0_ffn_W_fc"].T, "w_projT": rows(a["L0_ffn_W_proj"].T),
        "w1_inT": a["L1_xattn_in_proj_weight"].T, "w1_outT": a["L1_xattn_out_w"].T,
        "b1_cols": a["L1_xattn_in_proj_bias"].reshape(3, D).T,
        "w2_in": np.concatenate([q2, turned(q2, 32), k2, turned(k2, 32), v2], axis=1),
        "w2_out": a["L2_xattn_out_w"].reshape(D, D),
        "rope_q": rope(np.arange(S, S + T)), "rope_k": rope(np.arange(S)),
        "rms_scale": a["L2_xattn_rms_scale"].reshape(D, 1),
        "w3": np.concatenate([a[f"L3_xattn_W{k}"].T for k in "qkvo"], axis=1),
        "b3_cols": np.stack([a["L3_xattn_bk"], a["L3_xattn_bv"]], axis=1),
    }
    for k in ("L0_xattn_W_lin", "L0_xattn_W_gate", "L0_xattn_b_lin", "L0_xattn_b_gate", "L1_xattn_out_b",
              "L3_xattn_bq", "L3_xattn_bo"):
        arrays[k] = a[k]
    arrays = {k: np.ascontiguousarray(v) for k, v in arrays.items()}
    nc = bacc.Bacc("TRN2", target_bir_lowering=False, num_devices=1)
    io = {k: nc.dram_tensor(f"in_{k}", v.shape, mybir.dt.from_np(v.dtype), kind="ExternalInput").ap()
          for k, v in arrays.items()}
    out = nc.dram_tensor("out", (B * T, D), F32, kind="ExternalOutput").ap()
    build(nc, io, out)
    r = run_bass_kernel_spmd(nc, [{f"in_{k}": v for k, v in arrays.items()}], core_ids=[0])
    return r.results[0]["out"].reshape(B, T, D)
```

```python
from contextlib import ExitStack

import numpy as np

import concourse.bass as bass
from concourse import mybir

ALU = mybir.AluOpType
ACT = mybir.ActivationFunctionType
AX = mybir.AxisListType
F32 = mybir.dt.float32
BF16 = mybir.dt.bfloat16
F16 = mybir.dt.float16
I32 = mybir.dt.int32
U32 = mybir.dt.uint32
U8 = mybir.dt.uint8

P = 128
B, T, D = 32, 128, 128
S = 77
NT = B * T // P
E = 8
LN_EPS = 1e-5


def cnt(value):
    return max(value, 0) if isinstance(value, int) else value


def span(n, size):
    return bass.ds(n * size, size)


class Unit:

    def __init__(self, i, w, unroll):
        self.n, self.v, self.round = i * unroll + w, w % unroll, i + w // unroll
        self.w = w
        self.two = self.v % 2


def pipeline(eng, units, lag, unroll, step, begin=None):
    first, full = -(-(lag + unroll) // unroll), units // unroll

    def straight(t):
        if begin and t % unroll == 0:
            begin(t // unroll)
        i, u = t // unroll, t % unroll
        step(lambda k: Unit(i, u - k, unroll) if 0 <= t - k < units else None)

    for t in range(first * unroll):
        straight(t)
    with eng.Fori(first, full) as i:
        if begin:
            begin(i)
        for u in range(unroll):
            step(lambda k, u=u: Unit(i, u - k, unroll))
    for t in range(full * unroll, units + lag):
        straight(t)


class Chain:

    def __init__(self, eng, sem, base=0):
        self.eng, self.sem, self.base, self.n = eng, sem, base, 0

    def mark(self, instruction):
        self.n += 1
        instruction.then_inc(self.sem, 1)

    def link(self, instruction):
        self.mark(instruction)
        self.eng.wait_ge(self.sem, self.base + self.n)


class Memory:

    used = []

    def __init__(self, nc, ctx, prefix):
        self.nc, self.ctx, self.prefix = nc, ctx, prefix

    def sb(self, name, shape, dtype=F32):
        return self.ctx.enter_context(self.nc.sbuf_tensor(f"{self.prefix}_{name}", shape, dtype))

    def ps(self, name, shape=(P, 512), dtype=F32):
        return self.ctx.enter_context(self.nc.psum_tensor(f"{self.prefix}_{name}", list(shape), dtype))

    def sem(self, name):
        handle = self.nc.alloc_semaphore(name=f"{self.prefix}_{name}")
        self.used.append(handle)
        return handle


def recycle_semaphores(nc):
    nc.clear_and_free_semaphores(Memory.used)
    Memory.used.clear()
    nc.all_engine_barrier()


def row_bcast(ap, parts=P):
    n = ap.shape[-1]
    return ap.rearrange("(o n) -> o n", o=1).broadcast_to([parts, n])


def load_inputs(nc, g, io):
    with ExitStack() as ctx:
        block = ctx.enter_context(nc.Block())

        @block.sync
        def _(sp):
            for dst, src in g.loads["start"]:
                sp.dma_start(dst, src).then_inc(g.start_in, 16)
            for half in range(2):
                tiles = slice(half * NT // 2, (half + 1) * NT // 2)
                sp.dma_start(g.x[:, tiles, :], io["x"][:, tiles, :]).then_inc(g.x_in[half], 16)
            for name in ("L0a", "L0f"):
                for dst, src in g.loads[name]:
                    sp.dma_start(dst, src).then_inc(g.weights_in[name], 16)

        @block.scalar
        def _(act):
            act.wait_ge(g.start_in, 16 * len(g.loads["start"]))
            act.activation(g.tanh_gate[:, :], g.gates[:, :], ACT.Tanh).then_inc(g.gates_done, 1)

        @block.vector
        def _(dve):
            dve.memset(g.carrier[:, :], 0.0)
            dve.memset(g.ones[:, :], 1.0)
            dve.memset(g.ones16[:, :], 1.0)
            dve.memset(g.bias_router[:, 0, :], 0.0)
            for half in range(2):
                dve.wait_ge(g.x_in[half], 16)
                with dve.Fori(half * NT // 16, (half + 1) * NT // 16) as i:
                    for u in range(8):
                        dve.bn_stats(tile_of(g.bn6, i * 8 + u), tile_of(g.x, i * 8 + u)).then_inc(g.stats_done, 1)
            dve.wait_ge(g.stats_done, NT)


def load_later(nc, g):
    with nc.Block() as block:
        @block.sync
        def _(sp):
            sp.wait_ge(g.weights_in["L1f"], 16 * len(g.loads["L1f"]))
            for dst, src in g.loads["L3f"]:
                sp.dma_start(dst, src).then_inc(g.weights_in["L3f"], 16)


def rstd_block(nc, g, name, rms=False):
    with ExitStack() as ctx:
        m = Memory(nc, ctx, name)
        a, b = m.sb("a", [P, NT]), m.sb("b", [P, NT])
        shifted, rooted = m.sem("shifted"), m.sem("rooted")
        STEPS = 8
        block = ctx.enter_context(nc.Block())
        even, odd = g.bn6[:, :, 1], g.bn6[:, :, 4]
        even2, odd2 = g.bn6[:, :, 2], g.bn6[:, :, 5]
        mean, var = g.mv[:, :, 0], g.mv[:, :, 1]

        @block.vector
        def _(dve):
            ch = Chain(dve, shifted)
            ch.link(dve.tensor_tensor(a[:, :], even, odd, ALU.subtract))
            ch.link(dve.tensor_tensor(a[:, :], a[:, :], a[:, :], ALU.mult))
            ch.link(dve.tensor_tensor(b[:, :], even2, odd2, ALU.add))
            ch.link(dve.tensor_scalar(b[:, :], b[:, :], 1.0 / D, None, ALU.mult))
            ch.link(dve.scalar_tensor_tensor(var, a[:, :], 0.25, b[:, :], ALU.mult, ALU.add))
            ch.link(dve.tensor_tensor(b[:, :], even, odd, ALU.add))
            ch.link(dve.tensor_scalar(mean, b[:, :], 0.5, None, ALU.mult))
            ch.mark(dve.tensor_scalar(a[:, :], var, LN_EPS, None, ALU.add))
            assert ch.n == STEPS
            dve.wait_ge(rooted, 1)
            ch.link(dve.reciprocal(g.rstd[:, :], b[:, :]))
            if rms:
                ch.link(dve.tensor_tensor(a[:, :], g.rstd[:, :], g.rstd[:, :], ALU.mult))
                ch.link(dve.tensor_tensor(a[:, :], a[:, :], var, ALU.mult))
                ch.mark(dve.tensor_scalar(a[:, :], a[:, :], 1e-6, None, ALU.add))
                dve.wait_ge(rooted, 2)
                ch.link(dve.reciprocal(a[:, :], b[:, :]))
                ch.link(dve.tensor_tensor(g.rstd[:, :], g.rstd[:, :], a[:, :], ALU.mult))

        @block.scalar
        def _(act):
            act.wait_ge(shifted, STEPS)
            act.activation(b[:, :], a[:, :], ACT.Sqrt).then_inc(rooted, 1)
            if rms:
                act.wait_ge(shifted, STEPS + 4)
                act.activation(b[:, :], a[:, :], ACT.Sqrt).then_inc(rooted, 1)


def layer_norm(dve, g, out, n):
    return dve.tensor_scalar(out, tile_of(g.x, n), mv_of(g, n)[:, 0:1], g.rstd[:, bass.ds(n, 1)],
                             ALU.subtract, ALU.mult)


def mv_of(g, n):
    return g.mv[:, bass.ds(n, 1), :].rearrange("p a c -> p (a c)")


def tile_of(tensor, n):
    return tensor[:, bass.ds(n, 1), :].rearrange("p a d -> p (a d)")


ADD_STEPS = 2


def add_into_x(dve, g, ch, value, scale, n):
    ch.mark(dve.scalar_tensor_tensor(tile_of(g.x, n), value, scale, tile_of(g.x, n), ALU.mult, ALU.add))
    tile_stats(dve, g, ch, n)


def tile_stats(dve, g, ch, n):
    dve.wait_ge(ch.sem, ch.base + ch.n)
    dve.tensor_scalar(g.carrier[:, 0:1], g.carrier[:, 1:2], 0.0, None, ALU.mult)
    ch.mark(dve.bn_stats(tile_of(g.bn6, n), tile_of(g.x, n)))


def l0_attention(nc, g, io):
    with ExitStack() as outer:
        mo = Memory(nc, outer, "a0")
        attn = mo.sb("attn", [S, NT, T])
        sumsq = mo.sb("sumsq", [S, NT])
        root = mo.sb("root", [S, NT])
        nine = mo.sb("nine", [S, NT])
        xn_all = mo.sb("xn_all", [P, NT, D])
        xT_all = mo.sb("xT_all", [P, NT, T])
        l0_scores(nc, g, io, attn, sumsq, xn_all, xT_all)
        l0_norms(nc, g, sumsq, root, nine)
        l0_mix(nc, g, io, attn, nine, xn_all, xT_all)


def l0_scores(nc, g, io, attn, sumsq, xn_all, xT_all):
    with ExitStack() as ctx:
        m = Memory(nc, ctx, "a0s")
        xn = m.sb("xn", [P, 2, D])
        xT = m.sb("xT", [P, 2, T])
        ctxT = m.sb("ctxT", [P, 4, S])
        tenth = m.sb("tenth", [S, 2, T])
        junk = m.sb("junk", [S, 2, T])
        pT = [m.ps(f"pT{i}") for i in range(2)]
        pS = [m.ps(f"pS{i}") for i in range(2)]
        ctx_in = [m.sem(f"ctx_in{i}") for i in range(4)]
        normed, turned, copied, scored, tenthed, leaked, squared = (
            m.sem(k) for k in ("normed", "turned", "copied", "scored", "tenthed", "leaked", "squared"))
        block = ctx.enter_context(nc.Block())

        @block.sync
        def _(sp):
            def step(at):
                if k := at(0):
                    sp.wait_ge(scored, cnt(k.n - 3))
                    sp.dma_start(ctxT[:, k.v, :], io["ctxT"][bass.ds(k.n, 1), :, :].rearrange("a p s -> p (a s)")
                                 ).then_inc(ctx_in[k.v], 16)
            pipeline(sp, NT, 0, 4, step)

        @block.vector
        def _(dve):
            def step(at):
                if k := at(0):
                    dve.wait_ge(turned, cnt(k.n - 1))
                    layer_norm(dve, g, xn[:, k.two, :], k.n).then_inc(normed, 1)
                    layer_norm(dve, g, tile_of(xn_all, k.n), k.n).then_inc(normed, 1)
                if k := at(2):
                    dve.wait_ge(tenthed, k.n + 1)
                    dve.tensor_tensor(tile_of(attn, k.n), pS[k.two][0:S, 0:T], tenth[:, k.two, :],
                                      ALU.max).then_inc(leaked, 1)
            pipeline(dve, NT, 3, 4, step)

        @block.tensor
        def _(pe):
            def step(at):
                if k := at(0):
                    pe.wait_ge(normed, k.n * 2 + 1)
                    pe.wait_ge(copied, cnt(k.n * 2 - 2))
                    pe.transpose(pT[k.two][:, 0:T], xn[:, k.two, :], g.ident[:, :]).then_inc(turned, 1)
                if k := at(1):
                    pe.wait_ge(ctx_in[k.v], k.round * 16 + 16)
                    pe.wait_ge(copied, k.n * 2 + 1)
                    pe.wait_ge(leaked, cnt(k.n - 1))
                    pe.matmul(pS[k.two][0:S, 0:T], ctxT[:, k.v, :], xT[:, k.two, :],
                              start=True, stop=True).then_inc(scored, 1)
            pipeline(pe, NT, 3, 4, step)

        @block.scalar
        def _(act):
            def step(at):
                if k := at(0):
                    act.wait_ge(turned, k.n + 1)
                    act.wait_ge(scored, cnt(k.n - 1))
                    act.copy(xT[:, k.two, :], pT[k.two][:, 0:T]).then_inc(copied, 1)
                    act.copy(tile_of(xT_all, k.n), pT[k.two][:, 0:T]).then_inc(copied, 1)
                if k := at(1):
                    act.wait_ge(scored, k.n + 1)
                    act.wait_ge(leaked, cnt(k.n - 1))
                    act.mul(tenth[:, k.two, :], pS[k.two][0:S, 0:T], 0.1).then_inc(tenthed, 1)
                if k := at(3):
                    act.wait_ge(leaked, k.n + 1)
                    act.wait_ge(squared, cnt(k.n - 1))
                    act.activation(junk[:, k.two, :], tile_of(attn, k.n), ACT.Square,
                                   accum_out=sumsq[:, bass.ds(k.n, 1)]).then_inc(squared, 1)
            pipeline(act, NT, 3, 4, step)


def l0_norms(nc, g, sumsq, root, nine):
    with ExitStack() as ctx:
        m = Memory(nc, ctx, "a0n")
        shifted, rooted = m.sem("shifted"), m.sem("rooted")
        block = ctx.enter_context(nc.Block())

        @block.vector
        def _(dve):
            ch = Chain(dve, shifted)
            ch.mark(dve.tensor_scalar(sumsq[:, :], sumsq[:, :], 1e-8, None, ALU.add))
            dve.wait_ge(rooted, 1)
            ch.link(dve.tensor_scalar(root[:, :], root[:, :], 1e-8, None, ALU.add))
            ch.link(dve.reciprocal(nine[:, :], root[:, :]))
            ch.link(dve.tensor_scalar(nine[:, :], nine[:, :], 9.0, None, ALU.mult))

        @block.scalar
        def _(act):
            act.wait_ge(shifted, 1)
            act.activation(root[:, :], sumsq[:, :], ACT.Sqrt).then_inc(rooted, 1)


def l0_mix(nc, g, io, attn, nine, xn_all, xT_all):
    with ExitStack() as ctx:
        m = Memory(nc, ctx, "a0b")
        N2 = 2 * D
        ex = m.sb("ex", [S, 2, T])
        xT = m.sb("xT", [P, 2, T])
        numT = m.sb("numT", [P, 2, T])
        ctxr = m.sb("ctxr", [S, 4, D])
        ones = m.sb("ones", [S, 1])
        rden = m.sb("rden", [P, 2, 1])
        za, z, h = m.sb("za", [P, 2, N2]), m.sb("z", [P, 2, N2]), m.sb("h", [P, 2, N2])
        mix = m.sb("mix", [P, 2, D])
        junk = m.sb("junk", [S, 2, D])
        summed_ctx = m.sem("summed_ctx")
        pN, pA, pB = ([m.ps(f"{k}{i}") for i in range(2)] for k in ("pN", "pA", "pB"))
        ctx_in = [m.sem(f"ctx_in{i}") for i in range(4)]
        ready, exped, summed, num_copied, x_copied, x_part, ctx_part, added, inverted, divided, tanhed, mixed = (
            m.sem(k) for k in ("ready", "exped", "summed", "num_copied", "x_copied", "x_part", "ctx_part", "added",
                               "inverted", "divided", "tanhed", "mixed"))
        K = 3 + ADD_STEPS
        block = ctx.enter_context(nc.Block())

        @block.sync
        def _(sp):
            def step(at):
                if k := at(0):
                    sp.wait_ge(summed, cnt(k.n - 3))
                    sp.wait_ge(summed_ctx, cnt(k.n - 3))
                    sp.dma_start(ctxr[:, k.v, :], io["ctx"][bass.ds(k.n, 1), :, :].rearrange("a s d -> s (a d)")
                                 ).then_inc(ctx_in[k.v], 16)
            pipeline(sp, NT, 0, 4, step)

        @block.gpsimd
        def _(pool):
            pool.memset(ones[:, :], 1.0).then_inc(ready, 1)

        @block.scalar
        def _(act):
            def step(at):
                if k := at(0):
                    act.wait_ge(ctx_in[k.v], k.round * 16 + 16)
                    act.wait_ge(summed_ctx, cnt(k.n - 1))
                    act.activation(junk[:, k.two, :], ctxr[:, k.v, :], ACT.Square,
                                   accum_out=g.ctx_sum2[:, bass.ds(k.n, 1)]).then_inc(summed_ctx, 1)
                    act.wait_ge(summed, cnt(k.n - 1))
                    act.activation(ex[:, k.two, :], tile_of(attn, k.n), ACT.Exp,
                                   scale=nine[:, bass.ds(k.n, 1)]).then_inc(exped, 1)
                    act.wait_ge(x_part, cnt(k.n - 1))
                    act.copy(xT[:, k.two, :], tile_of(xT_all, k.n)).then_inc(x_copied, 1)
                if k := at(1):
                    act.wait_ge(summed, k.n + 1)
                    act.wait_ge(ctx_part, cnt(k.n - 1))
                    act.copy(numT[:, k.two, :], pN[k.two][:, 0:T]).then_inc(num_copied, 1)
                if k := at(3):
                    act.wait_ge(divided, k.n + 1)
                    act.wait_ge(mixed, cnt((k.n - 2) * K + 3))
                    act.activation(h[:, k.two, 0:D], z[:, k.two, 0:D], ACT.Tanh).then_inc(tanhed, 1)
                    act.activation(h[:, k.two, D:N2], z[:, k.two, D:N2], ACT.Tanh, scale=0.5).then_inc(tanhed, 1)
            pipeline(act, NT, 4, 4, step)

        @block.tensor
        def _(pe):
            pe.wait_ge(ready, 1)
            pe.wait_ge(g.weights_in["L0a"], 16 * len(g.loads["L0a"]))

            def step(at):
                if k := at(2):
                    pe.wait_ge(num_copied, k.n + 1)
                    pe.wait_ge(divided, cnt(k.n - 1))
                    pe.matmul(pB[k.two][:, 0:N2], numT[:, k.two, :], g.w_l0[:, 1, :], start=True,
                              stop=True).then_inc(ctx_part, 1)
                if k := at(0):
                    pe.wait_ge(exped, k.n + 1)
                    pe.wait_ge(ctx_in[k.v], k.round * 16 + 16)
                    pe.wait_ge(inverted, cnt(k.n - 1))
                    pe.matmul(pN[k.two][:, 0:T], ctxr[:, k.v, :], ex[:, k.two, :], start=True, stop=True)
                    pe.matmul(pN[k.two][:, T:T + 1], ex[:, k.two, :], ones[:, :], start=True,
                              stop=True).then_inc(summed, 1)
                    pe.wait_ge(x_copied, k.n + 1)
                    pe.wait_ge(added, cnt(k.n - 1))
                    pe.matmul(pA[k.two][:, 0:N2], xT[:, k.two, :], g.w_l0[:, 0, :], start=True,
                              stop=True).then_inc(x_part, 1)
            pipeline(pe, NT, 4, 4, step)

        @block.vector
        def _(dve):
            dve.wait_ge(g.weights_in["L0a"], 16 * len(g.loads["L0a"]))
            dve.wait_ge(g.gates_done, 1)

            def step(at):
                a, d, k = at(1), at(2), at(4)
                if k:
                    ch = Chain(dve, mixed, k.n * K)
                    hh, tt, mm = h[:, k.two, 0:D], h[:, k.two, D:N2], mix[:, k.two, :]
                    dve.wait_ge(tanhed, k.n * 2 + 2)
                    ch.mark(dve.tensor_tensor(mm, tile_of(xn_all, k.n), hh, ALU.subtract))
                if a:
                    dve.wait_ge(x_part, a.n + 1)
                    dve.wait_ge(divided, cnt(a.n - 1))
                    dve.tensor_tensor(za[:, a.two, :], pA[a.two][:, 0:N2], g.b_l0[:, :], ALU.add).then_inc(added, 1)
                if k:
                    dve.wait_ge(mixed, k.n * K + 1)
                    ch.mark(dve.scalar_tensor_tensor(mm, tt, 1.0, mm, ALU.add, ALU.mult))
                if d:
                    dve.wait_ge(inverted, d.n + 1)
                    dve.wait_ge(ctx_part, d.n + 1)
                    dve.wait_ge(added, d.n + 1)
                    dve.wait_ge(tanhed, cnt(d.n - 1) * 2)
                    dve.scalar_tensor_tensor(z[:, d.two, :], pB[d.two][:, 0:N2], rden[:, d.two, :], za[:, d.two, :],
                                             ALU.mult, ALU.add).then_inc(divided, 1)
                if k:
                    dve.wait_ge(mixed, k.n * K + 2)
                    ch.mark(dve.scalar_tensor_tensor(mm, mm, 0.5, hh, ALU.mult, ALU.add))
                if a:
                    dve.wait_ge(num_copied, a.n + 1)
                    dve.wait_ge(divided, cnt(a.n - 1))
                    dve.reciprocal(rden[:, a.two, :], pN[a.two][:, T:T + 1]).then_inc(inverted, 1)
                if k:
                    dve.wait_ge(mixed, k.n * K + 3)
                    add_into_x(dve, g, ch, mm, g.tanh_gate[:, 0:1], k.n)
                    assert ch.n == K
            pipeline(dve, NT, 4, 4, step)


SPIKES = 5


def l0_feed_forward(nc, g, io):
    FC = 512 // P
    T2 = 2 * T
    PAIRS = NT // 2

    def both(tensor, n):
        return tensor[:, bass.ds(n * 2, 2), :].rearrange("p a d -> p (a d)")

    with ExitStack() as ctx:
        m = Memory(nc, ctx, "f0")
        xn, xT = m.sb("xn", [P, 2, T2]), m.sb("xT", [P, 2, T2])
        act1, sq = m.sb("act1", [P, 2, FC * T2]), m.sb("sq", [P, 2, FC * T2])
        y, count, drive = m.sb("y", [P, 2, T2]), m.sb("count", [P, T2]), m.sb("drive", [P, T2])
        mem = m.sb("mem", [P, 2, T2])
        fifth = m.sb("fifth", [P, 1])
        pT, pY = ([m.ps(f"{k}{i}") for i in range(2)] for k in ("pT", "pY"))
        pH = [m.ps(f"pH{i}", (P, FC * T2)) for i in range(2)]
        ready, normed, turned, copied, hidden, relued, squared, projected, y_copied, spiked = (
            m.sem(k) for k in ("ready", "normed", "turned", "copied", "hidden", "relued", "squared", "projected",
                               "y_copied", "spiked"))
        K = 3 * SPIKES - 2 + 3
        block = ctx.enter_context(nc.Block())

        @block.sync
        def _(sp):
            for name in ("L1a", "moe", "L1f", "L2a", "L2f", "L3a", "L3c"):
                for dst, src in g.loads[name]:
                    sp.dma_start(dst, src).then_inc(g.weights_in[name], 16)

        @block.vector
        def _(dve):
            dve.tensor_scalar(fifth[:, :], g.tanh_gate[:, 4:5], 1.0 / SPIKES, None, ALU.mult).then_inc(ready, 1)
            dve.wait_ge(ready, 1)

            def step(at):
                if k := at(0):
                    dve.wait_ge(turned, cnt(k.n - 1))
                    for t in range(2):
                        layer_norm(dve, g, xn[:, k.two, t * D:(t + 1) * D], k.n * 2 + t).then_inc(normed, 1)
                if k := at(5):
                    ch = Chain(dve, spiked, k.n * K)
                    yy = y[:, k.two, :]
                    dve.wait_ge(y_copied, k.n + 1)
                    before = yy
                    for s in range(1, SPIKES):
                        if s > 1:
                            ch.mark(dve.scalar_tensor_tensor(drive[:, :], before, 1.0, yy, ALU.is_gt, ALU.subtract))
                            ch.mark(dve.scalar_tensor_tensor(count[:, :], before, 1.0, count[:, :], ALU.is_gt, ALU.add))
                        else:
                            ch.mark(dve.scalar_tensor_tensor(drive[:, :], before, 1.0, yy, ALU.is_gt, ALU.subtract))
                            ch.mark(dve.tensor_scalar(count[:, :], yy, 1.0, None, ALU.is_gt))
                        dve.wait_ge(spiked, ch.base + ch.n - 1)
                        ch.link(dve.scalar_tensor_tensor(mem[:, s % 2, :], before, 0.9, drive[:, :], ALU.mult,
                                                         ALU.subtract))
                        before = mem[:, s % 2, :]
                    ch.link(dve.scalar_tensor_tensor(count[:, :], before, 1.0, count[:, :], ALU.is_gt, ALU.add))
                    ch.mark(dve.scalar_tensor_tensor(both(g.x, k.n), count[:, :], fifth[:, 0:1], both(g.x, k.n),
                                                     ALU.mult, ALU.add))
                    for t in range(2):
                        tile_stats(dve, g, ch, k.n * 2 + t)
                    assert ch.n == K
            pipeline(dve, PAIRS, 5, 4, step)

        @block.tensor
        def _(pe):
            pe.wait_ge(g.weights_in["L0f"], 16 * len(g.loads["L0f"]))

            def step(at):
                if k := at(1):
                    pe.wait_ge(copied, k.n + 1)
                    pe.wait_ge(relued, cnt(k.n - 1))
                    for c in range(FC):
                        mm = pe.matmul(pH[k.two][:, c * T2:(c + 1) * T2], g.w_fc[:, c * P:(c + 1) * P], xT[:, k.two, :],
                                       start=True, stop=True)
                    mm.then_inc(hidden, 1)
                if k := at(0):
                    pe.wait_ge(normed, k.n * 2 + 2)
                    pe.wait_ge(copied, cnt(k.n - 1))
                    for t in range(2):
                        tr = pe.transpose(pT[k.two][:, t * T:(t + 1) * T], xn[:, k.two, t * D:(t + 1) * D],
                                          g.ident[:, :])
                    tr.then_inc(turned, 1)
                if k := at(3):
                    pe.wait_ge(squared, k.n + 1)
                    pe.wait_ge(y_copied, cnt(k.n - 1))
                    for t in range(2):
                        for c in range(FC):
                            start = c * T2 + t * T
                            mm = pe.matmul(pY[k.two][:, t * D:(t + 1) * D], sq[:, k.two, start:start + T],
                                           g.w_proj[:, c, :], start=(c == 0), stop=(c == FC - 1))
                    mm.then_inc(projected, 1)
            pipeline(pe, PAIRS, 5, 4, step)

        @block.scalar
        def _(act):
            def step(at):
                if k := at(4):
                    act.wait_ge(projected, k.n + 1)
                    act.wait_ge(spiked, cnt(k.n - 1) * K)
                    act.copy(y[:, k.two, :], pY[k.two][:, 0:T2]).then_inc(y_copied, 1)
                if k := at(1):
                    act.wait_ge(hidden, k.n + 1)
                    act.wait_ge(squared, cnt(k.n - 1))
                    act.activation(act1[:, k.two, :], pH[k.two][:, :], ACT.Relu).then_inc(relued, 1)
                if k := at(0):
                    act.wait_ge(turned, k.n + 1)
                    act.wait_ge(hidden, cnt(k.n - 1))
                    act.copy(xT[:, k.two, :], pT[k.two][:, 0:T2]).then_inc(copied, 1)
            pipeline(act, PAIRS, 5, 4, step)

        @block.gpsimd
        def _(pool):
            def step(at):
                if k := at(2):
                    pool.wait_ge(relued, k.n + 1)
                    pool.wait_ge(projected, cnt(k.n - 1))
                    pool.tensor_tensor(sq[:, k.two, :], act1[:, k.two, :], act1[:, k.two, :], ALU.mult
                                       ).then_inc(squared, 1)
            pipeline(pool, PAIRS, 5, 4, step)


MASK_FILL = -2.3819763e38
HIGH = 3.3e38


class Heads:

    def __init__(self, name, heads, wq, wk, wv, wo, load, gate, rope=None, rms=False, bq=None, bk=None, bv=None,
                 bo=None):
        self.name, self.heads, self.width = name, heads, D // heads
        self.wq, self.wk, self.wv, self.wo = wq, wk, wv, wo
        self.load, self.gate, self.rope, self.rms = load, gate, rope, rms
        self.bq, self.bk, self.bv, self.bo = bq, bk, bv, bo
        per = 512 // S
        self.banks = [(h, min(per, heads - h)) for h in range(0, heads, per)]
        self.chunks = -(-heads * PITCH // P)
        self.groups = [range(c, min(c + 4, self.chunks)) for c in range(0, self.chunks, 4)]
        self.blocks = len(self.groups)


PITCH = 80
PERIOD = 5
FIRST_HEAD = (0, 1, 3, 4, 5)


def attention(nc, g, io, a, merge=None):
    H, W = a.heads, a.width
    SB = len(a.banks)
    with ExitStack() as ctx:
        m = Memory(nc, ctx, a.name)
        xn, xT = m.sb("xn", [P, 2, D]), m.sb("xT", [P, 2, T])
        qT, kT = m.sb("qT", [P, 2, T]), m.sb("kT", [P, 2, S])
        kS = m.sb("kS", [P, 2, H, S])
        vS = m.sb("vS", [P, 4, a.chunks * D])
        ctxT = m.sb("ctxT", [P, 4, 3, PITCH])
        ex = m.sb("ex", [P, 2, a.chunks * P])
        exT = m.sb("exT", [P, 2, 4 * T])
        nmax, total, over = m.sb("nmax", [P, 2, H]), m.sb("total", [P, 2, H]), m.sb("over", [P, 2, H])
        overx, overT, oT = m.sb("overx", [P, 2, D]), m.sb("overT", [P, 2, T]), m.sb("oT", [P, 2, T])
        pF, pQ, pO = m.ps("pF"), m.ps("pQ"), m.ps("pO")
        pS = m.ps("pS", (P, SB, 512))
        pE = [m.ps(f"pE{i}") for i in range(2)]
        ctx_in = [m.sem(f"ctx_in{i}") for i in range(4)]
        (cleared, wide_bias, bias_product, bias_steps, scaled, normed, turned, x_copied, q_made, q_steps, q_turned,
         q_copied, k_made, k_copied, spread, v_taken, scored, shifted, exped, summed, spread_over, over_turned,
         over_copied, roped, ceiled, v_spread, ex_turned, ex_copied, weighted, divided, projected, added, biased, ctx_normed, ctx_turned,
         ctx_copied) = (m.sem(k) for k in (
             "cleared", "wide_bias", "bias_product", "bias_steps", "scaled", "normed", "turned", "x_copied", "q_made",
             "q_steps", "q_turned", "q_copied", "k_made", "k_copied", "spread", "v_taken", "scored",
             "shifted", "exped", "summed", "spread_over", "over_turned", "over_copied", "roped", "ceiled", "v_spread", "ex_turned", "ex_copied",
             "weighted", "divided", "projected", "added", "biased", "ctx_normed", "ctx_turned", "ctx_copied"))
        if a.rms:
            ctxr, ctxn = m.sb("ctxr", [S, 4, D]), m.sb("ctxn", [S, 2, D])
            ceiling, v_one = m.sb("ceiling", [P, NT * S]), m.sb("v_one", [P, 2, a.chunks * W])
            rq, rk = m.sb("rq", [P, 2, T]), m.sb("rk", [P, 2, S])
        if a.rope == "positions":
            qrow, biased_q, swapped = m.sb("qrow", [P, 2, D]), m.sb("biased_q", [P, 2, D]), m.sb("swapped", [P, D])
        if a.bo is not None:
            bv_wide, out_bias = m.sb("bv_wide", [P, P]), m.sb("out_bias", [P, D])
        SHIFT = 3 if a.rms else 2 * SB
        QSTEPS, QREADY = {None: (1, 1), "tables": (6, 5), "positions": (1, None)}[a.rope]
        ROPE = 4
        CLEARED = 3
        KC = 2 * T
        VC = KC + 2 * S if a.rms else T
        PLACE, GATHER, MERGE, SCALE = range(0, 4) if not merge else (0, 1, 3, 4)
        K0 = 5 if merge else 0
        LAST = K0 + 4
        if merge:
            where, yg = m.sb("where", [P, 4, CHOICES], U32), m.sb("yg", [P, 4, CHOICES, D])
            scratch = m.sb("scratch", [1, 4], I32)
            bn6, mv, spread2 = m.sb("bn6", [P, 4, 6]), m.sb("mv", [P, 4, 2]), m.sb("spread2", [P, 4])
            scale, square, consts = m.sb("scale", [P, 4]), m.sb("square", [P, 1]), m.sb("consts", [P, 2])
            y_in = [m.sem(f"y_in{i}") for i in range(4)]
            begun, placed, merged, scales, carried = (m.sem(k) for k in ("begun", "placed", "merged", "scales",
                                                                         "carried"))
            MERGES = 7
            SCALES = 6 if a.rms else 1
        block = ctx.enter_context(nc.Block())

        def ex_heads(two):
            return ex[:, two, 0:H * PITCH].rearrange("p (h x) -> p h x", x=PITCH)[:, :, 0:S]

        def rows_of(slot, c):
            start = c * P % PITCH
            return ctxT[:, slot, :, :].rearrange("p a x -> p (a x)")[:, start:start + P]

        @block.sync
        def _(sp):
            def step(at):
                if k := at(max(K0 - 1, 0)):
                    if a.rms:
                        sp.wait_ge(ctx_normed, cnt(k.n - 3))
                        sp.dma_start(ctxr[:, k.v, :], tile_rows(io["ctx"], k.n)).then_inc(ctx_in[k.v], 16)
                    else:
                        sp.wait_ge(q_made, cnt(k.n - 3))
                        sp.dma_start(ctxT[:, k.v, :, 0:S], tile_rows(io["ctxT"], k.n).unsqueeze(1).broadcast_to(
                            [P, 3, S])).then_inc(ctx_in[k.v], 16)
            sp.wait_ge(cleared, CLEARED)
            pipeline(sp, NT, LAST, 4, step)

        @block.gpsimd
        def _(pool):
            if merge:
                pool.memset(scratch[:, :], 0).then_inc(begun, 1)
                pool.memset(consts[:, 0:1], -0.5).then_inc(begun, 1)
                pool.memset(consts[:, 1:2], 1e-6).then_inc(begun, 1)
                pool.wait_ge(begun, 3)
            for t in (vS, ex, ctxT):
                pool.memset(t[:], 0.0).then_inc(cleared, 1)
            if a.bo is not None:
                pool.wait_ge(bias_steps, 2)

            def rope(k):
                ch = Chain(pool, roped, k.n * ROPE)
                pool.wait_ge(q_steps, k.n * QSTEPS + QSTEPS)
                pool.wait_ge(q_turned, cnt(k.n - 1))
                pool.wait_ge(roped, k.n * ROPE)
                q0, q2 = (v.rearrange("p (h c f) -> p h c f", c=2, f=W // 2)
                          for v in (biased_q[:, k.two, :], swapped[:, :]))
                cos, sin = tile_of(g.cos_q, k.n), tile_of(g.sin_q, k.n)
                for half in range(2):
                    ch.mark(pool.tensor_tensor(
                        q2[:, :, half, :], q0[:, :, 1 - half, :],
                        wide(sin[:, half * W // 2:(half + 1) * W // 2], H), ALU.mult))
                ch.link(pool.tensor_tensor(qrow[:, k.two, :].rearrange("p (g f) -> p g f", f=W // 2),
                                           biased_q[:, k.two, :].rearrange("p (g f) -> p g f", f=W // 2),
                                           wide(cos, 2 * H), ALU.mult))
                ch.mark(pool.tensor_tensor(qrow[:, k.two, :], qrow[:, k.two, :], swapped[:, :], ALU.add))
                assert ch.n == ROPE

            def step(at):
                if e := at(K0 + 3):
                    pool.wait_ge(summed, e.n * 2 + 2)
                    pool.wait_ge(over_turned, cnt(e.n - 1))
                    pool.tensor_tensor(overx[:, e.two, :].rearrange("p (h w) -> p h w", h=H),
                                       over[:, e.two, :].unsqueeze(2).broadcast_to([P, H, W]),
                                       g.ones[:, 0:D].rearrange("p (h w) -> p h w", h=H), ALU.mult
                                       ).then_inc(spread_over, 1)
                    if a.bo is not None:
                        pool.wait_ge(normed, e.n + 1)
                        pool.tensor_tensor(tile_of(g.x, e.n), tile_of(g.x, e.n), out_bias[:, :], ALU.add
                                           ).then_inc(biased, 1)
                if merge and (n := at(GATHER)):
                    pool.wait_ge(placed, n.n + 1)
                    pool.wait_ge(carried, cnt(n.n))
                    pool.tensor_tensor(scratch[:, 0:1], scratch[:, 2:3], scratch[:, 3:4], ALU.add
                                       ).then_inc(carried, 1)
                    for c in range(CHOICES):
                        pool.indirect_dma_start(yg[:, n.v, c, :], None, merge,
                                                bass.IndirectOffsetOnAxis(ap=where[:, n.v, c:c + 1], axis=0)
                                                ).then_inc(y_in[n.v], 16)
                if merge and (n := at(SCALE)):
                    ch = Chain(pool, scales, n.n * SCALES)
                    pool.wait_ge(merged, n.n * MERGES + MERGES)
                    pool.wait_ge(normed, cnt(n.n - 3))
                    s = scale[:, n.v:n.v + 1]
                    ch.link(pool.tensor_tensor(s, spread2[:, n.v:n.v + 1], consts[:, 0:1], ALU.pow))
                    if a.rms:
                        ch.link(pool.tensor_tensor(square[:, :], s, s, ALU.mult))
                        ch.link(pool.tensor_tensor(square[:, :], square[:, :], mv[:, n.v, 1:2], ALU.mult))
                        ch.link(pool.tensor_tensor(square[:, :], square[:, :], consts[:, 1:2], ALU.add))
                        ch.link(pool.tensor_tensor(square[:, :], square[:, :], consts[:, 0:1], ALU.pow))
                        ch.mark(pool.tensor_tensor(s, s, square[:, :], ALU.mult))
                    assert ch.n == SCALES
                k = at(K0)
                if k and a.rope == "positions":
                    rope(k)
                if k:
                    if a.rms:
                        pool.wait_ge(q_steps, k.n * QSTEPS + QSTEPS)
                    else:
                        pool.wait_ge(k_copied, k.n + 1)
                    pool.wait_ge(scored, cnt(k.n - 1) * SB)
                    pool.tensor_tensor(kS[:, k.two, :, :], wide(kT[:, k.two, :], H), heads_mask(g, a),
                                       ALU.mult).then_inc(spread, 1)
                if k and a.rms:
                    pool.wait_ge(v_taken, k.n + 1)
                    pool.wait_ge(weighted, cnt(k.n - 3) * a.blocks)
                    shape = [P, a.chunks, H, W]
                    pool.tensor_tensor(vS[:, k.v, :].rearrange("p (c h w) -> p c h w", h=H, w=W),
                                       v_one[:, k.two, :].rearrange("p (c w) -> p c w", w=W).unsqueeze(2
                                                                                                   ).broadcast_to(shape),
                                       g.own_head.unsqueeze(3).broadcast_to(shape), ALU.mult).then_inc(v_spread, 1)
            pipeline(pool, NT, LAST, 4, step)

        @block.tensor
        def _(pe):
            pe.wait_ge(g.weights_in[a.load], 16 * len(g.loads[a.load]))
            if a.bo is not None:
                pe.wait_ge(wide_bias, 1)
                pe.matmul(pO[:, 0:D], bv_wide[:, :], a.wo, start=True, stop=True).then_inc(bias_product, 1)
                pe.wait_ge(bias_steps, 1)
            if a.rms:
                pe.wait_ge(scaled, 3)

            def turn(k, b):
                pe.wait_ge(ex_copied, cnt(k.n * a.blocks + b - 1))
                r = (k.two * a.blocks + b) % 2
                for j, c in enumerate(a.groups[b]):
                    t = pe.transpose(pE[r][:, j * T:(j + 1) * T], ex[:, k.two, c * P:(c + 1) * P], g.ident[:, :])
                t.then_inc(ex_turned, 1)

            def weigh(k, b):
                pe.wait_ge(ex_copied, k.n * a.blocks + b + 1)
                r = (k.two * a.blocks + b) % 2
                for j, c in enumerate(a.groups[b]):
                    start = c * D - (0 if a.rms else W * (FIRST_HEAD[c % PERIOD] + c // PERIOD * H // 2))
                    t = pe.matmul(pO[:, 0:T], vS[:, k.v, start:start + D], exT[:, r, j * T:(j + 1) * T],
                                  start=(c == 0), stop=(c == a.chunks - 1))
                t.then_inc(weighted, 1)

            def make_v(k):
                for c in range(min(a.chunks, PERIOD)):
                    if a.rms:
                        t = pe.matmul(pQ[:, VC + c * W:VC + (c + 1) * W], rows_of(k.two, c), a.wv, start=True, stop=True)
                    else:
                        wv = a.wv.rearrange("p (g x) -> p g x", g=2)[:, :, W * FIRST_HEAD[c]:W * (FIRST_HEAD[c] + 3)]
                        t = pe.matmul(pQ[:, VC + c * 6 * W:VC + (c + 1) * 6 * W], rows_of(k.v, c), wv, start=True,
                                      stop=True)
                t.then_inc(q_made, 1)

            def q_and_k(k):
                pe.wait_ge(x_copied, k.n + 1)
                pe.wait_ge(v_taken, cnt(k.n))
                if a.rms:
                    pe.matmul(pQ[:, 0:T], a.wq[:, 0:D], xT[:, k.two, :], start=True, stop=True)
                    pe.matmul(pQ[:, T:2 * T], a.wq[:, D:2 * D], xT[:, k.two, :], start=True, stop=True)
                    pe.wait_ge(ctx_normed, k.n + 1)
                    pe.transpose(pF[:, 0:S], ctxn[:, k.two, :], g.ident[0:S, 0:S]).then_inc(ctx_turned, 1)
                    pe.wait_ge(ctx_copied, k.n + 1)
                    c = ctxT[:, k.two, 0, 0:S]
                    pe.matmul(pQ[:, KC:KC + S], a.wk[:, 0:D], c, start=True, stop=True)
                    pe.matmul(pQ[:, KC + S:KC + 2 * S], a.wk[:, D:2 * D], c, start=True, stop=True)
                    make_v(k)
                    return
                pe.wait_ge(ctx_in[k.v], k.round * 16 + 16)
                pe.matmul(pF[:, 0:S], a.wk, ctxT[:, k.v, 0, 0:S], start=True, stop=True).then_inc(k_made, 1)
                if a.rope == "positions":
                    pe.matmul(pQ[:, 0:D], xT[:, k.two, :], a.wq, start=True, stop=True)
                else:
                    pe.matmul(pQ[:, 0:T], a.wq, xT[:, k.two, :], start=True, stop=True)
                make_v(k)

            def turn_q(r, e, k):
                pe.wait_ge(roped, r.n * ROPE + ROPE)
                if e:
                    pe.wait_ge(over_copied, e.n + 1)
                elif k:
                    pe.wait_ge(k_copied, k.n + 1)
                pe.transpose(pF[:, 0:T], qrow[:, r.two, :], g.ident[:, :]).then_inc(q_turned, 1)

            def step(at):
                k, r, c, e, o = (at(K0 + lag) for lag in range(5))
                if c:
                    pe.wait_ge(spread, c.n + 1)
                    if QREADY:
                        pe.wait_ge(q_steps, c.n * QSTEPS + QREADY)
                    else:
                        pe.wait_ge(q_copied, c.n + 1)
                    pe.wait_ge(shifted, c.n * SHIFT)
                    for j, (h, n) in enumerate(a.banks):
                        pe.matmul(pS[:, j, 0:n * S], qT[:, c.two, :],
                                  kS[:, c.two, h:h + n, :].rearrange("p h s -> p (h s)"), start=True, stop=True
                                  ).then_inc(scored, 1)
                if o:
                    pe.wait_ge(divided, o.n + 1)
                    pe.matmul(pO[:, 0:D], oT[:, o.two, :], a.wo, start=True, stop=True).then_inc(projected, 1)
                if k:
                    pe.wait_ge(ctx_copied if a.rms else k_copied, k.n)
                    pe.wait_ge(over_copied, cnt(k.n - 3))
                    if a.rope == "positions":
                        pe.wait_ge(q_copied, cnt(k.n - 1))
                    pe.wait_ge(normed, k.n + 1)
                    pe.transpose(pF[:, 0:T], xn[:, k.two, :], g.ident[:, :]).then_inc(turned, 1)
                if e:
                    pe.wait_ge(exped, e.n + 1)
                    turn(e, 0)
                if k:
                    q_and_k(k)
                if e:
                    if a.blocks > 1:
                        turn(e, 1)
                    pe.wait_ge(spread_over, e.n + 1)
                    if k:
                        pe.wait_ge(ctx_copied if a.rms else k_copied, k.n + 1)
                    else:
                        pe.wait_ge(over_copied, e.n)
                        if a.rope == "positions":
                            pe.wait_ge(q_copied, min(e.n + 2, NT))
                    pe.transpose(pF[:, 0:T], overx[:, e.two, :], g.ident[:, :]).then_inc(over_turned, 1)
                    pe.wait_ge(v_spread if a.rms else v_taken, e.n + 1)
                    pe.wait_ge(added, e.n * ADD_STEPS)
                    for b in range(a.blocks):
                        if r and a.rope == "positions" and b == 1:
                            turn_q(r, e, k)
                        weigh(e, b)
                        if b + 2 < a.blocks:
                            turn(e, b + 2)
                if r and not e and a.rope == "positions":
                    turn_q(r, e, k)
            pipeline(pe, NT, LAST, 4, step)

        @block.scalar
        def _(act):
            def copy_heads(e, b):
                act.wait_ge(ex_turned, e.n * a.blocks + b + 1)
                act.wait_ge(weighted, cnt(e.n * a.blocks + b - 1))
                r = (e.two * a.blocks + b) % 2
                n = len(a.groups[b]) * T
                act.copy(exT[:, r, 0:n], pE[r][:, 0:n]).then_inc(ex_copied, 1)

            def step(at):
                k, r, c, e = (at(K0 + lag) for lag in range(4))
                if k:
                    act.wait_ge(turned, k.n + 1)
                    act.wait_ge(q_made, cnt(k.n - 1))
                    act.copy(xT[:, k.two, :], pF[:, 0:T]).then_inc(x_copied, 1)
                if e and not a.rms:
                    copy_heads(e, 0)
                if k and a.rms:
                    act.wait_ge(ctx_turned, k.n + 1)
                    act.wait_ge(q_made, cnt(k.n - 1))
                    act.copy(ctxT[:, k.two, :, 0:S], wide(pF[:, 0:S], 3)).then_inc(ctx_copied, 1)
                elif k:
                    act.wait_ge(k_made, k.n + 1)
                    act.wait_ge(spread, cnt(k.n - 1))
                    act.activation(kT[:, k.two, :], pF[:, 0:S], ACT.Identity, bias=a.bk).then_inc(k_copied, 1)
                if e:
                    copy_heads(e, 0 if a.rms else 1)
                    act.wait_ge(over_turned, e.n + 1)
                    act.wait_ge(divided, cnt(e.n - 1))
                    act.copy(overT[:, e.two, :], pF[:, 0:T]).then_inc(over_copied, 1)
                    for b in range(2, a.blocks):
                        copy_heads(e, b)
                if r and a.rope == "positions":
                    act.wait_ge(q_turned, r.n + 1)
                    act.wait_ge(scored, cnt(r.n - 1) * SB)
                    act.copy(qT[:, r.two, :], pF[:, 0:T]).then_inc(q_copied, 1)
                if c:
                    act.wait_ge(shifted, c.n * SHIFT + SHIFT)
                    e1 = ex_heads(c.two)
                    act.activation(e1, e1, ACT.Exp, scale=float(W) ** -0.5).then_inc(exped, 1)
            pipeline(act, NT, LAST, 4, step)

        @block.vector
        def _(dve):
            dve.wait_ge(g.weights_in[a.load], 16 * len(g.loads[a.load]))
            dve.wait_ge(g.gates_done, 1)
            dve.wait_ge(cleared, CLEARED)
            gate = g.tanh_gate[:, a.gate:a.gate + 1]
            if a.bo is not None:
                dve.tensor_scalar(bv_wide[:, :], g.ones[:, 0:P], a.bv, None, ALU.mult).then_inc(wide_bias, 1)
                dve.wait_ge(bias_product, 1)
                ch = Chain(dve, bias_steps)
                ch.link(dve.tensor_tensor(out_bias[:, :], pO[:, 0:D], a.bo, ALU.add))
                ch.mark(dve.tensor_scalar(out_bias[:, :], out_bias[:, :], gate, None, ALU.mult))
            if a.rms:
                dve.tensor_scalar(ceiling[:, :], g.mask8, HIGH, MASK_FILL, ALU.mult, ALU.add).then_inc(ceiled, 1)
                dve.wait_ge(ceiled, 1)
                for w in (a.wq, a.wk, a.wv):
                    dve.tensor_scalar(w, w, g.rms_scale[:, 0:1], None, ALU.mult).then_inc(scaled, 1)

            def shift(k, between):
                ch = Chain(dve, shifted, k.n * SHIFT)
                dve.wait_ge(scored, k.n * SB + 1)
                dve.wait_ge(ex_turned, cnt(k.n - 1) * a.blocks)
                if a.rms:
                    e1 = ex_heads(k.two)
                    if between:
                        between()
                    ch.link(dve.tensor_tensor(e1, pS[:, 0, 0:H * S].rearrange("p (h s) -> p h s", h=H),
                                              wide(ceiling[:, span(k.n, S)], H), ALU.min))
                    ch.link(dve.tensor_reduce(nmax[:, k.two, :], e1, AX.X, ALU.max, negate=True))
                    ch.mark(dve.tensor_tensor(e1, e1, nmax[:, k.two, :].unsqueeze(2).broadcast_to([P, H, S]), ALU.add))
                    assert ch.n == SHIFT
                    return
                for j, (h, n) in enumerate(a.banks):
                    dve.wait_ge(scored, k.n * SB + j + 1)
                    ch.mark(dve.tensor_reduce(nmax[:, k.two, h:h + n],
                                              pS[:, j, 0:n * S].rearrange("p (h s) -> p h s", h=n), AX.X, ALU.max,
                                              negate=True))
                if between:
                    between()
                for j, (h, n) in enumerate(a.banks):
                    dve.wait_ge(shifted, k.n * SHIFT + j + 1)
                    ch.mark(dve.tensor_tensor(ex_heads(k.two)[:, h:h + n, :],
                                              pS[:, j, 0:n * S].rearrange("p (h s) -> p h s", h=n),
                                              nmax[:, k.two, h:h + n].unsqueeze(2).broadcast_to([P, n, S]), ALU.add))
                assert ch.n == SHIFT

            def take_q(k):
                ch = Chain(dve, q_steps, k.n * QSTEPS)
                dve.wait_ge(q_made, k.n + 1)
                if a.rope is None:
                    dve.wait_ge(scored, cnt(k.n - 1) * SB)
                    ch.mark(dve.tensor_scalar(qT[:, k.two, :], pQ[:, 0:T], a.bq, None, ALU.add))
                elif a.rope == "tables":
                    dve.wait_ge(scored, cnt(k.n - 1))
                    r1, r2, k1, k2 = rq[:, 0, :], rq[:, 1, :], rk[:, 0, :], rk[:, 1, :]
                    ch.mark(dve.tensor_tensor(r1, pQ[:, 0:T], g.rope_q[:, 0, :], ALU.mult))
                    ch.mark(dve.tensor_tensor(r2, pQ[:, T:2 * T], g.rope_q[:, 1, :], ALU.mult))
                    ch.mark(dve.tensor_tensor(k1, pQ[:, KC:KC + S], g.rope_k[:, 0, :], ALU.mult))
                    ch.link(dve.tensor_tensor(k2, pQ[:, KC + S:KC + 2 * S], g.rope_k[:, 1, :], ALU.mult))
                    ch.mark(dve.tensor_tensor(qT[:, k.two, :], r1, r2, ALU.add))
                    dve.wait_ge(spread, cnt(k.n - 1))
                    ch.mark(dve.tensor_tensor(kT[:, k.two, :], k1, k2, ALU.add))
                else:
                    dve.wait_ge(roped, cnt(k.n - 1) * ROPE)
                    ch.mark(dve.tensor_tensor(biased_q[:, k.two, :], pQ[:, 0:D], a.bq, ALU.add))
                assert ch.n == QSTEPS

            def take_v(k):
                C = a.chunks
                if a.rms:
                    dve.wait_ge(v_spread, cnt(k.n - 1))
                    dve.tensor_scalar(v_one[:, k.two, :], pQ[:, VC:VC + C * W], 1.0, None, ALU.mult).then_inc(v_taken, 1)
                else:
                    dve.wait_ge(weighted, cnt(k.n - 3) * a.blocks)
                    v = pQ[:, VC:VC + C * 3 * W].rearrange("p (c g w) -> p g c w", g=2, w=3 * W)
                    to = vS[:, k.v, :].rearrange("p (g c x) -> p g c x", g=2, x=D)[:, :, :, 0:3 * W]
                    own = g.own_head_of3.unsqueeze(1).broadcast_to([P, 2, PERIOD, 3 * W])
                    dve.tensor_tensor(to, v, own, ALU.mult).then_inc(v_taken, 1)

            def take_results(n):
                ch = Chain(dve, merged, n.n * MERGES)
                dve.wait_ge(y_in[n.v], n.round * (16 * CHOICES) + 16 * CHOICES)
                for c in range(CHOICES):
                    ch.link(dve.scalar_tensor_tensor(tile_of(g.x, n.n), yg[:, n.v, c, :],
                                                     g.weight2[:, c, bass.ds(n.n, 1)], tile_of(g.x, n.n),
                                                     ALU.mult, ALU.add))
                ch.mark(dve.tensor_scalar(g.carrier[:, 0:1], g.carrier[:, 1:2], 0.0, None, ALU.mult))
                ch.link(dve.bn_stats(bn6[:, n.v, :], tile_of(g.x, n.n)))
                ch.mark(dve.tensor_scalar(g.carrier[:, 0:1], g.carrier[:, 1:2], 0.0, None, ALU.mult))
                ch.link(dve.bn_aggr(mv[:, n.v, :], bn6[:, n.v, :]))
                ch.mark(dve.tensor_scalar(spread2[:, n.v:n.v + 1], mv[:, n.v, 1:2], LN_EPS, None, ALU.add))
                assert ch.n == MERGES

            def step(at):
                k, c, e, o = at(K0), at(K0 + 2), at(K0 + 3), at(K0 + 4)

                def add_in():
                    dve.wait_ge(projected, o.n + 1)
                    if a.bo is not None:
                        dve.wait_ge(biased, o.n + 1)
                    add_into_x(dve, g, Chain(dve, added, o.n * ADD_STEPS), pO[:, 0:D], gate, o.n)

                if k:
                    dve.wait_ge(turned, cnt(k.n - 1))
                    if merge:
                        dve.wait_ge(scales, k.n * SCALES + SCALES)
                        dve.tensor_scalar(xn[:, k.two, :], tile_of(g.x, k.n), mv[:, k.v, 0:1], scale[:, k.v:k.v + 1],
                                          ALU.subtract, ALU.mult).then_inc(normed, 1)
                    else:
                        layer_norm(dve, g, xn[:, k.two, :], k.n).then_inc(normed, 1)
                    if a.rms:
                        dve.wait_ge(ctx_in[k.v], k.round * 16 + 16)
                        dve.wait_ge(ctx_turned, cnt(k.n - 1))
                        dve.tensor_scalar(ctxn[:, k.two, :], ctxr[:, k.v, :], g.ctx_rstd[:, bass.ds(k.n, 1)], None,
                                          ALU.mult).then_inc(ctx_normed, 1)
                if e:
                    dve.wait_ge(exped, e.n + 1)
                    dve.wait_ge(spread_over, cnt(e.n - 1))
                    dve.tensor_reduce(total[:, e.two, :], ex_heads(e.two), AX.X, ALU.add).then_inc(summed, 1)
                    dve.wait_ge(summed, e.n * 2 + 1)
                    dve.reciprocal(over[:, e.two, :], total[:, e.two, :]).then_inc(summed, 1)
                if c:
                    shift(c, add_in if o else None)
                elif o:
                    add_in()
                if merge and (n := at(MERGE)):
                    take_results(n)
                if merge and (n := at(PLACE)):
                    dve.wait_ge(merged, cnt(n.n - 3) * MERGES)
                    dve.tensor_scalar(where[:, n.v, :], tile_of(g.slots2, n.n), 1.0, None, ALU.mult).then_inc(placed, 1)
                if k:
                    take_q(k)
                    take_v(k)
                if e:
                    dve.wait_ge(weighted, e.n * a.blocks + a.blocks)
                    dve.wait_ge(over_copied, e.n + 1)
                    dve.wait_ge(projected, cnt(e.n - 1))
                    dve.tensor_tensor(oT[:, e.two, :], pO[:, 0:T], overT[:, e.two, :], ALU.mult).then_inc(divided, 1)
            pipeline(dve, NT, LAST, 4, step)


def wide(ap, heads):
    return ap.unsqueeze(1).broadcast_to([ap.shape[0], heads, ap.shape[1]])


def heads_mask(g, a):
    return g.head_mask[a.heads].unsqueeze(2).broadcast_to([P, a.heads, S])


def tile_rows(ap, n):
    return ap[bass.ds(n, 1), :, :].rearrange("a p s -> p (a s)")


def ctx_rms(nc, g):
    with ExitStack() as ctx:
        m = Memory(nc, ctx, "cr")
        a, b = m.sb("a", [S, NT]), m.sb("b", [S, NT])
        shifted, rooted = m.sem("shifted"), m.sem("rooted")
        block = ctx.enter_context(nc.Block())

        @block.vector
        def _(dve):
            dve.wait_ge(g.weights_in["L2a"], 16 * len(g.loads["L2a"]))
            ch = Chain(dve, shifted)
            ch.mark(dve.tensor_scalar(a[:, :], g.ctx_sum2[:, :], 1.0 / D, 1e-6, ALU.mult, ALU.add))
            ch.mark(dve.tensor_scalar(g.rms_scale[:, :], g.rms_scale[:, :], 1.0, None, ALU.add))
            dve.wait_ge(rooted, 1)
            ch.mark(dve.reciprocal(g.ctx_rstd[:, :], b[:, :]))

        @block.scalar
        def _(act):
            act.wait_ge(shifted, 1)
            act.activation(b[:, :], a[:, :], ACT.Sqrt).then_inc(rooted, 1)


ROPE_BASE = 10000.0
TWO_PI = (6.28125, 0.0019350051879882812, 3.0199159819e-07)
NEAREST = 12582912.0
HALF_PI = 1.5707963267948966


def rope_angles(nc, g):
    F = 4
    with ExitStack() as ctx:
        m = Memory(nc, ctx, "ra")
        pos = m.sb("posf", [P, NT])
        ang, turns, low = m.sb("ang", [P, NT, F]), m.sb("turns", [P, NT, F]), m.sb("low", [P, NT, F])
        steps, waved = m.sem("steps"), m.sem("waved")
        READY = 11
        block = ctx.enter_context(nc.Block())

        @block.vector
        def _(dve):
            dve.wait_ge(g.weights_in["L3a"], 16 * len(g.loads["L3a"]))
            ch = Chain(dve, steps)
            ch.link(dve.tensor_scalar(pos[:, :], g.pos[:, :], 1.0, None, ALU.mult))
            for f in range(F):
                inverse = float(np.float32(1.0) / np.float32(ROPE_BASE) ** np.float32(2 * f / (2 * F)))
                last = dve.tensor_scalar(ang[:, :, f], pos[:, :], inverse, None, ALU.mult)
                (ch.mark if f < F - 1 else ch.link)(last)
            ch.link(dve.tensor_scalar(turns[:, :, :], ang[:, :, :], 1.0 / (2 * np.pi), NEAREST, ALU.mult, ALU.add))
            ch.link(dve.tensor_scalar(turns[:, :, :], turns[:, :, :], -NEAREST, None, ALU.add))
            for part in TWO_PI:
                ch.link(dve.scalar_tensor_tensor(ang[:, :, :], turns[:, :, :], -part, ang[:, :, :], ALU.mult, ALU.add))
            ch.link(dve.tensor_scalar(ang[:, :, :], ang[:, :, :], 3.1415925, -3.1415925, ALU.min, ALU.max))
            ch.link(dve.scalar_tensor_tensor(low[:, :, :], ang[:, :, :], -1.0, ang[:, :, :], ALU.mult, ALU.min))
            ch.mark(dve.tensor_scalar(low[:, :, :], low[:, :, :], HALF_PI, None, ALU.add))
            assert ch.n == READY + 2
            dve.wait_ge(waved, 2)
            ch.mark(dve.tensor_scalar(g.sin_q[:, :, 0:F], g.sin_q[:, :, F:2 * F], -1.0, None, ALU.mult))

        @block.scalar
        def _(act):
            act.wait_ge(steps, READY + 2)
            act.activation(g.sin_q[:, :, F:2 * F], ang[:, :, :], ACT.Sin).then_inc(waved, 1)
            act.activation(g.cos_q[:, :, :], low[:, :, :], ACT.Sin).then_inc(waved, 1)


class Mixture:

    def __init__(self, name, kind, choices, tiles, row, hidden, load, gate, wg, bg, w_up, w_down, b_up=None,
                 b_down=None):
        self.name, self.kind, self.choices, self.tiles, self.row = name, kind, choices, tiles, row
        self.hidden, self.load, self.gate = hidden, load, gate
        self.wg, self.bg, self.w_up, self.w_down, self.b_up, self.b_down = wg, bg, w_up, w_down, b_up, b_down
        gelu = kind == "logits_first"
        self.PLACE, self.GATHER, self.TURN, self.X_COPY, self.UP = 0, 1, 3, 4, 5
        self.BIAS = self.UP + 1
        self.ACTIVATE = self.BIAS + 1 if gelu else self.UP + 1
        self.GATES, self.H_TURN, self.H_COPY, self.DOWN, self.SUM, self.STORE = (
            self.ACTIVATE + i for i in range(1, 7))
        self.asking = ((self.UP, self.DOWN), (self.BIAS, self.SUM))
        self.rounds = (tiles + self.STORE) // 4 + 1


CHOICES = 2
TOP2_TILES = -(-(CHOICES * NT + E - 1) // 4) * 4
CAPACITY = B * T // E
CHOSEN_TILES = B * T // P
NOWHERE = 60000.0


def moe_front(nc, g, mix, rows, logits):
    TILES = 4
    UNITS = NT // TILES
    with ExitStack() as ctx:
        m = Memory(nc, ctx, mix.name + "f")
        xn = m.sb("xn", [P, 2, TILES, D])
        xT = m.sb("xT", [P, 2, TILES * T])
        pT, pG = ([m.ps(f"{k}{i}") for i in range(2)] for k in ("pT", "pG"))
        stored = [m.sem(f"stored{i}") for i in range(2)]
        normed, turned, copied, scored, biased = (m.sem(k) for k in ("normed", "turned", "copied", "scored", "biased"))
        block = ctx.enter_context(nc.Block())

        @block.vector
        def _(dve):
            for name in ("moe", mix.load):
                dve.wait_ge(g.weights_in[name], 16 * len(g.loads[name]))
            if mix.kind != "experts_choose":
                dve.tensor_scalar(g.before[:, :], g.before_f[:, :], 1.0, None, ALU.mult)

            def step(at):
                if k := at(0):
                    dve.wait_ge(stored[k.v], k.round * 16)
                    dve.wait_ge(turned, cnt(k.n - 1))
                    for t in range(TILES):
                        layer_norm(dve, g, xn[:, k.v, t, :], k.n * TILES + t).then_inc(normed, 1)
                if k := at(2):
                    dve.wait_ge(scored, k.n + 1)
                    dve.tensor_tensor(logits[:, bass.ds(k.n * TILES, TILES), :],
                                      pG[k.v][:, 0:TILES * E].rearrange("p (t e) -> p t e", e=E),
                                      mix.bg.unsqueeze(1).broadcast_to([P, TILES, E]), ALU.add).then_inc(biased, 1)
            pipeline(dve, UNITS, 2, 2, step)

        @block.tensor
        def _(pe):
            for name in ("moe", mix.load):
                pe.wait_ge(g.weights_in[name], 16 * len(g.loads[name]))

            def step(at):
                if k := at(1):
                    pe.wait_ge(copied, k.n + 1)
                    pe.wait_ge(biased, cnt(k.n - 1))
                    for t in range(TILES):
                        mm = pe.matmul(pG[k.v][:, t * E:(t + 1) * E], xT[:, k.v, t * T:(t + 1) * T], mix.wg, start=True,
                                       stop=True)
                    mm.then_inc(scored, 1)
                if k := at(0):
                    pe.wait_ge(normed, k.n * TILES + TILES)
                    pe.wait_ge(copied, cnt(k.n - 1))
                    for t in range(TILES):
                        tr = pe.transpose(pT[k.v][:, t * T:(t + 1) * T], xn[:, k.v, t, :], g.ident[:, :])
                    tr.then_inc(turned, 1)
            pipeline(pe, UNITS, 2, 2, step)

        @block.scalar
        def _(act):
            def step(at):
                if k := at(0):
                    act.wait_ge(turned, k.n + 1)
                    act.wait_ge(scored, cnt(k.n - 1))
                    act.copy(xT[:, k.v, :], pT[k.v][:, 0:TILES * T]).then_inc(copied, 1)
            pipeline(act, UNITS, 2, 2, step)

        @block.sync
        def _(sp):
            def step(at):
                if k := at(0):
                    sp.wait_ge(normed, k.n * TILES + TILES)
                    sp.dma_start(rows[bass.ds(k.n * (TILES * P), TILES * P), 0:D].rearrange("(t p) d -> p t d", p=P),
                                 xn[:, k.v, :, :]).then_inc(stored[k.v], 16)
            pipeline(sp, UNITS, 2, 2, step)
            for i in range(2):
                sp.wait_ge(stored[i], 16 * UNITS // 2)


def each_expert(ap):
    return ap.unsqueeze(2).broadcast_to([P, NT, E])


def each_tile(ap):
    return ap.unsqueeze(1).broadcast_to([P, NT, E])


def route_top2(nc, g, mix, logits, slots, weight, packed, parity):
    with ExitStack() as ctx:
        m = Memory(nc, ctx, mix.name + "r")
        sc, t1, t2 = m.sb("sc", [P, NT, E]), m.sb("t1", [P, NT, E]), m.sb("t2", [P, NT, E])
        one = [m.sb(f"one{c}", [P, NT, E]) for c in range(CHOICES)]
        value = [m.sb(f"value{c}", [P, NT]) for c in range(CHOICES)]
        row = m.sb("row", [P, NT])
        chosen = m.sb("chosen", [P, NT, E], BF16)
        inc = m.sb("inc", [P, NT, E])
        tiles_i, tiles_f, base = m.sb("tiles_i", [P, E], I32), m.sb("tiles_f", [P, E]), m.sb("base", [P, E])
        past = m.sb("past", [P, mix.tiles, E - 1])
        MARGIN = mix.STORE
        lined = m.sb("lined", [P, MARGIN + 4 * mix.rounds + MARGIN])
        sum8 = m.sb("sum8", [P, 2, mix.rounds])
        expert_f, expert_i = m.sb("expert_f", [P, mix.tiles]), m.sb("expert_i", [P, mix.tiles], I32)
        pP, pT = m.ps("pP"), m.ps("pT")
        steps, exped, prefixed = m.sem("steps"), m.sem("exped"), m.sem("prefixed")
        marks = {}
        block = ctx.enter_context(nc.Block())

        @block.vector
        def _(dve):
            ch = Chain(dve, steps)
            for t in (lined, sum8):
                ch.link(dve.memset(t[:], 0.0))

            def note(name):
                marks[name] = ch.n

            if mix.kind == "softmax_first":
                ch.link(dve.tensor_reduce(row[:, :], logits[:, :, :], AX.X, ALU.max, negate=True))
                ch.link(dve.tensor_tensor(sc[:, :, :], logits[:, :, :], each_expert(row[:, :]), ALU.add))
                note("shifted")
                dve.wait_ge(exped, 1)
                ch.link(dve.tensor_reduce(row[:, :], sc[:, :, :], AX.X, ALU.add))
                ch.link(dve.reciprocal(row[:, :], row[:, :]))
                ch.link(dve.tensor_tensor(sc[:, :, :], sc[:, :, :], each_expert(row[:, :]), ALU.mult))
            else:
                ch.link(dve.tensor_scalar(sc[:, :, :], logits[:, :, :], 1.0, None, ALU.mult))
            for c in range(CHOICES):
                ch.link(dve.tensor_reduce(value[c][:, :], sc[:, :, :], AX.X, ALU.max))
                ch.link(dve.tensor_tensor(t1[:, :, :], sc[:, :, :], each_expert(value[c][:, :]), ALU.is_equal))
                ch.link(dve.tensor_tensor(t1[:, :, :], t1[:, :, :], each_tile(g.down[:, :]), ALU.mult))
                ch.link(dve.tensor_reduce(row[:, :], t1[:, :, :], AX.X, ALU.max))
                ch.link(dve.tensor_tensor(one[c][:, :, :], t1[:, :, :], each_expert(row[:, :]), ALU.is_equal))
                if c < CHOICES - 1:
                    ch.link(dve.scalar_tensor_tensor(sc[:, :, :], one[c][:, :, :], -3.0e38, sc[:, :, :], ALU.mult,
                                                     ALU.add))
            ch.link(dve.tensor_tensor(chosen[:, :, :], one[0][:, :, :], one[1][:, :, :], ALU.add))
            note("chosen")
            if mix.kind == "softmax_first":
                for c in range(CHOICES):
                    ch.mark(dve.tensor_scalar(weight[:, c, :], value[c][:, :], g.tanh_gate[:, mix.gate:mix.gate + 1],
                                              None, ALU.mult))
            else:
                ch.link(dve.tensor_tensor(value[1][:, :], value[1][:, :], value[0][:, :], ALU.subtract))
                note("shifted")
                dve.wait_ge(exped, 1)
                ch.link(dve.tensor_scalar(row[:, :], value[1][:, :], 1.0, None, ALU.add))
                ch.link(dve.reciprocal(row[:, :], row[:, :]))
                ch.link(dve.tensor_scalar(weight[:, 0, :], row[:, :], g.tanh_gate[:, mix.gate:mix.gate + 1], None,
                                          ALU.mult))
                ch.link(dve.tensor_tensor(weight[:, 1, :], weight[:, 0, :], value[1][:, :], ALU.mult))
            dve.wait_ge(prefixed, 1)
            ch.link(dve.tensor_scalar(t2[:, :, :], pT[:, 0:NT * E].rearrange("p (n e) -> p n e", e=E), 1.0, None,
                                      ALU.mult))
            for e in range(E):
                scan = dve.tensor_tensor_scan(inc[:, :, e], g.ones[:, 0:NT], t2[:, :, e], 0.0, ALU.mult, ALU.add)
                (ch.mark if e < E - 1 else ch.link)(scan)
            ch.link(dve.tensor_scalar(tiles_i[:, :], inc[:, NT - 1, :], float(P - 1), None, ALU.add))
            ch.link(dve.tensor_scalar(tiles_i[:, :], tiles_i[:, :], 7, None, ALU.logical_shift_right))
            ch.link(dve.tensor_scalar(tiles_f[:, :], tiles_i[:, :], 1.0, None, ALU.mult))
            ch.link(dve.tensor_tensor_scan(base[:, :], g.ones[:, 0:E], tiles_f[:, :], 0.0, ALU.mult, ALU.add))
            ch.link(dve.tensor_tensor(past[:, :, :], g.up[:, 0:mix.tiles].unsqueeze(2).broadcast_to([P, mix.tiles, E - 1]),
                                      base[:, 0:E - 1].unsqueeze(1).broadcast_to([P, mix.tiles, E - 1]), ALU.is_ge))
            ch.link(dve.tensor_tensor(base[:, :], base[:, :], tiles_f[:, :], ALU.subtract))
            ch.link(dve.tensor_reduce(expert_f[:, :], past[:, :, :], AX.X, ALU.add))
            ch.link(dve.tensor_scalar(lined[:, MARGIN:MARGIN + mix.tiles], expert_f[:, :], 1.0, None, ALU.mult))
            for which, lags in enumerate(mix.asking):
                for n, (u, lag) in enumerate((u, lag) for lag in lags for u in range(4)):
                    start = MARGIN + u - lag
                    asked = lined[:, start:start + 4 * mix.rounds].rearrange("p (r f) -> p r f", f=4)[:, :, 0]
                    ch.link(dve.scalar_tensor_tensor(sum8[:, which, :], asked, float(E ** n), sum8[:, which, :],
                                                     ALU.mult, ALU.add))
            ch.mark(dve.tensor_scalar(packed[:, :, :], sum8[:, :, :], 1.0, None, ALU.mult))
            ch.link(dve.tensor_scalar(expert_i[:, :], expert_f[:, :], 1.0, None, ALU.mult))
            ch.link(dve.tensor_scalar(expert_i[:, :], expert_i[:, :], 1, None, ALU.bitwise_and))
            ch.link(dve.tensor_scalar(parity[:, 1, :], expert_i[:, :], 0.5, None, ALU.mult))
            ch.mark(dve.tensor_scalar(parity[:, 0, :], parity[:, 1, :], -2.0, 1.0, ALU.mult, ALU.add))
            ch.link(dve.tensor_scalar(base[:, :], base[:, :], float(P), None, ALU.mult))
            ch.link(dve.tensor_tensor(inc[:, :, :], inc[:, :, :], t2[:, :, :], ALU.subtract))
            ch.link(dve.tensor_tensor(inc[:, :, :], inc[:, :, :], each_tile(base[:, :]), ALU.add))
            ch.link(dve.tensor_tensor(inc[:, :, :], inc[:, :, :], pP[:, 0:NT * E].rearrange("p (n e) -> p n e", e=E),
                                      ALU.add))
            for c in range(CHOICES):
                ch.link(dve.tensor_tensor(t1[:, :, :], inc[:, :, :], one[c][:, :, :], ALU.mult))
                ch.link(dve.tensor_reduce(slots[:, :, c], t1[:, :, :], AX.X, ALU.add))

        @block.scalar
        def _(act):
            act.wait_ge(steps, marks["shifted"])
            v = sc[:, :, :] if mix.kind == "softmax_first" else value[1][:, :]
            act.activation(v, v, ACT.Exp).then_inc(exped, 1)

        @block.tensor
        def _(pe):
            pe.wait_ge(steps, marks["chosen"])
            flat = chosen[:, :, :].rearrange("p n e -> p (n e)")
            pe.matmul(pP[:, 0:NT * E], g.before[:, :], flat, start=True, stop=True)
            pe.matmul(pT[:, 0:NT * E], g.ones16[:, :], flat, start=True, stop=True).then_inc(prefixed, 1)


def build_index(nc, g, mix, slots, index):
    C, N = mix.choices, mix.tiles
    own = mix.kind == "experts_choose"
    reach = N // E if own else N
    with ExitStack() as ctx:
        m = Memory(nc, ctx, mix.name + "i")
        whole, low = m.sb("whole", [P, NT, C], I32), m.sb("low", [P, NT, C], I32)
        col, tile = m.sb("col", [P, NT, C]), m.sb("tile", [P, NT, C])
        columns, value = m.sb("columns", [P, 2, C, P], F16), m.sb("value", [P, 2, C, reach], F16)
        if own:
            values = m.sb("values", [P, NT, N], F16)
        zero = m.sb("zero", [P, P], F16)
        pI = m.ps("pI")
        steps, made, placed, cleared = (m.sem(k) for k in ("steps", "made", "placed", "cleared"))
        K = 1 if own else 2 * C
        block = ctx.enter_context(nc.Block())
        up = g.up16[:, 0:N].rearrange("p (c t) -> p c t", c=C) if own else \
            g.up16[:, 0:N].unsqueeze(1).broadcast_to([P, C, N])

        @block.gpsimd
        def _(pool):
            pool.memset(zero[:, :], 0.0).then_inc(cleared, 1)

        @block.vector
        def _(dve):
            ch = Chain(dve, steps)
            ch.link(dve.tensor_scalar(whole[:, :, :], slots[:, :, 0:C], 1.0, None, ALU.mult))
            ch.mark(dve.tensor_scalar(low[:, :, :], whole[:, :, :], P - 1, None, ALU.bitwise_and))
            ch.link(dve.tensor_scalar(whole[:, :, :], whole[:, :, :], 7, None, ALU.logical_shift_right))
            ch.mark(dve.tensor_scalar(col[:, :, :], low[:, :, :], 1.0, None, ALU.mult))
            ch.link(dve.tensor_scalar(tile[:, :, :], whole[:, :, :], 1.0, None, ALU.mult))

            if own:
                ch.link(dve.tensor_tensor(values[:, :, :].rearrange("p n (c t) -> p n c t", t=reach),
                                          up.unsqueeze(1).broadcast_to([P, NT, C, reach]),
                                          tile[:, :, :].unsqueeze(3).broadcast_to([P, NT, C, reach]), ALU.is_equal))
                ch.link(dve.tensor_tensor(values[:, :, :], values[:, :, :],
                                          g.token[:, :].unsqueeze(2).broadcast_to([P, NT, N]), ALU.mult))

            def step(at):
                k = at(0)
                ch = Chain(dve, made, k.n * K)
                dve.wait_ge(placed, cnt(k.n - 1))
                c1, t1 = tile_of(col, k.n), tile_of(tile, k.n)
                if own:
                    ch.mark(dve.tensor_tensor(columns[:, k.two, :, :], g.up16[:, 0:P].unsqueeze(1).broadcast_to([P, C, P]),
                                              c1.unsqueeze(2).broadcast_to([P, C, P]), ALU.is_equal))
                    return
                for c in range(C):
                    ch.mark(dve.tensor_scalar(columns[:, k.two, c, :], g.up16[:, 0:P], c1[:, c:c + 1], None,
                                              ALU.is_equal))
                    ch.mark(dve.tensor_scalar(value[:, k.two, c, :], up[:, c, :], t1[:, c:c + 1],
                                              g.token[:, bass.ds(k.n, 1)], ALU.is_equal, ALU.mult))
            pipeline(dve, NT, 0, 4, step)
            dve.wait_ge(placed, NT)
            ch.link(dve.tensor_scalar(index[:, 0:N], pI[:, 0:N], float(B * T // 2), None, ALU.add))

        @block.tensor
        def _(pe):
            pe.wait_ge(cleared, 1)
            pe.matmul(pI[:, 0:N], zero[:, :], zero[:, 0:N], start=True, stop=True)

            def step(at):
                k = at(0)
                pe.wait_ge(made, k.n * K + K)
                for c in range(C):
                    to = slice(c * reach, (c + 1) * reach) if own else slice(0, N)
                    of = tile_of(values, k.n)[:, to] if own else value[:, k.two, c, :]
                    mm = pe.matmul(pI[:, to], columns[:, k.two, c, :], of, start=False, stop=True,
                                   skip_group_check=True)
                mm.then_inc(placed, 1)
            pipeline(pe, NT, 0, 4, step)


def rounds(eng, n, step, unroll=4):
    for i in range(n % unroll):
        step(i)
    with eng.Fori(0, n // unroll) as r:
        for u in range(unroll):
            step(r * unroll + (n % unroll + u))


def choose_tokens(nc, g, mix, logits, slots, weight, rows):
    H2, R2 = 2, NT // 2
    with ExitStack() as ctx:
        m = Memory(nc, ctx, mix.name + "c")
        bits, flt = m.sb("bits", [P, H2, P], I32), m.sb("flt", [P, H2, P])
        part = [m.sb(f"part{i}", [P, H2, P], I32) for i in range(2)]
        sign, high, low = m.sb("sign", [P, H2, P]), m.sb("high", [P, H2, P]), m.sb("low", [P, H2, P])
        key, junk = m.sb("key", [P, H2, P]), m.sb("junk", [P, 3, H2 * P])
        above, equal, run = m.sb("above", [P, H2, P]), m.sb("equal", [P, H2, P]), m.sb("run", [P, H2, P])
        least, gain = m.sb("least", [P, 1]), m.sb("gain", [P, 1])
        width = m.sb("width", [P, 2])
        cand, count, met = (m.sb(k, [P, 3]) for k in ("cand", "count", "met"))
        need, offset = m.sb("need", [P, 1]), m.sb("offset", [P, H2])
        sel, shift = m.sb("sel", [P, NT, E]), m.sb("shift", [P, NT, E])
        best, best8, diag = m.sb("best", [P, E]), m.sb("best8", [E, 1]), m.sb("diag", [E, E])
        sums, share = m.sb("sums", [P, E]), m.sb("share", [P, E])
        pL, pC, pM, pW = (m.ps(k) for k in ("pL", "pC", "pM", "pW"))
        steps, counted, exped, stored = (m.sem(k) for k in ("steps", "counted", "exped", "stored"))
        LOOP = 7
        marks, products = {}, {}
        block = ctx.enter_context(nc.Block())
        flat = lambda t: t[:, :, :].rearrange("p h t -> p (h t)")
        by_expert = lambda t: t[:, :, :].rearrange("p n e -> p e n")

        @block.vector
        def _(dve):
            dve.wait_ge(g.weights_in["L3c"], 16 * len(g.loads["L3c"]))
            ch = Chain(dve, steps)
            seen = [0]

            def product(name, instruction=None):
                marks[name] = ch.n
                seen[0] += 1
                products[name] = seen[0]
                dve.wait_ge(counted, seen[0])

            ch.link(dve.tensor_reduce(best[:, :], by_expert(logits), AX.X, ALU.max))
            product("turned")
            ch.mark(dve.tensor_reduce(best8[:, :], pM[0:E, 0:P], AX.X, ALU.max))
            dve.wait_ge(steps, ch.n)
            ch.link(dve.tensor_scalar(diag[:, :], g.ident[0:E, 0:E], best8[:, :], None, ALU.mult))
            product("best")
            ch.link(dve.tensor_tensor(shift[:, :, :], logits[:, :, :], each_tile(pM[:, 0:E]), ALU.subtract))
            marks["shifted"] = ch.n
            ch.link(dve.tensor_scalar(flat(flt), pL[:, 0:H2 * P], 1.0, None, ALU.mult))
            ch.link(dve.tensor_scalar(flat(bits), flat(flt).bitcast(I32), 0x7fffffff, None, ALU.bitwise_and))
            ch.mark(dve.tensor_scalar(flat(part[0]), flat(bits), 16, None, ALU.logical_shift_right))
            ch.mark(dve.tensor_scalar(flat(part[1]), flat(bits), 0xffff, None, ALU.bitwise_and))
            ch.link(dve.tensor_scalar(flat(sign), flat(flt), 0.0, -2.0, ALU.is_lt, ALU.mult))
            ch.link(dve.tensor_scalar(flat(sign), flat(sign), 1.0, None, ALU.add))
            ch.mark(dve.tensor_tensor(flat(high), flat(part[0]), flat(sign), ALU.mult))
            ch.link(dve.tensor_tensor(flat(low), flat(part[1]), flat(sign), ALU.mult))

            def search(source, quarterings, name):
                ch.mark(dve.memset(least[:, :], -2.0 * 4 ** (quarterings - 1)))
                for t in range(2):
                    ch.mark(dve.memset(width[:, t:t + 1], 1.0 * 4 ** (quarterings - t)))
                ch.link(dve.tensor_scalar(cand[:, :], g.up[:, 1:4], 1.0 * 4 ** (quarterings - 1),
                                          -2.0 * 4 ** (quarterings - 1), ALU.mult, ALU.add))
                marks[name], n0, first = ch.n, ch.n, seen[0]

                def quarter(i):
                    def at_step(s):
                        dve.wait_ge(steps, i * LOOP + (n0 + s))
                    for t in range(3):
                        dve.tensor_scalar(junk[:, t, :], source, cand[:, t:t + 1], None, ALU.is_ge, ALU.add,
                                          accum_out=count[:, t:t + 1]).then_inc(steps, 1)
                    dve.tensor_scalar(width[:, :], width[:, :], 0.25, None, ALU.mult).then_inc(steps, 1)
                    dve.wait_ge(counted, i + (first + 1))
                    dve.tensor_scalar(met[:, :], pC[:, 0:3], CAPACITY - 0.5, None, ALU.is_ge, ALU.add,
                                      accum_out=gain[:, :]).then_inc(steps, 1)
                    at_step(5)
                    dve.scalar_tensor_tensor(least[:, :], gain[:, :], width[:, 0:1], least[:, :], ALU.mult, ALU.add
                                             ).then_inc(steps, 1)
                    at_step(6)
                    dve.tensor_scalar(cand[:, :], g.up[:, 1:4], width[:, 1:2], least[:, :], ALU.mult, ALU.add
                                      ).then_inc(steps, 1)
                    at_step(7)

                rounds(dve, quarterings, quarter)
                ch.n += quarterings * LOOP
                seen[0] += quarterings

            search(flat(high), 8, "high")
            ch.link(dve.tensor_scalar(flat(key), flat(high), least[:, :], float(2 ** 17), ALU.subtract, ALU.mult))
            ch.link(dve.tensor_tensor(flat(key), flat(key), flat(low), ALU.add))
            search(flat(key), 9, "both")
            ch.mark(dve.tensor_scalar(flat(above), flat(key), least[:, :], None, ALU.is_gt, ALU.add,
                                      accum_out=count[:, 0:1]))
            ch.link(dve.tensor_scalar(flat(equal), flat(key), least[:, :], None, ALU.is_equal))
            product("above")
            ch.link(dve.tensor_scalar(need[:, :], pC[:, 0:1], -1.0, float(CAPACITY), ALU.mult, ALU.add))

            def rank(source, name):
                for h in range(H2):
                    (ch.mark if h < H2 - 1 else ch.link)(dve.tensor_tensor_scan(
                        run[:, h, :], g.ones[:, 0:P], source[:, h, :], 0.0, ALU.mult, ALU.add))
                product(name)
                ch.link(dve.tensor_scalar(offset[:, :], pC[:, 0:H2], 1.0, None, ALU.mult))
                ch.link(dve.tensor_tensor(run[:, :, :], run[:, :, :], source[:, :, :], ALU.subtract))
                for h in range(H2):
                    (ch.mark if h < H2 - 1 else ch.link)(dve.tensor_scalar(
                        run[:, h, :], run[:, h, :], offset[:, h:h + 1], None, ALU.add))

            rank(equal, "ties")
            ch.link(dve.scalar_tensor_tensor(flat(equal), flat(run), need[:, :], flat(equal), ALU.is_lt, ALU.mult))
            ch.link(dve.tensor_tensor(flat(above), flat(above), flat(equal), ALU.add))
            rank(above, "ranks")
            ch.link(dve.tensor_scalar(flat(run), flat(run), g.row_base[:, 0:1], -NOWHERE, ALU.add, ALU.add))
            ch.link(dve.tensor_tensor(flat(run), flat(run), flat(above), ALU.mult))
            ch.link(dve.tensor_scalar(flat(run), flat(run), NOWHERE, None, ALU.add))
            product("slots")
            ch.link(dve.tensor_scalar(slots[:, :, :].rearrange("p n e -> p (n e)"), pL[:, 0:NT * E], 1.0, None,
                                      ALU.mult))
            ch.link(dve.tensor_scalar(sel[:, :, :], slots[:, :, :], NOWHERE, None, ALU.is_lt))
            dve.wait_ge(exped, 1)
            ch.link(dve.tensor_tensor(shift[:, :, :], shift[:, :, :], sel[:, :, :], ALU.mult))
            ch.link(dve.tensor_reduce(sums[:, :], by_expert(shift), AX.X, ALU.add))
            product("sums")
            ch.link(dve.reciprocal(share[:, :], pW[:, 0:E]))
            ch.link(dve.tensor_scalar(share[:, :], share[:, :], g.tanh_gate[:, mix.gate:mix.gate + 1], None, ALU.mult))
            ch.mark(dve.tensor_tensor(weight[:, :, :], shift[:, :, :], each_tile(share[:, :]), ALU.mult))
            marks["weights"] = ch.n

        @block.scalar
        def _(act):
            act.wait_ge(steps, marks["shifted"])
            act.activation(shift[:, :, :], shift[:, :, :], ACT.Exp).then_inc(exped, 1)

        @block.tensor
        def _(pe):
            pe.wait_ge(g.weights_in["L3c"], 16 * len(g.loads["L3c"]))
            count_done = [0]

            def after(name):
                count_done[0] += 1
                assert products[name] == count_done[0]
                pe.wait_ge(steps, marks[name])

            after("turned")
            for h in range(H2):
                pe.transpose(pL[:, h * P:(h + 1) * P], logits[:, h * R2:(h + 1) * R2, :].rearrange("p n e -> p (n e)"),
                             g.ident[:, :])
            pe.transpose(pM[0:E, 0:P], best[:, :], g.ident[:, :]).then_inc(counted, 1)
            after("best")
            pe.matmul(pM[:, 0:E], g.ones[0:E, :], diag[:, :], start=True, stop=True).then_inc(counted, 1)
            for name, quarterings in (("high", 8), ("both", 9)):
                def quarter(i, name=name):
                    pe.wait_ge(steps, i * LOOP + (marks[name] + 3))
                    pe.matmul(pC[:, 0:3], g.same_expert, count[:, :], start=True, stop=True).then_inc(counted, 1)

                rounds(pe, quarterings, quarter)
                count_done[0] += quarterings
            after("above")
            pe.matmul(pC[:, 0:1], g.same_expert, count[:, 0:1], start=True, stop=True).then_inc(counted, 1)
            for name in ("ties", "ranks"):
                after(name)
                last = [run[:, h, P - 1:P] for h in range(H2)]
                pe.matmul(pC[:, 0:1], g.earlier_row, last[0], start=True, stop=True)
                pe.matmul(pC[:, 1:2], g.same_expert, last[0], start=True, stop=False)
                pe.matmul(pC[:, 1:2], g.earlier_row, last[1], start=False, stop=True).then_inc(counted, 1)
            after("slots")
            for h in range(H2):
                t = pe.transpose(pL[:, h * P:(h + 1) * P], run[:, h, :], g.ident[:, :])
            t.then_inc(counted, 1)
            after("sums")
            pe.matmul(pW[:, 0:E], g.ones[:, :], sums[:, :], start=True, stop=True).then_inc(counted, 1)

        @block.sync
        def _(sp):
            sp.wait_ge(steps, marks["weights"])
            sp.dma_start(rows[:, D:D + E].rearrange("(n p) e -> p n e", p=P), weight[:, :, :]).then_inc(stored, 16)
            sp.wait_ge(stored, 16)


def run_experts(nc, g, mix, rows, index, packed, parity, results):
    N, R, FH = mix.tiles, mix.row, mix.hidden
    HC = FH // P
    gelu, chosen = mix.kind == "logits_first", mix.kind == "experts_choose"
    with ExitStack() as ctx:
        m = Memory(nc, ctx, mix.name + "e")
        where = m.sb("where", [P, 4], U32)
        xg, xT = m.sb("xg", [P, 4, R]), m.sb("xT", [P, 2, P])
        first, gated = m.sb("first", [P, 2, FH]), m.sb("gated", [P, 2, FH])
        hT, y = m.sb("hT", [P, 2, FH]), m.sb("y", [P, 4, D])
        scratch = m.sb("scratch", [1, 4], I32)
        carried = [m.sem(f"carried{i}") for i in range(2)]
        pX, pU, pH, pY = ([m.ps(f"{k}{i}") for i in range(2)] for k in ("pX", "pU", "pH", "pY"))
        xg_in, y_out = ([m.sem(f"{k}{i}") for i in range(4)] for k in ("xg_in", "y_out"))
        (cleared, placed, turned, x_copied, upped, biased, acted, gates, h_turned, h_copied, downed, y_made, halved,
         x_stored) = (
            m.sem(k) for k in ("cleared", "placed", "turned", "x_copied", "upped", "biased", "acted", "gates",
                               "h_turned", "h_copied", "downed", "y_made", "halved", "x_stored"))
        if gelu:
            hid, tanh_h, halves = m.sb("hid", [P, 2, FH]), m.sb("tanh_h", [P, 2, FH]), m.sb("halves", [P, 2, FH])
        if chosen:
            to, share, noted = m.sb("to", [P, 4], U32), m.sb("share", [P, N]), m.sem("noted")
        ACTS, GATE, YS = (2, 2, 1) if gelu else (1, 1, 2) if chosen else (1, 1, 1)
        PLACE, GATHER, TURN, X_COPY, UP, BIAS = mix.PLACE, mix.GATHER, mix.TURN, mix.X_COPY, mix.UP, mix.BIAS
        ACTIVATE, GATES, H_TURN, H_COPY = mix.ACTIVATE, mix.GATES, mix.H_TURN, mix.H_COPY
        DOWN, SUM, STORE = mix.DOWN, mix.SUM, mix.STORE
        read_up = biased if gelu else gates
        block = ctx.enter_context(nc.Block())

        class Experts:

            def __init__(self, eng, which):
                self.eng, self.which = eng, which

            def begin(self, i):
                if not chosen:
                    self.packed = self.eng.value_load(packed[0:1, self.which, bass.ds(i, 1)], min_val=0,
                                                      max_val=E ** 8 - 1)

            def of(self, k, stage):
                if chosen:
                    return k.round
                lag = mix.asking[self.which][stage]
                return (self.packed >> 3 * (4 * stage + k.w + lag)) & (E - 1)

        @block.gpsimd
        def _(pool):
            pool.memset(scratch[:, :], 0).then_inc(cleared, 1)
            pool.wait_ge(cleared, 1)
            if chosen:
                pool.wait_ge(x_stored, 16)

            def step(at):
                if chosen and (k := at(STORE)):
                    if k.v == 0:
                        for i in range(4):
                            pool.wait_ge(y_out[i], k.round * 16)
                    pool.wait_ge(y_made, k.n * YS + YS)
                    pool.wait_ge(carried[1], cnt(k.n))
                    pool.tensor_tensor(scratch[:, 1:2], scratch[:, 2:3], scratch[:, 3:4], ALU.add
                                       ).then_inc(carried[1], 1)
                    pool.indirect_dma_start(results, bass.IndirectOffsetOnAxis(ap=to[:, k.v:k.v + 1], axis=0),
                                            y[:, k.v, :], None, compute_op=ALU.add).then_inc(y_out[k.v], 16)
                if gelu and (k := at(ACTIVATE)):
                    pool.wait_ge(biased, k.n + 1)
                    pool.wait_ge(gates, cnt(k.n - 1) * GATE)
                    pool.tensor_tensor(halves[:, k.two, :], hid[:, k.two, :],
                                       parity[:, 1, bass.ds(k.n, 1)].broadcast_to([P, FH]), ALU.mult
                                       ).then_inc(halved, 1)
                if k := at(GATHER):
                    pool.wait_ge(placed, k.n + 1)
                    pool.wait_ge(carried[0], cnt(k.n))
                    pool.tensor_tensor(scratch[:, 0:1], scratch[:, 2:3], scratch[:, 3:4], ALU.add
                                       ).then_inc(carried[0], 1)
                    pool.indirect_dma_start(xg[:, k.v, :], None, rows,
                                            bass.IndirectOffsetOnAxis(ap=where[:, k.v:k.v + 1], axis=0)
                                            ).then_inc(xg_in[k.v], 16)
            pipeline(pool, N, STORE, 4, step)
            if chosen:
                for i in range(4):
                    pool.wait_ge(y_out[i], 16 * N // 4)

        @block.sync
        def _(sp):
            if chosen:
                sp.dma_start(results.rearrange("(n p) d -> p n d", p=P), g.x[:, :, :]).then_inc(x_stored, 16)
                return

            def step(at):
                if k := at(STORE):
                    sp.wait_ge(y_made, k.n * YS + YS)
                    sp.dma_start(results[bass.ds(k.n * P, P), :], y[:, k.v, :]).then_inc(y_out[k.v], 16)
            pipeline(sp, N, STORE, 4, step)
            for i in range(4):
                sp.wait_ge(y_out[i], 16 * N // 4)

        @block.tensor
        def _(pe):
            experts = Experts(pe, 0)

            def step(at):
                if k := at(DOWN):
                    e = experts.of(k, 1)
                    pe.wait_ge(h_copied, k.n + 1)
                    pe.wait_ge(y_made, cnt(k.n - 1) * YS)
                    for c in range(HC):
                        t = pe.matmul(pY[k.two][:, 0:D], hT[:, k.two, c * P:(c + 1) * P],
                                      mix.w_down[:, bass.ds(e * FH + c * D, D)], start=(c == 0), stop=(c == HC - 1))
                    t.then_inc(downed, 1)
                if k := at(H_TURN):
                    pe.wait_ge(gates, k.n * GATE + GATE)
                    pe.wait_ge(h_copied, cnt(k.n - 1))
                    for c in range(HC):
                        t = pe.transpose(pH[k.two][:, c * P:(c + 1) * P], gated[:, k.two, c * P:(c + 1) * P],
                                         g.ident[:, :])
                    t.then_inc(h_turned, 1)
                if k := at(UP):
                    e = experts.of(k, 0)
                    pe.wait_ge(x_copied, k.n + 1)
                    pe.wait_ge(read_up, cnt(k.n - 1) * (1 if gelu else GATE))
                    pe.matmul(pU[k.two][:, :], xT[:, k.two, :], mix.w_up[:, bass.ds(e * 512, 512)], start=True,
                              stop=True).then_inc(upped, 1)
                if k := at(TURN):
                    pe.wait_ge(xg_in[k.v], k.round * 16 + 16)
                    pe.wait_ge(x_copied, cnt(k.n - 1))
                    pe.transpose(pX[k.two][:, 0:P], xg[:, k.v, 0:D], g.ident[:, :]).then_inc(turned, 1)
            pipeline(pe, N, STORE, 4, step, experts.begin)

        @block.scalar
        def _(act):
            def step(at):
                if k := at(H_COPY):
                    act.wait_ge(h_turned, k.n + 1)
                    act.wait_ge(downed, cnt(k.n - 1))
                    act.copy(hT[:, k.two, :], pH[k.two][:, 0:FH]).then_inc(h_copied, 1)
                if k := at(ACTIVATE):
                    act.wait_ge(gates, cnt(k.n - 1) * GATE)
                    if gelu:
                        act.wait_ge(biased, k.n + 1)
                        act.activation(first[:, k.two, :], hid[:, k.two, :], ACT.Gelu).then_inc(acted, 1)
                        act.activation(tanh_h[:, k.two, :], hid[:, k.two, :], ACT.Tanh, scale=0.5).then_inc(acted, 1)
                    else:
                        act.wait_ge(upped, k.n + 1)
                        act.activation(first[:, k.two, :], pU[k.two][:, 0:FH], ACT.Silu).then_inc(acted, 1)
                if k := at(X_COPY):
                    act.wait_ge(turned, k.n + 1)
                    act.wait_ge(upped, cnt(k.n - 1))
                    act.copy(xT[:, k.two, :], pX[k.two][:, 0:P]).then_inc(x_copied, 1)
            pipeline(act, N, STORE, 4, step)

        @block.vector
        def _(dve):
            experts = Experts(dve, 1)

            def step(at):
                if k := at(SUM):
                    ch = Chain(dve, y_made, k.n * YS)
                    dve.wait_ge(y_out[k.v], k.round * 16)
                    dve.wait_ge(downed, k.n + 1)
                    if gelu:
                        e = experts.of(k, 1)
                        ch.mark(dve.tensor_tensor(y[:, k.v, :], pY[k.two][:, 0:D], mix.b_down[:, bass.ds(e * D, D)],
                                                  ALU.add))
                    elif chosen:
                        dve.wait_ge(noted, k.n + 1)
                        ch.mark(dve.tensor_scalar(y[:, k.v, :], pY[k.two][:, 0:D], share[:, bass.ds(k.n, 1)], None,
                                                  ALU.mult))
                        ch.mark(dve.tensor_scalar(to[:, k.v:k.v + 1], index[:, bass.ds(k.n, 1)], 1.0, None, ALU.mult))
                    else:
                        ch.mark(dve.tensor_scalar(y[:, k.v, :], pY[k.two][:, 0:D], 1.0, None, ALU.mult))

                if gelu and (k := at(GATES)):
                    ch = Chain(dve, gates, k.n * GATE)
                    dve.wait_ge(acted, k.n * ACTS + ACTS)
                    dve.wait_ge(halved, k.n + 1)
                    dve.wait_ge(h_turned, cnt(k.n - 1))
                    ch.link(dve.scalar_tensor_tensor(halves[:, k.two, :], tanh_h[:, k.two, :], 1.0,
                                                     halves[:, k.two, :], ALU.add, ALU.mult))
                    ch.mark(dve.scalar_tensor_tensor(gated[:, k.two, :], first[:, k.two, :],
                                                     parity[:, 0, bass.ds(k.n, 1)], halves[:, k.two, :],
                                                     ALU.mult, ALU.add))
                if not gelu and (k := at(GATES)):
                    dve.wait_ge(acted, k.n + 1)
                    dve.wait_ge(h_turned, cnt(k.n - 1))
                    dve.tensor_tensor(gated[:, k.two, :], first[:, k.two, :], pU[k.two][:, FH:2 * FH], ALU.mult
                                      ).then_inc(gates, 1)
                if gelu and (k := at(BIAS)):
                    e = experts.of(k, 0)
                    dve.wait_ge(upped, k.n + 1)
                    dve.wait_ge(acted, cnt(k.n - 1) * ACTS)
                    dve.wait_ge(halved, cnt(k.n - 1))
                    dve.tensor_tensor(hid[:, k.two, :], pU[k.two][:, 0:FH], mix.b_up[:, bass.ds(e * 512, 512)],
                                      ALU.add).then_inc(biased, 1)
                if chosen and (k := at(TURN)):
                    dve.wait_ge(xg_in[k.v], k.round * 16 + 16)
                    dve.tensor_scalar(share[:, bass.ds(k.n, 1)], xg[:, k.v, bass.ds(k.round + D, 1)], 1.0, None, ALU.mult
                                      ).then_inc(noted, 1)
                if k := at(PLACE):
                    dve.wait_ge(xg_in[k.v], k.round * 16)
                    dve.wait_ge(turned, cnt(k.n - 3))
                    if chosen:
                        dve.wait_ge(noted, cnt(k.n - 3))
                    dve.tensor_scalar(where[:, k.v:k.v + 1], index[:, bass.ds(k.n, 1)], 1.0, None, ALU.mult
                                      ).then_inc(placed, 1)
            pipeline(dve, N, STORE, 4, step, experts.begin if gelu else None)


def mixture(nc, g, mix, rows, results):
    C, N = mix.choices, mix.tiles
    with ExitStack() as ctx:
        m = Memory(nc, ctx, mix.name)
        logits, index = m.sb("logits", [P, NT, E]), m.sb("index", [P, N], U32)
        if mix.kind == "experts_choose":
            slots, weight = m.sb("slots", [P, NT, C]), m.sb("weight", [P, C, NT])
        else:
            slots, weight = g.slots2, g.weight2
        packed, parity = m.sb("packed", [P, 2, mix.rounds], I32), m.sb("parity", [P, 2, N])
        moe_front(nc, g, mix, rows, logits)
        if mix.kind == "experts_choose":
            by_tile = weight[:, :, :].rearrange("p c n -> p (c n)").rearrange("p (n e) -> p n e", e=E)
            choose_tokens(nc, g, mix, logits, slots, by_tile, rows)
            build_index(nc, g, mix, slots, index)
            run_experts(nc, g, mix, rows, index, None, None, results)
            return
        route_top2(nc, g, mix, logits, slots, weight, packed, parity)
        build_index(nc, g, mix, slots, index)
        run_experts(nc, g, mix, rows, index, packed, parity, results)


class Globals:
    pass


def build(nc, io, out):
    with ExitStack() as ctx:
        m = Memory(nc, ctx, "g")
        g = Globals()
        g.x = m.sb("x", [P, NT, D])
        g.mv = m.sb("mv", [P, NT, 2])
        g.rstd = m.sb("rstd", [P, NT])
        g.bn6 = m.sb("bn6", [P, NT, 6])
        g.carrier = m.sb("carrier", [P, 2])
        g.gates, g.tanh_gate = m.sb("gates", [P, 8]), m.sb("tanh_gate", [P, 8])
        g.ident = m.sb("ident", [P, P])
        g.start_in, g.gates_done, g.stats_done, stored = (
            m.sem(k) for k in ("start_in", "gates_done", "stats_done", "stored"))
        g.x_in = [m.sem(f"x_in{half}") for half in range(2)]
        g.w_l0, g.b_l0 = m.sb("w_l0", [P, 2, 2 * D]), m.sb("b_l0", [P, 2 * D])
        g.w_fc, g.w_proj = m.sb("w_fc", [P, 512]), m.sb("w_proj", [P, 4, D])
        g.ones = m.sb("ones", [P, P])
        g.head_mask = {16: m.sb("mask16", [P, 16])[:, :], 4: m.sb("mask4", [P, 4])[:, :]}
        w1 = m.sb("w_l1", [P, 4 * D])
        b1 = m.sb("b_l1", [P, 3 + D])
        w2 = m.sb("w_l2", [P, 4 * D + 32 + D])
        w3 = m.sb("w_l3", [P, 4 * D])
        up_swiglu, down_swiglu = m.sb("up_swiglu", [P, E * 512]), m.sb("down_swiglu", [P, E * 256])
        up2, down2 = m.sb("up2", [P, E * 512]), m.sb("down2", [P, E * 512])
        bias_up2, bias_down2 = m.sb("bias_up2", [P, E * 512]), m.sb("bias_down2", [P, E * D])
        router, bias_router = m.sb("router", [P, 3, E]), m.sb("bias_router", [P, 2, E])
        g.down, g.up, g.token = m.sb("down", [P, E]), m.sb("up", [P, P]), m.sb("token", [P, NT])
        g.up16, g.before = m.sb("up16", [P, P], F16), m.sb("before", [P, P], BF16)
        g.ones16 = m.sb("ones16", [P, P], BF16)
        g.before_f = m.sb("before_f", [P, P])
        chooser = m.sb("chooser", [P, 2 * P + 1])
        g.same_expert, g.earlier_row, g.row_base = chooser[:, 0:P], chooser[:, P:2 * P], chooser[:, 2 * P:]
        b3 = m.sb("b_l3", [P, 2 + 2 * D])
        own_of3, own = m.sb("own_of3", [P, PERIOD * 24]), m.sb("own", [P, 3 * 4])
        g.own_head_of3 = own_of3[:, :].rearrange("p (c x) -> p c x", c=PERIOD)
        g.own_head = own[:, :].rearrange("p (c h) -> p c h", h=4)
        g.slots2, g.weight2 = m.sb("slots2", [P, NT, CHOICES]), m.sb("weight2", [P, CHOICES, NT])
        g.rms_scale = m.sb("rms_scale", [P, 1])
        g.rope_q, g.rope_k = m.sb("rope_q", [P, 2, T]), m.sb("rope_k", [P, 2, S])
        mask_words = m.sb("mask_words", [P, NT * S // 4], I32)
        g.mask8 = mask_words[:, :].bitcast(U8)
        g.ctx_sum2, g.ctx_rstd = m.sb("ctx_sum2", [S, NT]), m.sb("ctx_rstd", [S, NT])
        g.pos = m.sb("pos", [P, NT], I32)
        g.cos_q, g.sin_q = m.sb("cos_q", [P, NT, 4]), m.sb("sin_q", [P, NT, 8])

        w = {
            "start": [(g.ident[:, :], io["ident"]), (g.gates[:, 0:4], row_bcast(io["g_xattn"])),
                      (g.gates[:, 4:8], row_bcast(io["g_ffn"]))],
            "L0a": [(g.w_l0[:, :, 0:D], io["L0_xattn_W_lin"].rearrange("(c p) n -> p c n", p=P)),
                    (g.w_l0[:, :, D:2 * D], io["L0_xattn_W_gate"].rearrange("(c p) n -> p c n", p=P)),
                    (g.b_l0[:, 0:D], row_bcast(io["L0_xattn_b_lin"])),
                    (g.b_l0[:, D:2 * D], row_bcast(io["L0_xattn_b_gate"]))],
            "L0f": [(g.w_fc[:, :], io["w_fcT"]), (g.w_proj[:, :, :], io["w_projT"])],
            "L1a": [(w1[:, 0:3 * D], io["w1_inT"]), (w1[:, 3 * D:4 * D], io["w1_outT"]), (b1[:, 0:3], io["b1_cols"]),
                    (b1[:, 3:3 + D], row_bcast(io["L1_xattn_out_b"])), (g.head_mask[16], io["mask16"]),
                    (g.head_mask[4], io["mask4"]), (own_of3[:, :], io["own_of3"]), (own[:, :], io["own"])],
            "L1f": [(up_swiglu[:, :], io["up1"]), (down_swiglu[:, :], io["down1"])],
            "moe": [(router[:, :, :], io["routers"]),
                    (g.down[:, :], io["down_to_1"]), (g.up[:, :], io["up_from_0"]), (g.token[:, :], io["token"]),
                    (g.up16[:, :], io["up16"]), (g.before_f[:, :], io["before"])],
            "L2a": [(w2[:, 0:4 * D + 32], io["w2_in"]), (w2[:, 4 * D + 32:], io["w2_out"]),
                    (g.rope_q[:, :, :], io["rope_q"]), (g.rope_k[:, :, :], io["rope_k"]),
                    (g.rms_scale[:, :], io["rms_scale"]), (mask_words[:, :], row_bcast(io["mask_words"]))],
            "L2f": [(up2[:, :], io["up2"]), (down2[:, :], io["down2"]), (bias_up2[:, :], row_bcast(io["bias_up2"])),
                    (bias_down2[:, :], row_bcast(io["bias_down2"])), (bias_router[:, 1, :], row_bcast(io["L2_ffn_bg"]))],
            "L3a": [(w3[:, :], io["w3"]), (b3[:, 0:2], io["b3_cols"]), (b3[:, 2:2 + D], row_bcast(io["L3_xattn_bq"])),
                    (b3[:, 2 + D:], row_bcast(io["L3_xattn_bo"])), (g.pos[:, :], io["pos"])],
            "L3c": [(chooser[:, :], io["chooser"])],
            "L3f": [(up_swiglu[:, :], io["up3"]), (down_swiglu[:, :], io["down3"])],
        }
        g.loads = w
        g.bias_router = bias_router
        rows = [nc.dram_tensor(f"rows{i}", (B * T, n), F32, kind="Internal").ap()
                for i, n in ((1, D), (2, D), (3, D + E))]
        results = [nc.dram_tensor(f"results{i}", (TOP2_TILES * P, D), F32, kind="Internal").ap() for i in (1, 2)]
        mix1 = Mixture("m1", "softmax_first", CHOICES, TOP2_TILES, D, 256, "L1f", 5, router[:, 0, :],
                       bias_router[:, 0, :], up_swiglu, down_swiglu)
        mix2 = Mixture("m2", "logits_first", CHOICES, TOP2_TILES, D, 512, "L2f", 6, router[:, 1, :],
                       bias_router[:, 1, :], up2, down2, bias_up2, bias_down2)
        mix3 = Mixture("m3", "experts_choose", E, CHOSEN_TILES, D + E, 256, "L3f", 7, router[:, 2, :],
                       bias_router[:, 0, :], up_swiglu, down_swiglu)
        g.weights_in = {k: m.sem(f"w_{k}") for k in w}
        heads1 = Heads("a1", 16, w1[:, 0:D], w1[:, D:2 * D], w1[:, 2 * D:3 * D], w1[:, 3 * D:], "L1a", 1,
                       bq=b1[:, 0:1], bk=b1[:, 1:2], bv=b1[:, 2:3], bo=b1[:, 3:])
        heads2 = Heads("a2", 4, w2[:, 0:2 * D], w2[:, 2 * D:4 * D], w2[:, 4 * D:4 * D + 32], w2[:, 4 * D + 32:],
                       "L2a", 2, rope="tables", rms=True)
        heads3 = Heads("a3", 16, w3[:, 0:D], w3[:, D:2 * D], w3[:, 2 * D:3 * D], w3[:, 3 * D:], "L3a", 3,
                       rope="positions", bq=b3[:, 2:2 + D], bk=b3[:, 0:1], bv=b3[:, 1:2], bo=b3[:, 2 + D:])
        blocks = [
            lambda: (rstd_block(nc, g, "r0"), l0_attention(nc, g, io)),
            lambda: (rstd_block(nc, g, "r1"), l0_feed_forward(nc, g, io)),
            lambda: (rstd_block(nc, g, "r2"), attention(nc, g, io, heads1)),
            lambda: (rstd_block(nc, g, "r3"), mixture(nc, g, mix1, rows[0], results[0])),
            lambda: (ctx_rms(nc, g), attention(nc, g, io, heads2, merge=results[0])),
            lambda: (rstd_block(nc, g, "r5"), mixture(nc, g, mix2, rows[1], results[1])),
            lambda: (rope_angles(nc, g), attention(nc, g, io, heads3, merge=results[1])),
            lambda: (load_later(nc, g), rstd_block(nc, g, "r7"), mixture(nc, g, mix3, rows[2], out)),
        ]
        Memory.used.clear()
        load_inputs(nc, g, io)
        for b, block in enumerate(blocks):
            block()
            if b in (2, 4, 5):
                recycle_semaphores(nc)


def kernel(**inputs):
    import concourse.bacc as bacc
    from concourse.bass_utils import run_bass_kernel_spmd

    a = {k: np.asarray(v) for k, v in inputs.items()}
    def rows(v):
        return v.reshape(-1, P, v.shape[-1]).transpose(1, 0, 2)

    def turned(v, width):
        return np.roll(v.reshape(D, -1, 2, width // 2), 1, axis=2).reshape(v.shape)

    q2 = a["L2_xattn_q_w"].transpose(1, 0, 2).reshape(D, D)
    k2 = np.tile(a["L2_xattn_kv_w"][0, 0], (1, 4))
    v2 = a["L2_xattn_kv_w"][1, 0]
    timescale = np.float32(10000.0) ** (np.float32(2.0 / 32) * np.arange(16, dtype=np.float32))
    part = np.arange(P) % 32

    def rope(positions):
        angle = positions.astype(np.float32)[None, :] / timescale[part % 16][:, None]
        sign = np.where(part < 16, -1, 1).astype(np.float32)[:, None]
        return np.stack([np.cos(angle), sign * np.sin(angle)], axis=1).astype(np.float32)

    def beside(parts):
        return parts.transpose(1, 0, 2).reshape(parts.shape[1], -1)

    def chunks(v):
        return v.reshape(E, -1, P, D).transpose(2, 0, 1, 3).reshape(P, -1)

    at = np.arange(P)
    same = at[:, None] % E == at[None, :] % E

    flat = np.arange(3 * P).reshape(3, P).T
    flat5 = np.arange(PERIOD * P).reshape(PERIOD, P).T
    own = (flat[:, :, None] // PITCH == np.arange(4)) & (flat[:, :, None] % PITCH < S)
    near = np.array(FIRST_HEAD)[:, None] + np.arange(3)
    own_of3 = (flat5[:, :, None] // PITCH == near) & (flat5[:, :, None] % PITCH < S)

    arrays = {
        "own": own.reshape(P, -1).astype(np.float32),
        "own_of3": np.repeat(own_of3, 8, axis=2).reshape(P, -1).astype(np.float32),
        "up1": beside(np.concatenate([a["L1_ffn_w1"], a["L1_ffn_w3"]], axis=2)), "down1": chunks(a["L1_ffn_w2"]),
        "up3": beside(np.concatenate([a["L3_ffn_W1"], a["L3_ffn_W3"]], axis=1).transpose(0, 2, 1)),
        "down3": chunks(a["L3_ffn_W2"].transpose(0, 2, 1)),
        "up2": beside(a["L2_ffn_W1"]), "down2": chunks(a["L2_ffn_W2"]),
        "bias_up2": a["L2_ffn_b1"].reshape(-1), "bias_down2": a["L2_ffn_b2"].reshape(-1), "L2_ffn_bg": a["L2_ffn_bg"],
        "routers": np.stack([a["L1_ffn_gate_w"].T, a["L2_ffn_Wg"], a["L3_ffn_Wg"].T], axis=1),
        "down_to_1": np.tile(np.arange(E, 0, -1, dtype=np.float32), (P, 1)),
        "up_from_0": np.tile(at.astype(np.float32), (P, 1)), "up16": np.tile(at.astype(np.float16), (P, 1)),
        "token": (np.arange(NT)[None, :] * P + at[:, None] - B * T // 2).astype(np.float32),
        "before": (at[:, None] < at[None, :]).astype(np.float32),
        "chooser": np.concatenate([same, same & (at[:, None] < at[None, :]), at[:, None] % E * CAPACITY],
                                  axis=1).astype(np.float32),
        "x": a["x"].transpose(1, 0, 2),
        "ctx": a["ctx_1024"],
        "ctxT": a["ctx_1024"].transpose(0, 2, 1),
        "pos": a["itok_BxS_1_4095"].astype(np.int32).T,
        "mask_words": a["mask_BxS2_bk0"].reshape(-1).view(np.int32),
        "g_xattn": a["g_xattn"], "g_ffn": a["g_ffn"],
        "ident": np.eye(P, dtype=np.float32),
        "mask16": (np.arange(P)[:, None] // 8 == np.arange(16)).astype(np.float32),
        "mask4": (np.arange(P)[:, None] // 32 == np.arange(4)).astype(np.float32),
        "w_fcT": a["L0_ffn_W_fc"].T, "w_projT": rows(a["L0_ffn_W_proj"].T),
        "w1_inT": a["L1_xattn_in_proj_weight"].T, "w1_outT": a["L1_xattn_out_w"].T,
        "b1_cols": a["L1_xattn_in_proj_bias"].reshape(3, D).T,
        "w2_in": np.concatenate([q2, turned(q2, 32), k2, turned(k2, 32), v2], axis=1),
        "w2_out": a["L2_xattn_out_w"].reshape(D, D),
        "rope_q": rope(np.arange(S, S + T)), "rope_k": rope(np.arange(S)),
        "rms_scale": a["L2_xattn_rms_scale"].reshape(D, 1),
        "w3": np.concatenate([a[f"L3_xattn_W{k}"].T for k in "qkvo"], axis=1),
        "b3_cols": np.stack([a["L3_xattn_bk"], a["L3_xattn_bv"]], axis=1),
    }
    for k in ("L0_xattn_W_lin", "L0_xattn_W_gate", "L0_xattn_b_lin", "L0_xattn_b_gate", "L1_xattn_out_b",
              "L3_xattn_bq", "L3_xattn_bo"):
        arrays[k] = a[k]
    arrays = {k: np.ascontiguousarray(v) for k, v in arrays.items()}
    nc = bacc.Bacc("TRN2", target_bir_lowering=False, num_devices=1)
    io = {k: nc.dram_tensor(f"in_{k}", v.shape, mybir.dt.from_np(v.dtype), kind="ExternalInput").ap()
          for k, v in arrays.items()}
    out = nc.dram_tensor("out", (B * T, D), F32, kind="ExternalOutput").ap()
    build(nc, io, out)
    r = run_bass_kernel_spmd(nc, [{f"in_{k}": v for k, v in arrays.items()}], core_ids=[0])
    return r.results[0]["out"].reshape(B, T, D)
```
